# Optimizing a Trainium2 kernel written in Bass

```python
import numpy as np
import jax
import jax.numpy as jnp

def _softmax(x, axis=-1):
    return jax.nn.softmax(x, axis=axis)

def _gelu(x):
    return jax.nn.gelu(x, approximate=True)

def _silu(x):
    return jax.nn.silu(x)

def _sigmoid(x):
    return jax.nn.sigmoid(x)

def _layernorm(x, axis=-1, eps=1e-05):
    m = jnp.mean(x, axis=axis, keepdims=True)
    v = jnp.var(x, axis=axis, keepdims=True)
    return (x - m) / jnp.sqrt(v + eps)

def _scatter_add(tgt, idx, src, axis=0):
    return tgt.at[idx].add(src)

def _segment_sum(src, seg, n):
    return jax.ops.segment_sum(src, seg, n)
kernel_name = 'mk_xattn_seq_d4_seqx_r8_ba34ef'

def setup_inputs(seed: int=0):
    np.random.seed(seed)
    _w = jnp.asarray

    def _rec_inputs():
        import jax
        import jax.numpy as jnp
        _rk = jax.random.key(seed)
        x = -0.000125 + 0.9999 * jax.random.normal(jax.random.fold_in(_rk, 1), (4, 256, 256), jnp.float32)
        _lenS = 256 - jax.random.randint(jax.random.fold_in(_rk, 7), (4,), 0, max(1, 256 // 4) + 1, jnp.int32)
        _lenS2 = 256 - jax.random.randint(jax.random.fold_in(_rk, 8), (4,), 0, max(1, 256 // 4) + 1, jnp.int32)
        _ctx_1024P = jax.random.normal(jax.random.fold_in(_rk, 11), (4, 16, 128), jnp.float32)
        _ctx_1024c = jax.random.dirichlet(jax.random.fold_in(_rk, 511), 0.3 * jnp.ones((16,), jnp.float32), (4, 256))
        _ctx_1024t = jnp.einsum('bsk,bkd->bsd', _ctx_1024c, _ctx_1024P)
        _ctx_1024t = _ctx_1024t * jax.lax.rsqrt(jnp.mean(jnp.square(_ctx_1024t)) + 1e-12) * 0.953939
        ctx_1024 = 4.13588e-05 + 0.999923 * (_ctx_1024t + 0.3 * jax.random.normal(jax.random.fold_in(_rk, 611), (4, 256, 128), jnp.float32))
        pos_1xS = jnp.broadcast_to(jnp.arange(256, dtype=jnp.int32), (1, 256))
        _validS = jnp.arange(256)[None, :] < _lenS[:, None]
        _validS2 = jnp.arange(256)[None, :] < _lenS2[:, None]
        _causal = jnp.tril(jnp.ones((256, 256), dtype=bool))
        mask_BxS_ik0 = jnp.where(jnp.broadcast_to(_validS[:, :], (4, 256)), 0, 1).astype(jnp.int32)
        mask_BxS2_bk0 = jnp.logical_not(jnp.broadcast_to(_validS2[:, :], (4, 256)))
        return (x, ctx_1024, pos_1xS, mask_BxS_ik0, mask_BxS2_bk0)
    x, ctx_1024, pos_1xS, mask_BxS_ik0, mask_BxS2_bk0 = _rec_inputs()

    def _L0_xattn_setup():
        import jax, jax.numpy as jnp
        import numpy as np
        EPS = 1e-06

        def _rmsnorm(x, w):
            var = jnp.mean(jnp.square(x), axis=-1, keepdims=True)
            return x * jax.lax.rsqrt(var + EPS) * w
        key = jax.random.key(seed)
        ks = jax.random.split(key, 6)
        B, N, M = (4, 512, 256)
        d_model, memory_dim = (256, 128)
        hidden_states = jax.random.normal(ks[0], (B, N, d_model), dtype=jnp.float32)
        memory = jax.random.normal(ks[1], (B, M, memory_dim), dtype=jnp.float32)
        W_mem = jax.random.normal(ks[2], (d_model, memory_dim), dtype=jnp.float32) / np.sqrt(memory_dim)
        W_gate = jax.random.normal(ks[3], (d_model, 2 * d_model), dtype=jnp.float32) / np.sqrt(2 * d_model)
        b_gate = jax.random.normal(ks[4], (d_model,), dtype=jnp.float32) * 0.01
        norm_w = jnp.ones((d_model,), dtype=jnp.float32)
        return {'hidden_states': hidden_states, 'memory': memory, 'W_mem': W_mem, 'W_gate': W_gate, 'b_gate': b_gate, 'norm_w': norm_w}
    _L0_xattn_all = _L0_xattn_setup()
    _L0_xattn_in = {k: v for k, v in _L0_xattn_all.items() if k in ('W_mem', 'W_gate', 'b_gate', 'norm_w')}
    del _L0_xattn_all

    def _L1_xattn_setup():
        import jax, jax.numpy as jnp
        import numpy as np
        H = 256
        NH = 16
        HD = H // NH
        CH = 128
        CC = 128
        CHD = CC // NH
        I = 688
        B = 2
        L = 256
        LE = 128
        EPS = 1e-06

        def rms_norm(x, w):
            xf = x.astype(jnp.float32)
            var = jnp.mean(xf * xf, axis=-1, keepdims=True)
            return (w * (xf * jax.lax.rsqrt(var + EPS))).astype(x.dtype)

        def expert_mask(tt):
            vm = jnp.zeros(tt.shape, dtype=bool)
            vm = vm.at[:, :-1].set((tt[:, :-1] == 1) & (tt[:, 1:] == 1))
            return vm

        def rotate_half(x):
            d = x.shape[-1] // 2
            return jnp.concatenate([-x[..., d:], x[..., :d]], axis=-1)

        def apply_rotary(q, k, position_ids, seq_len):
            inv = 1.0 / 10000.0 ** (jnp.arange(0, HD, 2, dtype=jnp.float32) / HD)
            t = jnp.arange(seq_len, dtype=jnp.float32)
            freqs = jnp.outer(t, inv)
            emb = jnp.concatenate([freqs, freqs], axis=-1)
            cos = jnp.cos(emb)[position_ids][:, None].astype(q.dtype)
            sin = jnp.sin(emb)[position_ids][:, None].astype(q.dtype)
            return (q * cos + rotate_half(q) * sin, k * cos + rotate_half(k) * sin)

        def sdpa(q, k, v, causal):
            scale = 1.0 / np.sqrt(q.shape[-1])
            scores = jnp.einsum('bhqd,bhkd->bhqk', q * scale, k)
            if causal:
                mask = jnp.tril(jnp.ones((q.shape[-2], k.shape[-2]), dtype=bool))
                scores = jnp.where(mask, scores, jnp.finfo(jnp.float32).min)
            p = jax.nn.softmax(scores.astype(jnp.float32), axis=-1).astype(q.dtype)
            return jnp.einsum('bhqk,bhkd->bhqd', p, v)

        def heads(x, nh, hd):
            b, l, _ = x.shape
            return x.reshape(b, l, nh, hd).transpose(0, 2, 1, 3)
        key = jax.random.key(seed)
        ks = jax.random.split(key, 20)
        s = 0.02
        f32 = jnp.float32
        return {'hidden_states': jax.random.normal(ks[0], (B, L, H), f32), 'encoder_outputs': jax.random.normal(ks[1], (B, LE, CH), f32), 'token_type_ids': jax.random.randint(ks[2], (B, L), 0, 2, jnp.int32), 'position_ids': jnp.arange(L, dtype=jnp.int32)[None, :], 'ln_in_w': jnp.ones((H,), f32), 'ln_post_attn_w': jnp.ones((H,), f32), 'ln_post_cross_w': jnp.ones((H,), f32), 'v_qkv': jax.random.normal(ks[3], (H, 3 * H), f32) * s, 'l_qkv': jax.random.normal(ks[4], (H, 3 * H), f32) * s, 'v_dense': jax.random.normal(ks[5], (H, H), f32) * s, 'l_dense': jax.random.normal(ks[6], (H, H), f32) * s, 'cq_w': jax.random.normal(ks[7], (H, CC), f32) * s, 'ckv_w': jax.random.normal(ks[8], (CH, 2 * CC), f32) * s, 'cdense_w': jax.random.normal(ks[9], (CC, H), f32) * s, 'v_gate': jax.random.normal(ks[10], (H, I), f32) * s, 'v_up': jax.random.normal(ks[11], (H, I), f32) * s, 'v_down': jax.random.normal(ks[12], (I, H), f32) * s, 'l_gate': jax.random.normal(ks[13], (H, I), f32) * s, 'l_up': jax.random.normal(ks[14], (H, I), f32) * s, 'l_down': jax.random.normal(ks[15], (I, H), f32) * s}
    _L1_xattn_all = _L1_xattn_setup()
    _L1_xattn_in = {k: v for k, v in _L1_xattn_all.items() if k in ('ln_in_w', 'ln_post_attn_w', 'ln_post_cross_w', 'v_qkv', 'l_qkv', 'v_dense', 'l_dense', 'cq_w', 'ckv_w', 'cdense_w', 'v_gate', 'v_up', 'v_down', 'l_gate', 'l_up', 'l_down')}
    del _L1_xattn_all

    def _L2_xattn_setup():
        import jax, jax.numpy as jnp
        import numpy as np
        DIM = 256
        DIM_MEDIA = 128
        HEADS = 16
        DIM_HEAD = 64
        INNER = HEADS * DIM_HEAD
        FF_INNER = 4 * DIM
        B, N_TOK, N_LAT = (4, 256, 64)
        EPS = 1e-05

        def layernorm(x, g, b):
            mu = jnp.mean(x, axis=-1, keepdims=True)
            var = jnp.var(x, axis=-1, keepdims=True)
            return (x - mu) * jax.lax.rsqrt(var + EPS) * g + b
        key = jax.random.key(seed)
        ks = jax.random.split(key, 12)
        x = jax.random.normal(ks[0], (B, N_TOK, DIM), dtype=jnp.float32)
        media = jax.random.normal(ks[1], (B, N_LAT, DIM_MEDIA), dtype=jnp.float32)
        media_mask = jax.random.randint(ks[2], (B, N_LAT), 0, 2).astype(bool)
        media_mask = media_mask.at[:, 0].set(True)
        s = lambda d: 1.0 / np.sqrt(d)
        Wq = jax.random.normal(ks[3], (DIM, INNER), dtype=jnp.float32) * s(DIM)
        Wkv = jax.random.normal(ks[4], (DIM_MEDIA, 2 * INNER), dtype=jnp.float32) * s(DIM_MEDIA)
        Wo = jax.random.normal(ks[5], (INNER, DIM), dtype=jnp.float32) * s(INNER)
        W1 = jax.random.normal(ks[6], (DIM, FF_INNER), dtype=jnp.float32) * s(DIM)
        W2 = jax.random.normal(ks[7], (FF_INNER, DIM), dtype=jnp.float32) * s(FF_INNER)
        return {'x': x, 'media': media, 'media_mask': media_mask, 'ln_q_g': jnp.ones((DIM,), jnp.float32), 'ln_q_b': jnp.zeros((DIM,), jnp.float32), 'Wq': Wq, 'Wkv': Wkv, 'Wo': Wo, 'attn_gate': jax.random.normal(ks[8], (1,), jnp.float32) * 0.5, 'ln_ff_g': jnp.ones((DIM,), jnp.float32), 'ln_ff_b': jnp.zeros((DIM,), jnp.float32), 'W1': W1, 'W2': W2, 'ff_gate': jax.random.normal(ks[9], (1,), jnp.float32) * 0.5}
    _L2_xattn_all = _L2_xattn_setup()
    _L2_xattn_in = {k: v for k, v in _L2_xattn_all.items() if k in ('ln_q_g', 'ln_q_b', 'Wq', 'Wkv', 'Wo', 'attn_gate', 'ln_ff_g', 'ln_ff_b', 'W1', 'W2', 'ff_gate')}
    del _L2_xattn_all

    def _L3_xattn_setup():
        import jax, jax.numpy as jnp
        import numpy as np
        EPS = 1e-06

        def _rmsnorm(x, w):
            var = jnp.mean(jnp.square(x), axis=-1, keepdims=True)
            return x * jax.lax.rsqrt(var + EPS) * w
        key = jax.random.key(seed)
        ks = jax.random.split(key, 6)
        B, N, M = (4, 512, 256)
        d_model, memory_dim = (256, 128)
        hidden_states = jax.random.normal(ks[0], (B, N, d_model), dtype=jnp.float32)
        memory = jax.random.normal(ks[1], (B, M, memory_dim), dtype=jnp.float32)
        W_mem = jax.random.normal(ks[2], (d_model, memory_dim), dtype=jnp.float32) / np.sqrt(memory_dim)
        W_gate = jax.random.normal(ks[3], (d_model, 2 * d_model), dtype=jnp.float32) / np.sqrt(2 * d_model)
        b_gate = jax.random.normal(ks[4], (d_model,), dtype=jnp.float32) * 0.01
        norm_w = jnp.ones((d_model,), dtype=jnp.float32)
        return {'hidden_states': hidden_states, 'memory': memory, 'W_mem': W_mem, 'W_gate': W_gate, 'b_gate': b_gate, 'norm_w': norm_w}
    _L3_xattn_all = _L3_xattn_setup()
    _L3_xattn_in = {k: v for k, v in _L3_xattn_all.items() if k in ('W_mem', 'W_gate', 'b_gate', 'norm_w')}
    del _L3_xattn_all
    return {'x': x, 'ctx_1024': ctx_1024, 'pos_1xS': pos_1xS, 'mask_BxS_ik0': mask_BxS_ik0, 'mask_BxS2_bk0': mask_BxS2_bk0, 'L0_xattn_W_mem': _L0_xattn_in['W_mem'], 'L0_xattn_W_gate': _L0_xattn_in['W_gate'], 'L0_xattn_b_gate': _L0_xattn_in['b_gate'], 'L0_xattn_norm_w': _L0_xattn_in['norm_w'], 'L1_xattn_ln_in_w': _L1_xattn_in['ln_in_w'], 'L1_xattn_ln_post_attn_w': _L1_xattn_in['ln_post_attn_w'], 'L1_xattn_ln_post_cross_w': _L1_xattn_in['ln_post_cross_w'], 'L1_xattn_v_qkv': _L1_xattn_in['v_qkv'], 'L1_xattn_l_qkv': _L1_xattn_in['l_qkv'], 'L1_xattn_v_dense': _L1_xattn_in['v_dense'], 'L1_xattn_l_dense': _L1_xattn_in['l_dense'], 'L1_xattn_cq_w': _L1_xattn_in['cq_w'], 'L1_xattn_ckv_w': _L1_xattn_in['ckv_w'], 'L1_xattn_cdense_w': _L1_xattn_in['cdense_w'], 'L1_xattn_v_gate': _L1_xattn_in['v_gate'], 'L1_xattn_v_up': _L1_xattn_in['v_up'], 'L1_xattn_v_down': _L1_xattn_in['v_down'], 'L1_xattn_l_gate': _L1_xattn_in['l_gate'], 'L1_xattn_l_up': _L1_xattn_in['l_up'], 'L1_xattn_l_down': _L1_xattn_in['l_down'], 'L2_xattn_ln_q_g': _L2_xattn_in['ln_q_g'], 'L2_xattn_ln_q_b': _L2_xattn_in['ln_q_b'], 'L2_xattn_Wq': _L2_xattn_in['Wq'], 'L2_xattn_Wkv': _L2_xattn_in['Wkv'], 'L2_xattn_Wo': _L2_xattn_in['Wo'], 'L2_xattn_attn_gate': _L2_xattn_in['attn_gate'], 'L2_xattn_ln_ff_g': _L2_xattn_in['ln_ff_g'], 'L2_xattn_ln_ff_b': _L2_xattn_in['ln_ff_b'], 'L2_xattn_W1': _L2_xattn_in['W1'], 'L2_xattn_W2': _L2_xattn_in['W2'], 'L2_xattn_ff_gate': _L2_xattn_in['ff_gate'], 'L3_xattn_W_mem': _L3_xattn_in['W_mem'], 'L3_xattn_W_gate': _L3_xattn_in['W_gate'], 'L3_xattn_b_gate': _L3_xattn_in['b_gate'], 'L3_xattn_norm_w': _L3_xattn_in['norm_w']}

def reference(x, ctx_1024, pos_1xS, mask_BxS_ik0, mask_BxS2_bk0, L0_xattn_W_mem, L0_xattn_W_gate, L0_xattn_b_gate, L0_xattn_norm_w, L1_xattn_ln_in_w, L1_xattn_ln_post_attn_w, L1_xattn_ln_post_cross_w, L1_xattn_v_qkv, L1_xattn_l_qkv, L1_xattn_v_dense, L1_xattn_l_dense, L1_xattn_cq_w, L1_xattn_ckv_w, L1_xattn_cdense_w, L1_xattn_v_gate, L1_xattn_v_up, L1_xattn_v_down, L1_xattn_l_gate, L1_xattn_l_up, L1_xattn_l_down, L2_xattn_ln_q_g, L2_xattn_ln_q_b, L2_xattn_Wq, L2_xattn_Wkv, L2_xattn_Wo, L2_xattn_attn_gate, L2_xattn_ln_ff_g, L2_xattn_ln_ff_b, L2_xattn_W1, L2_xattn_W2, L2_xattn_ff_gate, L3_xattn_W_mem, L3_xattn_W_gate, L3_xattn_b_gate, L3_xattn_norm_w):
    import jax
    import jax.numpy as jnp

    def _L0_xattn_ref(hidden_states, memory, W_mem, W_gate, b_gate, norm_w):
        import jax, jax.numpy as jnp
        import numpy as np
        EPS = 1e-06

        def _rmsnorm(x, w):
            var = jnp.mean(jnp.square(x), axis=-1, keepdims=True)
            return x * jax.lax.rsqrt(var + EPS) * w
        D = hidden_states.shape[-1]
        memory_proj = jnp.einsum('bme,de->bmd', memory, W_mem)
        scores = jnp.einsum('bnd,bmd->bnm', hidden_states, memory_proj) / jnp.sqrt(jnp.float32(D))
        attn = jax.nn.softmax(scores, axis=-1)
        memory_context = jnp.einsum('bnm,bmd->bnd', attn, memory_proj)
        gate_input = jnp.concatenate([hidden_states, memory_context], axis=-1)
        gate = jax.nn.sigmoid(jnp.einsum('bnf,df->bnd', gate_input, W_gate) + b_gate)
        fused = hidden_states + gate * memory_context
        return _rmsnorm(fused, norm_w)

    def _L1_xattn_ref(hidden_states, encoder_outputs, token_type_ids, position_ids, ln_in_w, ln_post_attn_w, ln_post_cross_w, v_qkv, l_qkv, v_dense, l_dense, cq_w, ckv_w, cdense_w, v_gate, v_up, v_down, l_gate, l_up, l_down):
        import jax, jax.numpy as jnp
        import numpy as np
        H = 256
        NH = 16
        HD = H // NH
        CH = 128
        CC = 128
        CHD = CC // NH
        I = 688
        B = 2
        L = 256
        LE = 128
        EPS = 1e-06

        def rms_norm(x, w):
            xf = x.astype(jnp.float32)
            var = jnp.mean(xf * xf, axis=-1, keepdims=True)
            return (w * (xf * jax.lax.rsqrt(var + EPS))).astype(x.dtype)

        def expert_mask(tt):
            vm = jnp.zeros(tt.shape, dtype=bool)
            vm = vm.at[:, :-1].set((tt[:, :-1] == 1) & (tt[:, 1:] == 1))
            return vm

        def rotate_half(x):
            d = x.shape[-1] // 2
            return jnp.concatenate([-x[..., d:], x[..., :d]], axis=-1)

        def apply_rotary(q, k, position_ids, seq_len):
            inv = 1.0 / 10000.0 ** (jnp.arange(0, HD, 2, dtype=jnp.float32) / HD)
            t = jnp.arange(seq_len, dtype=jnp.float32)
            freqs = jnp.outer(t, inv)
            emb = jnp.concatenate([freqs, freqs], axis=-1)
            cos = jnp.cos(emb)[position_ids][:, None].astype(q.dtype)
            sin = jnp.sin(emb)[position_ids][:, None].astype(q.dtype)
            return (q * cos + rotate_half(q) * sin, k * cos + rotate_half(k) * sin)

        def sdpa(q, k, v, causal):
            scale = 1.0 / np.sqrt(q.shape[-1])
            scores = jnp.einsum('bhqd,bhkd->bhqk', q * scale, k)
            if causal:
                mask = jnp.tril(jnp.ones((q.shape[-2], k.shape[-2]), dtype=bool))
                scores = jnp.where(mask, scores, jnp.finfo(jnp.float32).min)
            p = jax.nn.softmax(scores.astype(jnp.float32), axis=-1).astype(q.dtype)
            return jnp.einsum('bhqk,bhkd->bhqd', p, v)

        def heads(x, nh, hd):
            b, l, _ = x.shape
            return x.reshape(b, l, nh, hd).transpose(0, 2, 1, 3)
        b, l, _ = hidden_states.shape
        vm = expert_mask(token_type_ids)[..., None]
        residual = hidden_states
        x = rms_norm(hidden_states, ln_in_w)
        mixed = jnp.where(vm, x @ v_qkv, x @ l_qkv)
        q, k, v = jnp.split(mixed, 3, axis=-1)
        q, k, v = (heads(q, NH, HD), heads(k, NH, HD), heads(v, NH, HD))
        q, k = apply_rotary(q, k, position_ids, l)
        ctx = sdpa(q, k, v, causal=True)
        ctx = ctx.transpose(0, 2, 1, 3).reshape(b, l, H)
        attn_out = jnp.where(vm, ctx @ v_dense, ctx @ l_dense)
        hidden_states = residual + attn_out
        ci = rms_norm(hidden_states, ln_post_cross_w)
        cq = heads(ci @ cq_w, NH, CHD)
        ckv = encoder_outputs @ ckv_w
        ck, cv = jnp.split(ckv, 2, axis=-1)
        ck, cv = (heads(ck, NH, CHD), heads(cv, NH, CHD))
        cctx = sdpa(cq, ck, cv, causal=False)
        cctx = cctx.transpose(0, 2, 1, 3).reshape(b, l, CC)
        hidden_states = hidden_states + cctx @ cdense_w
        mi = rms_norm(hidden_states, ln_post_attn_w)
        v_out = jax.nn.silu(mi @ v_gate) * (mi @ v_up) @ v_down
        l_out = jax.nn.silu(mi @ l_gate) * (mi @ l_up) @ l_down
        hidden_states = hidden_states + jnp.where(vm, v_out, l_out)
        return hidden_states

    def _L2_xattn_ref(x, media, media_mask, ln_q_g, ln_q_b, Wq, Wkv, Wo, attn_gate, ln_ff_g, ln_ff_b, W1, W2, ff_gate):
        import jax, jax.numpy as jnp
        import numpy as np
        DIM = 256
        DIM_MEDIA = 128
        HEADS = 16
        DIM_HEAD = 64
        INNER = HEADS * DIM_HEAD
        FF_INNER = 4 * DIM
        B, N_TOK, N_LAT = (4, 256, 64)
        EPS = 1e-05

        def layernorm(x, g, b):
            mu = jnp.mean(x, axis=-1, keepdims=True)
            var = jnp.var(x, axis=-1, keepdims=True)
            return (x - mu) * jax.lax.rsqrt(var + EPS) * g + b
        scale = DIM_HEAD ** (-0.5)
        qn = layernorm(x, ln_q_g, ln_q_b)
        q = qn @ Wq * scale
        kv = media @ Wkv
        k, v = jnp.split(kv, 2, axis=-1)
        split_heads = lambda t: t.reshape(t.shape[0], t.shape[1], HEADS, DIM_HEAD).transpose(0, 2, 1, 3)
        q, k, v = (split_heads(q), split_heads(k), split_heads(v))
        sim = jnp.einsum('bhid,bhjd->bhij', q, k)
        neg_inf = jnp.finfo(sim.dtype).min
        sim = jnp.where(media_mask[:, None, None, :], sim, neg_inf)
        attn = jax.nn.softmax(sim, axis=-1)
        out = jnp.einsum('bhij,bhjd->bhid', attn, v)
        out = out.transpose(0, 2, 1, 3).reshape(x.shape[0], x.shape[1], INNER)
        attn_out = out @ Wo
        x = x + jnp.tanh(attn_gate) * attn_out
        h = layernorm(x, ln_ff_g, ln_ff_b)
        h = jax.nn.gelu(h @ W1, approximate=False) @ W2
        x = x + jnp.tanh(ff_gate) * h
        return x

    def _L3_xattn_ref(hidden_states, memory, W_mem, W_gate, b_gate, norm_w):
        import jax, jax.numpy as jnp
        import numpy as np
        EPS = 1e-06

        def _rmsnorm(x, w):
            var = jnp.mean(jnp.square(x), axis=-1, keepdims=True)
            return x * jax.lax.rsqrt(var + EPS) * w
        D = hidden_states.shape[-1]
        memory_proj = jnp.einsum('bme,de->bmd', memory, W_mem)
        scores = jnp.einsum('bnd,bmd->bnm', hidden_states, memory_proj) / jnp.sqrt(jnp.float32(D))
        attn = jax.nn.softmax(scores, axis=-1)
        memory_context = jnp.einsum('bnm,bmd->bnd', attn, memory_proj)
        gate_input = jnp.concatenate([hidden_states, memory_context], axis=-1)
        gate = jax.nn.sigmoid(jnp.einsum('bnf,df->bnd', gate_input, W_gate) + b_gate)
        fused = hidden_states + gate * memory_context
        return _rmsnorm(fused, norm_w)
    x = _L0_xattn_ref(x, ctx_1024, L0_xattn_W_mem, L0_xattn_W_gate, L0_xattn_b_gate, L0_xattn_norm_w)
    x = _L1_xattn_ref(x, ctx_1024, mask_BxS_ik0, pos_1xS, L1_xattn_ln_in_w, L1_xattn_ln_post_attn_w, L1_xattn_ln_post_cross_w, L1_xattn_v_qkv, L1_xattn_l_qkv, L1_xattn_v_dense, L1_xattn_l_dense, L1_xattn_cq_w, L1_xattn_ckv_w, L1_xattn_cdense_w, L1_xattn_v_gate, L1_xattn_v_up, L1_xattn_v_down, L1_xattn_l_gate, L1_xattn_l_up, L1_xattn_l_down)
    x = _L2_xattn_ref(x, ctx_1024, mask_BxS2_bk0, L2_xattn_ln_q_g, L2_xattn_ln_q_b, L2_xattn_Wq, L2_xattn_Wkv, L2_xattn_Wo, L2_xattn_attn_gate, L2_xattn_ln_ff_g, L2_xattn_ln_ff_b, L2_xattn_W1, L2_xattn_W2, L2_xattn_ff_gate)
    x = _L3_xattn_ref(x, ctx_1024, L3_xattn_W_mem, L3_xattn_W_gate, L3_xattn_b_gate, L3_xattn_norm_w)
    return x

_drawn_inputs = setup_inputs


def setup_inputs(seed=0):
    import zlib

    import numpy as np

    out = dict(_drawn_inputs(seed))
    spreads = {'L0_xattn_norm_w': (1.0, 0.2),
     'L1_xattn_ln_in_w': (1.0, 0.6),
     'L1_xattn_ln_post_attn_w': (1.0, 0.6),
     'L1_xattn_ln_post_cross_w': (1.0, 0.6),
     'L2_xattn_ln_q_g': (1.0, 0.6),
     'L2_xattn_ln_q_b': (0.0, 0.8),
     'L2_xattn_ln_ff_g': (1.0, 0.6),
     'L2_xattn_ln_ff_b': (0.0, 0.8),
     'L3_xattn_norm_w': (1.0, 0.2)}
    factors = {'L0_xattn_b_gate': 21.845,
     'L1_xattn_v_qkv': 8.0,
     'L1_xattn_v_dense': 7.315,
     'L1_xattn_cq_w': 23.296,
     'L1_xattn_cdense_w': 2.705,
     'L1_xattn_v_gate': 5.962,
     'L1_xattn_v_up': 5.9,
     'L1_xattn_v_down': 5.945,
     'L2_xattn_W1': 3.12,
     'L2_xattn_W2': 2.818,
     'L3_xattn_b_gate': 57.187}
    for name, (base, spread) in spreads.items():
        noise = np.random.default_rng([zlib.crc32(name.encode()), seed]).standard_normal(out[name].shape)
        drawn = base * np.exp(spread * noise) if base else spread * noise
        out[name] = jnp.asarray(drawn.astype(out[name].dtype))
    for name, factor in factors.items():
        out[name] = (out[name] * factor).astype(out[name].dtype)
    return out
```

```python
from contextlib import ExitStack

import numpy as np

import concourse.bass as bass
from concourse import mybir

F32 = mybir.dt.float32
BF16 = mybir.dt.bfloat16
I32 = mybir.dt.int32
U8 = mybir.dt.uint8
ALU = mybir.AluOpType
ACT = mybir.ActivationFunctionType
AX = mybir.AxisListType

P = 128
B, S, D = 4, 256, 256
C = 128
LANES = 2
PAIRS = B // LANES
DC = D // P
ST = S // P
HEADS = 16
I_PAD = 768
IC = I_PAD // P
INNER = 1024
NC2 = INNER // P
BIG = 2.0 ** 100

SELF, CROSS, LATENT = range(3)
HEAD_DIM = [16, 8, 64]
SCALE = [16 ** -0.5, 8 ** -0.5, 64 ** -0.5]
GROUP = [4, 8, 1]
V_PAD = 56
VROW = V_PAD + HEADS * P


def columns(*sizes):
    at = [0]
    for s in sizes:
        at.append(at[-1] + s)
    return at


GM_MEM, GM_GATE, GM_END = columns(D, 2 * DC * D)
(A_VQKV, A_LQKV, A_VDENSE, A_LDENSE, A_CQ, A_CKV, A_CDENSE, A_END) = columns(
    DC * 3 * D, DC * 3 * D, DC * D, DC * D, DC * P, 2 * P, D)
(M_VGATE, M_LGATE, M_VUP, M_LUP, M_VDOWN, M_LDOWN, M_END) = columns(
    DC * I_PAD, DC * I_PAD, DC * I_PAD, DC * I_PAD, IC * D, IC * D)
(Q_WQ, Q_WKV, Q_END) = columns(DC * INNER, 2 * INNER)
(F_WO, F_W1, F_W2, F_END) = columns(NC2 * D, DC * INNER, NC2 * D)
VECTORS = ["L0_xattn_b_gate", "L0_xattn_norm_w", "L1_xattn_ln_in_w", "L1_xattn_ln_post_cross_w",
           "L1_xattn_ln_post_attn_w", "L2_xattn_ln_q_g", "L2_xattn_ln_q_b", "L2_xattn_ln_ff_g",
           "L2_xattn_ln_ff_b", "L3_xattn_b_gate", "L3_xattn_norm_w"]
VEC = {n: DC * i for i, n in enumerate(VECTORS)}
VEC_GATES = DC * len(VECTORS)
VEC_END = VEC_GATES + 2
(K_IDENT, K_ONES, K_ROT, K_HEAD16, K_HEAD8, K_HALF, K_IOTA, K_EPS, K_END) = columns(
    P, P, P, 8, 16, 2, 1, 2)
(T_COS, T_SIN, T_END) = columns(ST * P, ST * P)
(KB_IDENT, KB_CAUSAL, KB_CAUSAL_T, KB_SEL, KB_ONEROW, KB_END) = columns(P, S, S, HEADS * P, P)


class Signal:

    def __init__(self, sem, per_pass):
        self.sem, self.per_pass = sem, per_pass

    def at(self, it, k):
        return self.sem, it * self.per_pass + k


class Steps:

    def __init__(self, engine, raised, it):
        self.engine, self.raised, self.it, self.n = engine, raised, it, 0

    def done(self, instruction):
        self.n += 1
        instruction.then_inc(self.raised.sem, 1)
        self.engine.wait_ge(*self.raised.at(self.it, self.n))


def build(nc, x_d, ctx_d, pos_d, expert_d, keep_row_d, keep_col_d, gm_d, l1a_d, l1m_d, l2q_d, l2f_d,
          vec_d, const_d, constb_d, trig_d, out_d):
    with ExitStack() as stack:
        def sb(name, cols, dt=F32):
            return stack.enter_context(nc.sbuf_tensor(name, [P, cols], dt))

        def signal(name, per_pass=1):
            return Signal(stack.enter_context(nc.semaphore(name)), per_pass)

        gm_w = [sb(f"gm_w{g}", GM_END) for g in range(2)]
        attn_w = sb("attn_w", A_END)
        ffn_w = sb("ffn_w", M_END)
        vec = sb("vec", VEC_END)
        const = sb("const", K_END)
        constb = sb("constb", KB_END, BF16)
        cos = sb("cos", S)
        sin = sb("sin", S)
        tanh_gates = sb("tanh_gates", 2)
        pos_i = sb("pos_i", S, I32)

        weights_in = {n: signal(f"weights_in_{n}") for n in ("gm", "l1a", "l1m", "l2q", "l2f")}
        const_in = signal("const_in")
        onehot_ready = signal("onehot_ready")
        trig_done = signal("trig_done")
        trig_ready = signal("trig_ready")
        tanh_ready = signal("tanh_ready")
        pool_waits = signal("pool_waits")
        vec_step = signal("vec_step", 64)
        act_step = signal("act_step", 58)

        class Lane:
            def __init__(self, t):
                self.t = t

                def s(name, per_pass=1):
                    return signal(f"{name}_{'AB'[t]}", per_pass)

                def m(name, cols, dt=F32):
                    return sb(f"{name}_{'AB'[t]}", cols, dt)

                self.ps = stack.enter_context(nc.psum_tensor(f"ps_{'AB'[t]}", [P, 4, 512], F32))
                self.x = m("x", DC * S)
                self.ctx = m("ctx", S)
                self.kz = m("kz", HEADS * S)
                self.xin = self.kz[:, 0:DC * S]
                self.expert_i = self.kz[:, DC * S:DC * S + S].bitcast(I32)
                self.v = m("v", ST * VROW)
                self.big = m("big", NC2 * S)
                self.big2 = m("big2", NC2 * S)
                self.probs = m("probs", 2 * 512)
                self.xn = m("xn", DC * S)
                self.xv = m("xv", DC * S)
                self.xl = m("xl", DC * S)
                self.sq = self.probs[:, 0:DC * S]
                self.rstd = m("rstd", S)
                self.recip = self.xn[:]
                self.is_v = m("is_v", S)
                self.keep_col = m("keep_col", ST, U8)
                self.keep_row = m("keep_row", S, U8)
                self.key_bias = m("key_bias", ST)
                self.mask_row = m("mask_row", S, BF16)
                self.max = m("max", ST * HEADS)
                self.max_parts = m("max_parts", ST * 32, BF16)
                self.max_rows = m("max_rows", S, BF16)
                self.stat = m("stat", 8)

                self.inputs_in = s("inputs_in")
                self.out_in_dram = s("out_in_dram", 16)
                self.v_cleared = s("v_cleared", 3)
                self.v_resized = s("v_resized", 2)
                self.masks_ready = s("masks_ready")
                self.mem_done = s("mem_done", 4)
                self.mem_saved = s("mem_saved", 4)
                self.gm_scores = s("gm_scores", 2)
                self.gm_max = s("gm_max", 2)
                self.gm_exp = s("gm_exp", 4)
                self.gm_probs = s("gm_probs", 2)
                self.gm_turned = s("gm_turned", 2)
                self.gm_turned_saved = s("gm_turned_saved", 2)
                self.gm_context = s("gm_context", 2)
                self.gm_context_saved = s("gm_context_saved", 2)
                self.gate_done = s("gate_done", 2)
                self.gate_saved = s("gate_saved", 4)
                self.sum_done = s("sum_done", 2)
                self.sq_ready = s("sq_ready", 7)
                self.sumsq_done = s("sumsq_done", 7)
                self.rstd_ready = s("rstd_ready", 7)
                self.normed = s("normed", 7)
                self.split = s("split", 3)
                self.qk_done = s("qk_done", 2)
                self.qk_saved = s("qk_saved", 2)
                self.rot_done = s("rot_done")
                self.rotated = s("rotated")
                self.cross_done = s("cross_done")
                self.cross_saved = s("cross_saved")
                self.v_done = s("v_done", 6)
                self.v_saved = s("v_saved", 6)
                self.k_done = s("k_done", 4)
                self.q2_done = s("q2_done", 4)
                self.q2_saved = s("q2_saved", 4)
                self.key_ready = s("key_ready", 48)
                self.scores = s("scores", 48)
                self.max_ready = s("max_ready", 48)
                self.max_split = s("max_split", 3)
                self.max_turned = s("max_turned", 3)
                self.max_saved = s("max_saved", 3)
                self.scores_t = s("scores_t", 48)
                self.probs_ready = s("probs_ready", 48)
                self.pv_done = s("pv_done", 48)
                self.recip_ready = s("recip_ready", 22)
                self.head_out = s("head_out", 22)
                self.added_done = s("added_done", 5)
                self.added = s("added", 5)
                self.up_done = s("up_done", 6)
                self.silu_ready = s("silu_ready", 6)
                self.hidden = s("hidden", 6)
                self.w1_done = s("w1_done", 4)
                self.gelu_ready = s("gelu_ready", 4)

            def chunk(self, tile, c, lo=0, hi=S):
                return tile[:, c * S + lo:c * S + hi]

            def half(self, bank, h, lo=0, hi=S):
                return self.ps[:, bank, h * S + lo:h * S + hi]

            def values(self, a, h, kt):
                at = kt * VROW + V_PAD + h * P - HEAD_DIM[a] * (h % GROUP[a])
                return self.v[:, at:at + P]

            def slots(self, kt, lo, width):
                at = kt * VROW + V_PAD
                return self.v[:, at:at + HEADS * P].rearrange("p (h c) -> p h c", c=P)[:, :, lo:lo + width]

        lanes = [Lane(t) for t in range(LANES)]

        def w(tile, at, chunk, lo, hi, width):
            return tile[:, at + chunk * width + lo:at + chunk * width + hi]

        ident = const[:, K_IDENT:K_IDENT + P]
        ones = const[:, K_ONES:K_ONES + P]
        rot = const[:, K_ROT:K_ROT + P]
        identb = constb[:, KB_IDENT:KB_IDENT + P]
        onerow = constb[:, KB_ONEROW:KB_ONEROW + P]

        def sel(h):
            return constb[:, KB_SEL + h * P:KB_SEL + (h + 1) * P]

        GROUP_BASE = [0, 4, 6]

        block = stack.enter_context(nc.Block())

        @block.sync
        def _(sp):
            for L in lanes:
                sp.sem_inc(L.out_in_dram.sem, 16)
            sp.dma_start(const[:], const_d).then_inc(const_in.sem, 16)
            sp.dma_start(constb[:], constb_d.bitcast(BF16)).then_inc(const_in.sem, 16)
            sp.dma_start(lanes[1].big[:, 0:T_END], trig_d).then_inc(const_in.sem, 16)
            sp.dma_start(vec[:], vec_d).then_inc(const_in.sem, 16)
            sp.dma_start(pos_i[:], pos_d.rearrange("a s -> (a s)").partition_broadcast(P))\
                .then_inc(const_in.sem, 16)
            for g in range(2):
                sp.dma_start(gm_w[g][:], gm_d[g]).then_inc(weights_in["gm"].sem, 16)
            with sp.Fori(0, PAIRS) as it:
                for L in lanes:
                    for M in lanes:
                        sp.wait_ge(M.out_in_dram.sem, it * 16 + 16)
                    n = it * LANES + L.t
                    sp.dma_start(L.ctx[:], ctx_d[bass.ds(n, 1)].rearrange("a p n -> (a p) n"))\
                        .then_inc(L.inputs_in.sem, 16)
                    sp.dma_start(L.xin[:], x_d[bass.ds(n, 1)].rearrange("a p n -> (a p) n"))\
                        .then_inc(L.inputs_in.sem, 16)
                    sp.dma_start(L.expert_i[:],
                                 expert_d[bass.ds(n, 1)].rearrange("a s -> (a s)").partition_broadcast(P))\
                        .then_inc(L.inputs_in.sem, 16)
                    sp.dma_start(L.keep_col[:], keep_col_d[bass.ds(n, 1)].bitcast(U8).rearrange("a (p n) -> (a p) n", p=P))\
                        .then_inc(L.inputs_in.sem, 16)
                    sp.dma_start(L.keep_row[0:1, :], keep_row_d[bass.ds(n, 1)].bitcast(U8)).then_inc(L.inputs_in.sem, 16)
                sp.dma_start(attn_w[:], l1a_d).then_inc(weights_in["l1a"].sem, 16)
                sp.dma_start(ffn_w[:], l1m_d).then_inc(weights_in["l1m"].sem, 16)
                for L in lanes:
                    sp.wait_ge(*L.added_done.at(it, 2))
                sp.dma_start(attn_w[:, 0:Q_END], l2q_d).then_inc(weights_in["l2q"].sem, 16)
                for L in lanes:
                    sp.wait_ge(*L.added_done.at(it, 3))
                sp.dma_start(ffn_w[:, 0:F_END], l2f_d).then_inc(weights_in["l2f"].sem, 16)
                for L in lanes:
                    sp.wait_ge(*L.normed.at(it, 7))
                    n = it * LANES + L.t
                    sp.dma_start(out_d[bass.ds(n, 1)].rearrange("a p n -> (a p) n"), L.xn[:])\
                        .then_inc(L.out_in_dram.sem, 16)
            for L in lanes:
                sp.wait_ge(L.out_in_dram.sem, 16 + PAIRS * 16)

        @block.gpsimd
        def _(pool):
            def wait(sem, value):
                pool.wait_ge(sem, value)
                pool.sem_inc(pool_waits.sem, 1)

            with pool.Fori(0, PAIRS) as it:
                for L in lanes:
                    wait(L.out_in_dram.sem, it * 16 + 16)
                    nc.gpsimd.memset(L.v[:], 0.0).then_inc(L.v_cleared.sem, 1)
                    nc.gpsimd.memset(L.max_rows[:], 0.0)
                    nc.gpsimd.memset(L.mask_row[:], 0.0).then_inc(L.v_cleared.sem, 1)
                    wait(L.v_cleared.sem, it * 3 + 2)
                    for kt in range(ST):
                        last = nc.gpsimd.memset(L.slots(kt, 64, HEAD_DIM[SELF]), 1.0)
                    last.then_inc(L.v_cleared.sem, 1)
                for L in lanes:
                    wait(*L.pv_done.at(it, HEADS))
                    for kt in range(ST):
                        nc.gpsimd.memset(L.slots(kt, 8, 8), 0.0)
                        last = nc.gpsimd.memset(L.slots(kt, 72, 8), 0.0)
                    last.then_inc(L.v_resized.sem, 1)
                for L in lanes:
                    wait(*L.pv_done.at(it, 2 * HEADS))
                    for kt in range(ST):
                        last = nc.gpsimd.memset(L.slots(kt, 64, HEAD_DIM[LATENT]), 1.0)
                    last.then_inc(L.v_resized.sem, 1)

        @block.tensor
        def _(pe):
            mm = nc.tensor.matmul

            pe.wait_ge(const_in.sem, 80)
            pe.wait_ge(onehot_ready.sem, 1)
            for half, table in enumerate((T_COS, T_SIN)):
                for c in range(ST):
                    last = mm(lanes[0].half(0, half), lanes[1].big[:, table + c * P:table + (c + 1) * P],
                              lanes[0].chunk(lanes[0].big, c), start=(c == 0), stop=(c == ST - 1))
            last.then_inc(trig_done.sem, 1)
            pe.wait_ge(weights_in["gm"].sem, 32)

            with pe.Fori(0, PAIRS) as it:
                for L in lanes:
                    pe.wait_ge(L.out_in_dram.sem, it * 16 + 16)
                pe.wait_ge(trig_ready.sem, 1)

                def memory_projection(L, g):
                    W = gm_w[g]
                    if g == 0:
                        pe.wait_ge(L.inputs_in.sem, it * 80 + 80)
                    else:
                        pe.wait_ge(*L.added.at(it, 5))
                    for c in range(DC):
                        last = mm(L.half(0, c), W[:, GM_MEM + c * P:GM_MEM + (c + 1) * P], L.ctx[:, 0:S],
                                  start=True, stop=True)
                    last.then_inc(L.mem_done.sem, 1)
                    for kt in range(ST):
                        last = mm(L.half(1, kt), L.ctx[:, kt * P:(kt + 1) * P], W[:, GM_MEM:GM_MEM + D],
                                  start=True, stop=True)
                    last.then_inc(L.mem_done.sem, 1)

                def gm_scores(L, g):
                    x = L.xin if g == 0 else L.x
                    pe.wait_ge(*L.mem_saved.at(it, 2 * g + 1))
                    for qt in range(ST):
                        for c in range(DC):
                            last = mm(L.half(2, qt), L.chunk(x, c, qt * P, (qt + 1) * P),
                                      L.chunk(L.big2, c), start=(c == 0), stop=(c == DC - 1))
                    last.then_inc(L.gm_scores.sem, 1)

                def gm_turn(L, g):
                    pe.wait_ge(*L.gm_probs.at(it, g + 1))
                    for kt in range(ST):
                        for qt in range(ST):
                            last = nc.tensor.transpose(L.half(3, kt, qt * P, (qt + 1) * P),
                                                       L.chunk(L.big, qt, kt * P, (kt + 1) * P), ident)
                    last.then_inc(L.gm_turned.sem, 1)

                def gm_context(L, g):
                    pe.wait_ge(*L.mem_saved.at(it, 2 * g + 2))
                    pe.wait_ge(*L.gm_turned_saved.at(it, g + 1))
                    for c in range(DC):
                        for kt in range(ST):
                            last = mm(L.half(0, c), L.chunk(L.big2, 2 + kt, c * P, (c + 1) * P),
                                      L.chunk(L.big, 2 + kt), start=(kt == 0), stop=(kt == ST - 1))
                    last.then_inc(L.gm_context.sem, 1)

                def gm_gate(L, g):
                    x = L.xin if g == 0 else L.x
                    pe.wait_ge(*L.gm_context_saved.at(it, g + 1))
                    for c in range(DC):
                        for f in range(2 * DC):
                            src = L.chunk(x, f) if f < DC else L.chunk(L.xv, f - DC)
                            last = mm(L.half(1, c), w(gm_w[g], GM_GATE, f, c * P, (c + 1) * P, D), src,
                                      start=(f == 0), stop=(f == 2 * DC - 1))
                    last.then_inc(L.gate_done.sem, 1)

                def sum_squares(L, n):
                    pe.wait_ge(*L.sq_ready.at(it, n + 1))
                    for c in range(DC):
                        last = mm(L.half(2, 0), ones, L.chunk(L.sq, c), start=(c == 0), stop=(c == DC - 1))
                    last.then_inc(L.sumsq_done.sem, 1)

                def layer_norm_sum(L, n):
                    pe.wait_ge(*L.added.at(it, 3 + n))
                    pe.wait_ge(*L.v_saved.at(it, 6))
                    for c in range(DC):
                        last = mm(L.half(3, 0), ones, L.chunk(L.x, c), start=(c == 0), stop=(c == DC - 1))
                    last.then_inc(L.sum_done.sem, 1)

                def self_qkv(L):
                    if L.t == 0:
                        pe.wait_ge(weights_in["l1a"].sem, it * 16 + 16)
                    pe.wait_ge(*L.split.at(it, 1))
                    parts = [(A_VQKV, L.xv, c) for c in range(DC)] + [(A_LQKV, L.xl, c) for c in range(DC)]
                    for m in range(4):
                        for i, (at, src, c) in enumerate(parts):
                            last = mm(L.half(m // 2, m % 2), w(attn_w, at, c, m * P, (m + 1) * P, 3 * D),
                                      L.chunk(src, c), start=(i == 0), stop=(i == 3))
                        if m % 2:
                            last.then_inc(L.qk_done.sem, 1)
                    for kt in range(ST):
                        for i, (at, src, c) in enumerate(parts):
                            last = mm(L.half(3, kt), L.chunk(src, c, kt * P, (kt + 1) * P),
                                      w(attn_w, at, c, 2 * D, 3 * D, 3 * D), start=(i == 0), stop=(i == 3))
                    last.then_inc(L.v_done.sem, 1)

                def rotate_halves(L):
                    pe.wait_ge(*L.qk_saved.at(it, 2))
                    for m in range(4):
                        last = mm(L.half(m // 2, m % 2), rot, L.chunk(L.big, m), start=True, stop=True)
                    last.then_inc(L.rot_done.sem, 1)

                def query(L, a, h):
                    if a == SELF:
                        return lambda lo, hi: L.chunk(L.big, 4 + h // 8, lo, hi)
                    return lambda lo, hi: L.chunk(L.big, 0 if a == CROSS else h // 2, lo, hi)

                def scores_for_max(L, a):
                    if a == LATENT:
                        pe.wait_ge(*L.q2_saved.at(it, 4))
                        pe.wait_ge(*L.masks_ready.at(it, 1))
                    for h in range(HEADS):
                        n = a * HEADS + h
                        pe.wait_ge(*L.key_ready.at(it, n + 1))
                        if h >= 4:
                            pe.wait_ge(*L.max_ready.at(it, n - 3))
                        elif h == 0 and a == SELF:
                            pe.wait_ge(*L.v_saved.at(it, 1))
                        bank, q = h % 4, query(L, a, h)
                        if a == SELF:
                            mm(L.ps[:, bank, 0:P], q(0, P), L.chunk(L.kz, h, 0, P), start=True, stop=False)
                            mm(L.ps[:, bank, 0:P], identb, constb[:, KB_CAUSAL + P:KB_CAUSAL + S],
                               start=False, stop=True)
                            mm(L.ps[:, bank, P:P + S], q(P, S), L.chunk(L.kz, h), start=True, stop=False)
                            last = mm(L.ps[:, bank, P:P + S], identb, constb[:, KB_CAUSAL:KB_CAUSAL + S],
                                      start=False, stop=True)
                        else:
                            for qt in range(ST):
                                last = mm(L.half(bank, qt), q(qt * P, (qt + 1) * P), L.chunk(L.kz, h),
                                          start=True, stop=(a == CROSS))
                                if a == LATENT:
                                    last = mm(L.half(bank, qt), onerow, L.mask_row[:], start=False, stop=True)
                        last.then_inc(L.scores.sem, 1)

                def turn_max(L, a):
                    pe.wait_ge(*L.max_split.at(it, a + 1))
                    pe.wait_ge(*L.max_ready.at(it, a * HEADS + HEADS))
                    turned = L.ps[0:32, 3, 0:P].bitcast(BF16)
                    for qt in range(ST):
                        last = nc.tensor.transpose(turned[:, qt * P:(qt + 1) * P],
                                                   L.max_parts[:, qt * 32:(qt + 1) * 32], identb)
                    last.then_inc(L.max_turned.sem, 1)

                def attend(L, a):
                    def scores(h):
                        n = a * HEADS + h
                        if h == 0:
                            pe.wait_ge(*L.max_saved.at(it, a + 1))
                        if h >= 2:
                            pe.wait_ge(*L.probs_ready.at(it, n - 1))
                        bank, q = h % 2, query(L, a, h)
                        for kt in range(ST):
                            lo = kt * P if a == SELF else 0
                            out = L.ps[:, bank, kt * S:kt * S + S - lo]
                            mm(out, L.chunk(L.kz, h, kt * P, (kt + 1) * P), q(lo, S), start=True, stop=False)
                            if a == SELF:
                                mm(out, identb, constb[:, KB_CAUSAL_T:KB_CAUSAL_T + S - lo],
                                   start=False, stop=False)
                            last = mm(out, sel(h), L.max_rows[:, lo:S], start=False, stop=True)
                        last.then_inc(L.scores_t.sem, 1)

                    def weigh(h):
                        n = a * HEADS + h
                        g = h // GROUP[a]
                        if h % GROUP[a] == 0 and g >= 2:
                            pe.wait_ge(*L.head_out.at(it, GROUP_BASE[a] + g - 1))
                        pe.wait_ge(*L.probs_ready.at(it, n + 1))
                        if h == 0:
                            pe.wait_ge(*L.v_saved.at(it, [1, 2, 6][a]))
                            if a > SELF:
                                pe.wait_ge(*L.v_resized.at(it, a))
                        for kt in range(ST):
                            lo = kt * P if a == SELF else 0
                            at = (h % 2) * 512 + kt * S
                            last = mm(L.ps[:, 2 + g % 2, lo:S], L.values(a, h, kt),
                                      L.probs[:, at:at + S - lo],
                                      start=(h % GROUP[a] == 0 and kt == 0),
                                      stop=(h % GROUP[a] == GROUP[a] - 1 and kt == ST - 1))
                        last.then_inc(L.pv_done.sem, 1)

                    for h in range(HEADS + 1):
                        if h < HEADS:
                            scores(h)
                        if h >= 1:
                            weigh(h - 1)

                def self_dense(L):
                    pe.wait_ge(*L.split.at(it, 2))
                    for m in range(DC):
                        i = 0
                        for at, src in ((A_VDENSE, L.xv), (A_LDENSE, L.xl)):
                            for c in range(DC):
                                last = mm(L.half(0, m), w(attn_w, at, c, m * P, (m + 1) * P, D),
                                          L.chunk(src, c), start=(i == 0), stop=(i == 3))
                                i += 1
                    last.then_inc(L.added_done.sem, 1)

                def cross_qkv(L):
                    pe.wait_ge(*L.normed.at(it, 3))
                    for c in range(DC):
                        mm(L.half(0, 0), w(attn_w, A_CQ, c, 0, P, P), L.chunk(L.xn, c),
                           start=(c == 0), stop=(c == DC - 1))
                    mm(L.half(0, 1), attn_w[:, A_CKV:A_CKV + P], L.ctx[:], start=True, stop=True)\
                        .then_inc(L.cross_done.sem, 1)
                    for kt in range(ST):
                        last = mm(L.ps[:, 1, kt * P:(kt + 1) * P], L.ctx[:, kt * P:(kt + 1) * P],
                                  attn_w[:, A_CKV + P:A_CKV + 2 * P], start=True, stop=True)
                    last.then_inc(L.v_done.sem, 1)

                def cross_dense(L):
                    pe.wait_ge(*L.head_out.at(it, GROUP_BASE[CROSS] + 2))
                    for m in range(DC):
                        last = mm(L.half(0, m), attn_w[:, A_CDENSE + m * P:A_CDENSE + (m + 1) * P],
                                  L.chunk(L.big2, 0), start=True, stop=True)
                    last.then_inc(L.added_done.sem, 1)

                def experts_up(L):
                    if L.t == 0:
                        pe.wait_ge(weights_in["l1m"].sem, it * 16 + 16)
                    pe.wait_ge(*L.split.at(it, 3))
                    for m in range(IC):
                        if m >= 4:
                            pe.wait_ge(*L.hidden.at(it, m - 3))
                        for half, (wv, wl) in enumerate(((M_VGATE, M_LGATE), (M_VUP, M_LUP))):
                            i = 0
                            for at, src in ((wv, L.xv), (wl, L.xl)):
                                for c in range(DC):
                                    last = mm(L.half(m % 4, half), w(ffn_w, at, c, m * P, (m + 1) * P, I_PAD),
                                              L.chunk(src, c), start=(i == 0), stop=(i == 3))
                                    i += 1
                        last.then_inc(L.up_done.sem, 1)

                def experts_down(L):
                    for m in range(DC):
                        i = 0
                        for k in range(IC):
                            if m == 0:
                                pe.wait_ge(*L.hidden.at(it, max(k + 1, 4)))
                            for at, src in ((M_VDOWN, L.big), (M_LDOWN, L.big2)):
                                last = mm(L.half(2 + m, 0), w(ffn_w, at, k, m * P, (m + 1) * P, D),
                                          L.chunk(src, k), start=(i == 0), stop=(i == 2 * IC - 1))
                                i += 1
                    last.then_inc(L.added_done.sem, 1)

                def latent_kv(L):
                    if L.t == 0:
                        pe.wait_ge(weights_in["l2q"].sem, it * 16 + 16)
                    pe.wait_ge(*L.added.at(it, 3))
                    for m in range(NC2):
                        last = mm(L.half(m // 2, m % 2), attn_w[:, Q_WKV + m * P:Q_WKV + (m + 1) * P],
                                  L.ctx[:], start=True, stop=True)
                        if m % 2:
                            last.then_inc(L.k_done.sem, 1)
                    for j in range(4):
                        kt, n = j // 2, j % 2
                        pe.wait_ge(*L.key_ready.at(it, LATENT * HEADS + 4 * j + 4))
                        mm(L.ps[:, j, :], L.ctx[:, kt * P:(kt + 1) * P],
                           attn_w[:, Q_WKV + INNER + n * 512:Q_WKV + INNER + (n + 1) * 512],
                           start=True, stop=True).then_inc(L.v_done.sem, 1)

                def latent_q(L):
                    pe.wait_ge(*L.normed.at(it, 5))
                    for m in range(NC2):
                        if m % 2 == 0:
                            pe.wait_ge(*L.v_saved.at(it, 3 + m // 2))
                        for c in range(DC):
                            last = mm(L.half(m // 2, m % 2), w(attn_w, Q_WQ, c, m * P, (m + 1) * P, INNER),
                                      L.chunk(L.xn, c), start=(c == 0), stop=(c == DC - 1))
                        if m % 2:
                            last.then_inc(L.q2_done.sem, 1)

                def latent_dense(L):
                    if L.t == 0:
                        pe.wait_ge(weights_in["l2f"].sem, it * 16 + 16)
                    pe.wait_ge(*L.head_out.at(it, GROUP_BASE[LATENT] + HEADS))
                    for m in range(DC):
                        for k in range(NC2):
                            last = mm(L.half(0, m), w(ffn_w, F_WO, k, m * P, (m + 1) * P, D),
                                      L.chunk(L.big2, k), start=(k == 0), stop=(k == NC2 - 1))
                    last.then_inc(L.added_done.sem, 1)

                def ffn_up(L):
                    pe.wait_ge(*L.normed.at(it, 6))
                    for m in range(NC2):
                        for c in range(DC):
                            last = mm(L.half(m // 2, m % 2), w(ffn_w, F_W1, c, m * P, (m + 1) * P, INNER),
                                      L.chunk(L.xn, c), start=(c == 0), stop=(c == DC - 1))
                        if m % 2:
                            last.then_inc(L.w1_done.sem, 1)

                def ffn_down(L):
                    for m in range(DC):
                        for k in range(NC2):
                            if m == 0 and k % 2 == 0:
                                pe.wait_ge(*L.gelu_ready.at(it, k // 2 + 1))
                            last = mm(L.half(0, m), w(ffn_w, F_W2, k, m * P, (m + 1) * P, D),
                                      L.chunk(L.big, k), start=(k == 0), stop=(k == NC2 - 1))
                    last.then_inc(L.added_done.sem, 1)

                def each(stage, *args):
                    for L in lanes:
                        stage(L, *args)

                def gated_memory(g):
                    each(memory_projection, g)
                    each(gm_scores, g)
                    each(gm_turn, g)
                    each(gm_context, g)
                    each(gm_gate, g)

                gated_memory(0)
                each(sum_squares, 0)
                each(sum_squares, 1)
                each(self_qkv)
                each(rotate_halves)
                each(scores_for_max, SELF)
                each(turn_max, SELF)
                each(attend, SELF)
                each(self_dense)
                each(sum_squares, 2)
                each(cross_qkv)
                each(scores_for_max, CROSS)
                each(turn_max, CROSS)
                each(attend, CROSS)
                each(cross_dense)
                each(sum_squares, 3)
                each(experts_up)
                each(experts_down)
                each(latent_kv)
                each(layer_norm_sum, 0)
                each(sum_squares, 4)
                each(latent_q)
                each(scores_for_max, LATENT)
                each(turn_max, LATENT)
                each(attend, LATENT)
                each(latent_dense)
                each(layer_norm_sum, 1)
                each(sum_squares, 5)
                each(ffn_up)
                each(ffn_down)
                gated_memory(1)
                each(sum_squares, 6)

        @block.scalar
        def _(act):
            fn = nc.scalar.activation
            act.wait_ge(const_in.sem, 80)
            fn(tanh_gates[:], vec[:, VEC_GATES:VEC_GATES + 2], ACT.Tanh).then_inc(tanh_ready.sem, 1)
            act.wait_ge(trig_done.sem, 1)
            fn(cos[:], lanes[0].half(0, 0), ACT.Copy)
            fn(sin[:], lanes[0].half(0, 1), ACT.Copy).then_inc(trig_ready.sem, 1)

            with act.Fori(0, PAIRS) as it:
                step = Steps(act, act_step, it)
                nc.scalar.preload_act_table_set("natural_log_exp_and_others")
                for L in lanes:
                    act.wait_ge(L.out_in_dram.sem, it * 16 + 16)

                def memory_save(L, g):
                    for j in range(2):
                        act.wait_ge(*L.mem_done.at(it, 2 * g + j + 1))
                        fn(L.big2[:, j * 512:(j + 1) * 512], L.ps[:, j, :], ACT.Copy)\
                            .then_inc(L.mem_saved.sem, 1)

                def gm_exp(L, g):
                    act.wait_ge(*L.gm_max.at(it, g + 1))
                    for qt in range(ST):
                        fn(L.chunk(L.big, qt), L.half(2, qt), ACT.Exp, bias=L.stat[:, 2 + qt:3 + qt],
                           scale=D ** -0.5, accum_out=L.stat[:, 4 + qt:5 + qt]).then_inc(L.gm_exp.sem, 1)

                def gm_context_save(L, g):
                    act.wait_ge(*L.gm_context.at(it, g + 1))
                    fn(L.xv[:], L.ps[:, 0, :], ACT.Copy).then_inc(L.gm_context_saved.sem, 1)

                def gm_sigmoid(L, g):
                    bg = VEC[["L0_xattn_b_gate", "L3_xattn_b_gate"][g]]
                    act.wait_ge(*L.gate_done.at(it, g + 1))
                    for c in range(DC):
                        fn(L.chunk(L.xl, c), L.half(1, c), ACT.Sigmoid, bias=vec[:, bg + c:bg + c + 1])\
                            .then_inc(L.gate_saved.sem, 1)

                def rstd(L, n):
                    eps = const[:, K_EPS + (n in (4, 5)):K_EPS + (n in (4, 5)) + 1]
                    act.wait_ge(*L.sumsq_done.at(it, n + 1))
                    step.done(fn(L.rstd[:], L.half(2, 0), ACT.Ln, bias=eps, scale=1.0 / D))
                    fn(L.rstd[:], L.rstd[:], ACT.Exp, scale=-0.5).then_inc(L.rstd_ready.sem, 1)

                def qk_save(L):
                    for j in range(2):
                        act.wait_ge(*L.qk_done.at(it, j + 1))
                        fn(L.big[:, j * 512:(j + 1) * 512], L.ps[:, j, :], ACT.Copy)\
                            .then_inc(L.qk_saved.sem, 1)

                def cross_save(L):
                    act.wait_ge(*L.cross_done.at(it, 1))
                    fn(L.big[:, 0:512], L.ps[:, 0, :], ACT.Copy).then_inc(L.cross_saved.sem, 1)

                def latent_v_save(L):
                    for j in range(4):
                        kt, n = j // 2, j % 2
                        act.wait_ge(*L.v_done.at(it, 3 + j))
                        act.wait_ge(*L.pv_done.at(it, 2 * HEADS))
                        fn(L.slots(kt, 0, 64)[:, n * 8:n * 8 + 8, :],
                           L.ps[:, j, :].rearrange("p (h d) -> p h d", h=8), ACT.Copy)\
                            .then_inc(L.v_saved.sem, 1)

                def latent_q_save(L):
                    for j in range(4):
                        act.wait_ge(*L.q2_done.at(it, j + 1))
                        fn(L.big[:, j * 512:(j + 1) * 512], L.ps[:, j, :], ACT.Copy)\
                            .then_inc(L.q2_saved.sem, 1)

                def max_save(L, a):
                    act.wait_ge(*L.max_turned.at(it, a + 1))
                    act.wait_ge(L.v_cleared.sem, it * 3 + 3)
                    fn(L.max_rows[0:32, :], L.ps[0:32, 3, 0:P].bitcast(BF16), ACT.Copy)\
                        .then_inc(L.max_saved.sem, 1)

                def probabilities(L, a):
                    def exps(h):
                        n = a * HEADS + h
                        act.wait_ge(*L.scores_t.at(it, n + 1))
                        if h >= 2:
                            act.wait_ge(*L.pv_done.at(it, n - 1))
                        dst = L.probs[:, (h % 2) * 512:(h % 2 + 1) * 512]
                        if a == LATENT:
                            for kt in range(ST):
                                last = fn(dst[:, kt * S:(kt + 1) * S], L.half(h % 2, kt), ACT.Exp,
                                          bias=L.key_bias[:, kt:kt + 1], scale=SCALE[a])
                        else:
                            cols = S + P if a == SELF else 2 * S
                            last = fn(dst[:, 0:cols], L.ps[:, h % 2, 0:cols], ACT.Exp, scale=SCALE[a])
                        last.then_inc(L.probs_ready.sem, 1)

                    def reciprocals(g):
                        r = L.recip[0:64, (g % 2) * S:(g % 2 + 1) * S]
                        act.wait_ge(*L.pv_done.at(it, a * HEADS + (g + 1) * GROUP[a]))
                        if g >= 2:
                            act.wait_ge(*L.head_out.at(it, GROUP_BASE[a] + g - 1))
                        step.done(fn(r, L.ps[64:P, 2 + g % 2, 0:S], ACT.Ln))
                        fn(r, r, ACT.Exp, scale=-1.0).then_inc(L.recip_ready.sem, 1)

                    for h in range(HEADS + 1):
                        if h < HEADS:
                            exps(h)
                        if h >= 1 and h % GROUP[a] == 0:
                            reciprocals(h // GROUP[a] - 1)

                def silu(L):
                    for m in range(IC):
                        act.wait_ge(*L.up_done.at(it, m + 1))
                        if m >= 2:
                            act.wait_ge(*L.hidden.at(it, m - 1))
                        fn(L.probs[:, (m % 2) * 512:(m % 2) * 512 + S], L.half(m % 4, 0), ACT.Silu)\
                            .then_inc(L.silu_ready.sem, 1)

                def gelu(L):
                    for j in range(4):
                        act.wait_ge(*L.w1_done.at(it, j + 1))
                        fn(L.big[:, j * 512:(j + 1) * 512], L.ps[:, j, :], ACT.Gelu)\
                            .then_inc(L.gelu_ready.sem, 1)

                def each(stage, *args):
                    for L in lanes:
                        stage(L, *args)

                def log_exp_table():
                    nc.scalar.preload_act_table_set("natural_log_exp_and_others")

                def gated_memory(g):
                    each(memory_save, g)
                    each(gm_exp, g)
                    each(gm_context_save, g)
                    each(gm_sigmoid, g)
                    log_exp_table()

                gated_memory(0)
                each(rstd, 0)
                each(rstd, 1)
                each(qk_save)
                each(max_save, SELF)
                each(probabilities, SELF)
                each(rstd, 2)
                each(cross_save)
                each(max_save, CROSS)
                each(probabilities, CROSS)
                each(rstd, 3)
                each(silu)
                log_exp_table()
                each(latent_v_save)
                each(rstd, 4)
                each(latent_q_save)
                each(max_save, LATENT)
                each(probabilities, LATENT)
                each(rstd, 5)
                each(gelu)
                log_exp_table()
                gated_memory(1)
                each(rstd, 6)
                assert step.n == act_step.per_pass, step.n

        @block.vector
        def _(dve):
            tt = nc.vector.tensor_tensor
            ts = nc.vector.tensor_scalar
            stt = nc.vector.scalar_tensor_tensor

            dve.wait_ge(const_in.sem, 80)
            for c in range(ST):
                last = ts(lanes[0].chunk(lanes[0].big, c), pos_i[:], const[:, K_IOTA:K_IOTA + 1], float(c * P),
                          ALU.subtract, ALU.is_equal)
            last.then_inc(onehot_ready.sem, 1)

            def lines(tile, n, cols=S):
                return tile.rearrange("p (n s) -> p n s", s=cols)

            def spread(row, n):
                return row.unsqueeze(1).to_broadcast([P, n, S])

            with dve.Fori(0, PAIRS) as it:
                step = Steps(dve, vec_step, it)
                for L in lanes:
                    dve.wait_ge(L.out_in_dram.sem, it * 16 + 16)

                def masks(L):
                    dve.wait_ge(L.inputs_in.sem, it * 80 + 80)
                    step.done(ts(L.sq[:, 0:S], L.expert_i[:], 1.0, None, ALU.is_equal))
                    tt(L.is_v[:, 0:S - 1], L.sq[:, 0:S - 1], L.sq[:, 1:S], ALU.mult)
                    nc.vector.memset(L.is_v[:, S - 1:S], 0.0)
                    ts(L.key_bias[:], L.keep_col[:], 0.0, -BIG * SCALE[LATENT], ALU.is_equal, ALU.mult)
                    dve.wait_ge(L.v_cleared.sem, it * 3 + 3)
                    ins = ts(L.mask_row[0:1, :], L.keep_row[0:1, :], 0.0, -BIG, ALU.is_equal, ALU.mult)
                    ins.then_inc(L.masks_ready.sem, 1)
                    dve.wait_ge(*L.masks_ready.at(it, 1))

                def gm_max(L, g):
                    dve.wait_ge(*L.gm_scores.at(it, g + 1))
                    step.done(nc.vector.tensor_reduce(L.stat[:, 0:2], L.ps[:, 2, :].rearrange(
                        "p (q k) -> p q k", q=ST), AX.X, ALU.max))
                    ts(L.stat[:, 2:4], L.stat[:, 0:2], -D ** -0.5, None, ALU.mult).then_inc(L.gm_max.sem, 1)

                def gm_normalise(L, g):
                    dve.wait_ge(*L.gm_exp.at(it, 2 * g + 2))
                    step.done(nc.vector.reciprocal(L.stat[:, 6:8], L.stat[:, 4:6]))
                    for qt in range(ST):
                        last = ts(L.chunk(L.big, qt), L.chunk(L.big, qt), L.stat[:, 6 + qt:7 + qt], None, ALU.mult)
                    last.then_inc(L.gm_probs.sem, 1)

                def gm_turned_save(L, g):
                    dve.wait_ge(*L.gm_turned.at(it, g + 1))
                    nc.vector.tensor_copy(L.big[:, 512:1024], L.ps[:, 3, :]).then_inc(L.gm_turned_saved.sem, 1)

                def gm_fuse(L, g):
                    x = L.xin if g == 0 else L.x
                    dve.wait_ge(*L.gate_saved.at(it, 2 * g + 2))
                    step.done(tt(L.xl[:], L.xl[:], L.xv[:], ALU.mult))
                    step.done(tt(L.xl[:], L.xl[:], x[:], ALU.add))

                def square(L, src):
                    tt(L.sq[:], src[:], src[:], ALU.mult).then_inc(L.sq_ready.sem, 1)

                def normalise(L, n, src, dst, weight, bias=None):
                    at = VEC[weight]
                    dve.wait_ge(*L.rstd_ready.at(it, n + 1))
                    for c in range(DC):
                        last = stt(out=L.chunk(dst, c), in0=L.chunk(src, c), scalar=vec[:, at + c:at + c + 1],
                                   in1=L.rstd[:], op0=ALU.mult, op1=ALU.mult)
                    if bias:
                        step.done(last)
                        at = VEC[bias]
                        for c in range(DC):
                            last = ts(L.chunk(dst, c), L.chunk(dst, c), vec[:, at + c:at + c + 1], None, ALU.add)
                    last.then_inc(L.normed.sem, 1)
                    dve.wait_ge(*L.normed.at(it, n + 1))

                def split(L, src):
                    step.done(tt(lines(L.xv[:], DC), lines(src, DC), spread(L.is_v[:], DC), ALU.mult))
                    tt(L.xl[:], src, L.xv[:], ALU.subtract).then_inc(L.split.sem, 1)

                def self_values(L):
                    dve.wait_ge(*L.v_done.at(it, 1))
                    dve.wait_ge(L.v_cleared.sem, it * 3 + 3)
                    for kt in range(ST):
                        last = nc.vector.tensor_copy(L.slots(kt, 0, HEAD_DIM[SELF]), L.half(3, kt).rearrange(
                            "p (h d) -> p h d", h=HEADS))
                    last.then_inc(L.v_saved.sem, 1)

                def rotate(L):
                    dve.wait_ge(*L.qk_saved.at(it, 2))
                    tt(lines(L.big2[:, 0:1024], 4), lines(L.big[:, 0:1024], 4), spread(cos[:], 4), ALU.mult)
                    dve.wait_ge(*L.rot_done.at(it, 1))
                    step.done(tt(lines(L.big2[:, 1024:2048], 4),
                                 L.ps[:, 0:2, :].rearrange("p b (n s) -> p (b n) s", s=S), spread(sin[:], 4),
                                 ALU.mult))
                    last = tt(L.big[:, 1024:2048], L.big2[:, 0:1024], L.big2[:, 1024:2048], ALU.add)
                    last.then_inc(L.rotated.sem, 1)
                    dve.wait_ge(*L.rotated.at(it, 1))

                def keys(L, a):
                    if a == CROSS:
                        dve.wait_ge(*L.cross_saved.at(it, 1))
                    if a > SELF:
                        dve.wait_ge(*L.scores_t.at(it, a * HEADS))
                    for h in range(HEADS):
                        if a == SELF:
                            src, mask = L.chunk(L.big, 6 + h // 8), K_HEAD16 + h % 8
                        elif a == CROSS:
                            src, mask = L.chunk(L.big, 1), K_HEAD8 + h
                        else:
                            if h % 4 == 0:
                                dve.wait_ge(*L.k_done.at(it, h // 4 + 1))
                            src, mask = L.half(h // 4, h // 2 % 2), K_HALF + h % 2
                        ts(L.chunk(L.kz, h), src, const[:, mask:mask + 1], None, ALU.mult)\
                            .then_inc(L.key_ready.sem, 1)

                def cross_values(L):
                    dve.wait_ge(*L.v_done.at(it, 2))
                    dve.wait_ge(*L.pv_done.at(it, HEADS))
                    for kt in range(ST):
                        last = nc.vector.tensor_copy(
                            L.slots(kt, 0, HEAD_DIM[CROSS]),
                            L.ps[:, 1, kt * P:(kt + 1) * P].rearrange("p (h d) -> p h d", h=HEADS))
                    last.then_inc(L.v_saved.sem, 1)

                def maxima(L, a):
                    for h in range(HEADS):
                        n = a * HEADS + h
                        dve.wait_ge(*L.scores.at(it, n + 1))
                        mx = L.max[:].rearrange("p (q h) -> p q h", q=ST)
                        if a == SELF:
                            nc.vector.tensor_reduce(mx[:, 0:1, h], L.ps[:, h % 4, 0:P], AX.X, ALU.max)
                            last = nc.vector.tensor_reduce(mx[:, 1:2, h], L.ps[:, h % 4, P:P + S], AX.X, ALU.max)
                        else:
                            last = nc.vector.tensor_reduce(mx[:, :, h], L.ps[:, h % 4, :].rearrange(
                                "p (q k) -> p q k", q=ST), AX.X, ALU.max)
                        last.then_inc(L.max_ready.sem, 1)
                    dve.wait_ge(*L.max_ready.at(it, a * HEADS + HEADS))
                    parts = L.max_parts[:].rearrange("p (q n h) -> p q n h", q=ST, n=2)
                    mx = L.max[:].rearrange("p (q h) -> p q h", q=ST)
                    step.done(nc.vector.tensor_copy(parts[:, :, 0, :], mx))
                    tt(parts[:, :, 1, :], mx, parts[:, :, 0, :], ALU.subtract).then_inc(L.max_split.sem, 1)

                def head_outputs(L, a):
                    for g in range(HEADS // GROUP[a]):
                        dve.wait_ge(*L.recip_ready.at(it, GROUP_BASE[a] + g + 1))
                        lo = 64 * (g % 2)
                        tt(L.big2[lo:lo + 64, (g // 2) * S:(g // 2 + 1) * S], L.ps[0:64, 2 + g % 2, 0:S],
                           L.recip[0:64, (g % 2) * S:(g % 2 + 1) * S], ALU.mult).then_inc(L.head_out.sem, 1)

                def split_context(L):
                    dve.wait_ge(*L.head_out.at(it, 4))
                    split(L, L.big2[:, 0:512])

                def add(L, n):
                    dve.wait_ge(*L.added_done.at(it, n + 1))
                    src = L.ps[:, 2:4, 0:S] if n == 2 else L.ps[:, 0, :].rearrange("p (c s) -> p c s", s=S)
                    x = L.x[:].rearrange("p (c s) -> p c s", s=S)
                    if n < 3:
                        last = tt(x, src, x, ALU.add)
                    else:
                        if n == 3:
                            dve.wait_ge(tanh_ready.sem, 1)
                        last = stt(out=x, in0=src, scalar=tanh_gates[:, n - 3:n - 2], in1=x,
                                   op0=ALU.mult, op1=ALU.add)
                    last.then_inc(L.added.sem, 1)
                    dve.wait_ge(*L.added.at(it, n + 1))

                def hidden(L):
                    for m in range(IC):
                        dve.wait_ge(*L.silu_ready.at(it, m + 1))
                        s = L.probs[:, (m % 2) * 512:(m % 2) * 512 + S]
                        h = L.probs[:, (m % 2) * 512 + S:(m % 2) * 512 + 2 * S]
                        step.done(tt(h, L.half(m % 4, 1), s, ALU.mult))
                        step.done(tt(L.chunk(L.big, m), h, L.is_v[:], ALU.mult))
                        tt(L.chunk(L.big2, m), h, L.chunk(L.big, m), ALU.subtract).then_inc(L.hidden.sem, 1)

                def centre(L, n):
                    dve.wait_ge(*L.sum_done.at(it, n + 1))
                    for c in range(DC):
                        last = stt(out=L.chunk(L.xl, c), in0=L.half(3, 0), scalar=-1.0 / D, in1=L.chunk(L.x, c),
                                   op0=ALU.mult, op1=ALU.add)
                    step.done(last)
                    square(L, L.xl)

                def each(stage, *args):
                    for L in lanes:
                        stage(L, *args)

                def gated_memory(g):
                    each(gm_max, g)
                    each(gm_normalise, g)
                    each(gm_turned_save, g)
                    for L in lanes:
                        gm_fuse(L, g)
                        square(L, L.xl)

                each(masks)
                gated_memory(0)
                for L in lanes:
                    if L.t == 0:
                        dve.wait_ge(trig_ready.sem, 1)
                    normalise(L, 0, L.xl, L.x, "L0_xattn_norm_w")
                    square(L, L.x)
                for L in lanes:
                    normalise(L, 1, L.x, L.xn, "L1_xattn_ln_in_w")
                    split(L, L.xn[:])
                for L in lanes:
                    self_values(L)
                    rotate(L)
                    keys(L, SELF)
                each(maxima, SELF)
                each(head_outputs, SELF)
                each(split_context)
                for L in lanes:
                    add(L, 0)
                    square(L, L.x)
                for L in lanes:
                    normalise(L, 2, L.x, L.xn, "L1_xattn_ln_post_cross_w")
                for L in lanes:
                    cross_values(L)
                    keys(L, CROSS)
                each(maxima, CROSS)
                each(head_outputs, CROSS)
                for L in lanes:
                    add(L, 1)
                    square(L, L.x)
                for L in lanes:
                    normalise(L, 3, L.x, L.xn, "L1_xattn_ln_post_attn_w")
                    split(L, L.xn[:])
                each(hidden)
                each(add, 2)
                each(keys, LATENT)
                each(centre, 0)
                for L in lanes:
                    normalise(L, 4, L.xl, L.xn, "L2_xattn_ln_q_g", "L2_xattn_ln_q_b")
                each(maxima, LATENT)
                each(head_outputs, LATENT)
                each(add, 3)
                each(centre, 1)
                for L in lanes:
                    normalise(L, 5, L.xl, L.xn, "L2_xattn_ln_ff_g", "L2_xattn_ln_ff_b")
                each(add, 4)
                gated_memory(1)
                for L in lanes:
                    normalise(L, 6, L.xl, L.xn, "L3_xattn_norm_w")
                assert step.n == vec_step.per_pass, step.n


def tables():
    f = np.float32
    dim = HEAD_DIM[SELF]
    inv = (f(1.0) / np.power(f(10000.0), np.arange(0, dim, 2, dtype=f) / f(dim))).astype(f)
    freqs = np.outer(np.arange(S, dtype=f), inv).astype(f)
    emb = np.concatenate([freqs, freqs], axis=-1)
    rows = np.arange(P)
    const = np.zeros((P, K_END), f)
    const[:, K_IDENT:K_IDENT + P] = np.eye(P)
    const[:, K_ONES:K_ONES + P] = 1.0
    for r in range(P):
        j = r % dim
        const[r + dim // 2 if j < dim // 2 else r - dim // 2, K_ROT + r] = -1.0 if j < dim // 2 else 1.0
    trig = np.zeros((P, T_END), f)
    for at, table in ((T_COS, np.cos(emb)), (T_SIN, np.sin(emb))):
        spread = table[:, rows % dim]
        for c in range(ST):
            trig[:, at + c * P:at + (c + 1) * P] = spread[c * P:(c + 1) * P]
    const[rows, K_HEAD16 + rows // 16] = 1.0
    const[rows, K_HEAD8 + rows // 8] = 1.0
    const[rows, K_HALF + rows // 64] = 1.0
    const[:, K_IOTA] = rows
    const[:, K_EPS] = 1e-6
    const[:, K_EPS + 1] = 1e-5
    b = np.zeros((P, KB_END), f)
    b[:, KB_IDENT:KB_IDENT + P] = np.eye(P)
    b[:, KB_CAUSAL + P:KB_CAUSAL + S] = np.where(rows[None, :] > rows[:, None], -BIG, 0.0)
    b[:, KB_CAUSAL_T:KB_CAUSAL_T + P] = np.where(rows[:, None] > rows[None, :], -BIG, 0.0)
    for h in range(HEADS):
        b[h, KB_SEL + h * P:KB_SEL + (h + 1) * P] = -1.0
        b[16 + h, KB_SEL + h * P:KB_SEL + (h + 1) * P] = -1.0
    b[0, KB_ONEROW:KB_ONEROW + P] = 1.0
    return const, (b.view(np.uint32) >> 16).astype(np.uint16), trig


def kernel(**inputs):
    import concourse.bacc as _bacc
    from concourse.bass_utils import run_bass_kernel_spmd as _run

    a = {k: np.asarray(v) for k, v in inputs.items()}

    def chunks(m):
        k = m.shape[0] // P
        return m.reshape(k, P, m.shape[1]).transpose(1, 0, 2).reshape(P, k * m.shape[1])

    def padded(m, rows, cols):
        out = np.zeros((rows, cols), m.dtype)
        out[:m.shape[0], :m.shape[1]] = m
        return out

    def pack(*parts):
        return np.ascontiguousarray(np.concatenate(parts, axis=1))

    one = "L1_xattn_"
    two = "L2_xattn_"
    const, constb, trig = tables()
    arrays = {
        "x": np.ascontiguousarray(a["x"].transpose(0, 2, 1).reshape(B, DC, P, S)
                                  .transpose(0, 2, 1, 3).reshape(B, P, DC * S)),
        "ctx": np.ascontiguousarray(a["ctx_1024"].transpose(0, 2, 1)),
        "pos": np.ascontiguousarray(a["pos_1xS"]),
        "expert": np.ascontiguousarray(a["mask_BxS_ik0"]),
        "keep_row": np.ascontiguousarray(a["mask_BxS2_bk0"]).view(np.uint32),
        "keep_col": np.ascontiguousarray(
            a["mask_BxS2_bk0"].reshape(B, ST, P).transpose(0, 2, 1)).reshape(B, S).view(np.uint32),
        "gm": np.stack([pack(a[f"L{n}_xattn_W_mem"].T, chunks(a[f"L{n}_xattn_W_gate"].T)) for n in (0, 3)]),
        "l1a": pack(chunks(a[one + "v_qkv"]), chunks(a[one + "l_qkv"]), chunks(a[one + "v_dense"]),
                    chunks(a[one + "l_dense"]), chunks(a[one + "cq_w"]), a[one + "ckv_w"],
                    a[one + "cdense_w"]),
        "l1m": pack(*[chunks(padded(a[one + n], D, I_PAD)) for n in ("v_gate", "l_gate", "v_up", "l_up")],
                    *[chunks(padded(a[one + n], I_PAD, D)) for n in ("v_down", "l_down")]),
        "l2q": pack(chunks(a[two + "Wq"]), a[two + "Wkv"]),
        "l2f": pack(chunks(a[two + "Wo"]), chunks(a[two + "W1"]), chunks(a[two + "W2"])),
        "vec": pack(*[a[n].reshape(DC, P).T for n in VECTORS],
                    *[np.broadcast_to(a[two + n].reshape(1, 1), (P, 1)) for n in ("attn_gate", "ff_gate")]),
        "const": const,
        "constb": constb,
        "trig": trig,
    }
    nc = _bacc.Bacc("TRN2", target_bir_lowering=False, num_devices=1)
    args = [nc.dram_tensor(f"in_{n}", v.shape, mybir.dt.from_np(v.dtype), kind="ExternalInput").ap()
            for n, v in arrays.items()]
    args.append(nc.dram_tensor("out_0", (B, P, DC * S), F32, kind="ExternalOutput").ap())
    build(nc, *args)
    r = _run(nc, [{f"in_{n}": v for n, v in arrays.items()}], core_ids=[0])
    got = r.results[0]["out_0"]
    return got.reshape(B, P, DC, S).transpose(0, 3, 2, 1).reshape(B, S, D)
```

```python
from contextlib import ExitStack

import numpy as np

import concourse.bass as bass
from concourse import mybir

F32 = mybir.dt.float32
F32R = mybir.dt.float32r
BF16 = mybir.dt.bfloat16
I32 = mybir.dt.int32
U8 = mybir.dt.uint8
ALU = mybir.AluOpType
ACT = mybir.ActivationFunctionType
AX = mybir.AxisListType

P = 128
BATCH, S, D = 4, 256, 256
C = 128
LANES = 2
PAIRS = BATCH // LANES
DC = D // P
ST = S // P
HEADS = 16
I_PAD = 768
IC = I_PAD // P
INNER = 1024
NC2 = INNER // P
BIG = 2.0 ** 100

SELF, CROSS, LATENT = range(3)
BLOCKS = [(SELF, 0, 16), (CROSS, 0, 16), (LATENT, 0, 8), (LATENT, 8, 8)]
HEAD_DIM = [16, 8, 64]
SCALE = [16 ** -0.5, 8 ** -0.5, 64 ** -0.5]
GROUP = [4, 8, 1]
SHARE = [2, 4]
V_PAD = 56
VROW = V_PAD + HEADS * P


def columns(*sizes):
    at = [0]
    for s in sizes:
        at.append(at[-1] + s)
    return at


GM_MEM, GM_GATE, GM_END = columns(D, 2 * DC * D)
(A_VQKV, A_LQKV, A_VDENSE, A_LDENSE, A_CQ, A_CKV, A_CDENSE, A_END) = columns(
    DC * 3 * D, DC * 3 * D, DC * D, DC * D, DC * P, 2 * P, D)
(M_VGATE, M_LGATE, M_VUP, M_LUP, M_END) = columns(*[DC * I_PAD] * 4)
(M_VDOWN, M_LDOWN, M_DOWN_END) = columns(IC * D, IC * D)
(Q_WQ, Q_WKV, Q_END) = columns(DC * INNER, 2 * INNER)
(F_WO, F_W1, F_W2, F_END) = columns(NC2 * D, DC * INNER, NC2 * D)
VECTORS = ["L0_xattn_b_gate", "L0_xattn_norm_w", "L1_xattn_ln_in_w", "L1_xattn_ln_post_cross_w",
           "L1_xattn_ln_post_attn_w", "L2_xattn_ln_q_g", "L2_xattn_ln_q_b", "L2_xattn_ln_ff_g",
           "L2_xattn_ln_ff_b", "L3_xattn_b_gate", "L3_xattn_norm_w"]
VEC = {n: DC * i for i, n in enumerate(VECTORS)}
VEC_GATES = DC * len(VECTORS)
VEC_END = VEC_GATES + 2
(K_IDENT, K_ONES, K_ROT, K_OWN16, K_OWN8, K_SEL, K_HALF, K_IOTA, K_EPS, K_END) = columns(
    P, P, P, 2, 4, HEADS, 2, 1, 2)
PLACE_BLOCKS = "110010100"
PLACE_COLS = 32 * len(PLACE_BLOCKS)
Q_HI, Q_LO, K_HI, K_LO = (PLACE_BLOCKS.index(x) for x in ("1010", "0100", "1100", "0010"))
(T_COS, T_SIN, T_PLACE, T_END) = columns(ST * P, ST * P, 4 * PLACE_COLS)
(KB_IDENT, KB_CAUSAL, KB_CAUSAL_T, KB_SEL, KB_ONEROW, KB_END) = columns(P, P, P, 8, P)


class Signal:

    def __init__(self, sem, per_pass):
        self.sem, self.per_pass = sem, per_pass

    def at(self, it, k):
        return self.sem, it * self.per_pass + k


class Steps:

    def __init__(self, engine, raised, it):
        self.engine, self.raised, self.it, self.n = engine, raised, it, 0

    def done(self, instruction):
        self.n += 1
        instruction.then_inc(self.raised.sem, 1)
        self.engine.wait_ge(*self.raised.at(self.it, self.n))


def alternate(first, second):
    for _ in first:
        next(second, None)
    for _ in second:
        pass


PLAN = {
    ("self", 0): {"rotate": 0, "split": 2, "stack": 3, "max": 6, "heads": 3, "turn": 12, "end": 13},
    ("self", 1): {"rotate": 0, "split": 3, "stack": 4, "max": 7, "heads": 2, "turn": 15, "end": 16},
    ("cross", 0): {"dense": 0, "norm": 2, "project": 4, "stack": 6, "max": 8, "heads": 3, "turn": 15, "end": 16},
    ("cross", 1): {"dense": 0, "norm": 2, "project": 4, "stack": 6, "max": 8, "heads": 3, "turn": 15, "end": 16},
    ("latent", 0): {"values": 0, "mean": 2, "norm": 4, "project": 6, "max": 10, "heads": 1, "turn": 19, "end": 20},
    ("latent", 1): {"values": 0, "mean": 1, "norm": 2, "project": 3, "max": 5, "heads": 3, "turn": 8, "end": 9},
    ("half", 0): {"project": 0, "max": 3, "heads": 2, "turn": 8, "end": 9},
    ("half", 1): {"project": 0, "max": 3, "heads": 2, "turn": 8, "end": 9},
    ("experts", 0): {"dense": 0, "norm": 2, "split": 3, "end": 4},
    ("experts", 1): {"dense": 0, "norm": 2, "split": 3, "end": 4},
    ("ffn", 0): {"dense": 0, "mean": 2, "norm": 3, "end": 4},
    ("ffn", 1): {"dense": 0, "mean": 2, "norm": 3, "end": 4},
}


def heads_at(plan, step, heads):
    n = plan["heads"]
    return range(n * (step - plan["max"]), min(heads, n * (step - plan["max"] + 1))) if step >= plan["max"] else []


def alone(stage):
    for _ in stage:
        pass


def build(nc, x_d, ctx_d, pos_d, expert_d, keep_row_d, keep_col_d, gm_d, l1a_d, l1m_d, l1d_d, l2q_d, l2f_d,
          vec_d, const_d, constb_d, trig_d, out_d):
    with ExitStack() as stack:
        def sb(name, cols, dt=F32):
            return stack.enter_context(nc.sbuf_tensor(name, [P, cols], dt))

        def signal(name, per_pass=1):
            return Signal(stack.enter_context(nc.semaphore(name)), per_pass)

        gm_w = sb("gm_w", GM_END)
        attn_w = sb("attn_w", A_END)
        ffn_w = sb("ffn_w", M_END)
        vec = sb("vec", VEC_END)
        const = sb("const", K_END)
        constb = sb("constb", KB_END, BF16)
        place = sb("place", 4 * PLACE_COLS, F32R)
        cos = sb("cos", S)
        sin = sb("sin", S)
        tanh_gates = sb("tanh_gates", 2)

        weights_in = {n: signal(f"weights_in_{n}") for n in ("gm", "l1a", "l1m", "l1d", "l2q", "l2f")}
        const_in = signal("const_in")
        onehot_ready = signal("onehot_ready")
        trig_done = signal("trig_done")
        trig_ready = signal("trig_ready")
        tanh_ready = signal("tanh_ready")
        pool_waits = signal("pool_waits")
        vec_step = signal("vec_step", 66)
        act_step = signal("act_step", 58)

        class Lane:
            def __init__(self, t):
                self.t = t

                def s(name, per_pass=1):
                    return signal(f"{name}_{'AB'[t]}", per_pass)

                def m(name, cols, dt=F32):
                    return sb(f"{name}_{'AB'[t]}", cols, dt)

                self.ps = stack.enter_context(nc.psum_tensor(f"ps_{'AB'[t]}", [P, 4, 512], F32))
                self.x = m("x", DC * S)
                self.ctx = m("ctx", S)
                self.kz = m("kz", HEADS * S, F32R)
                self.parts = self.kz[:, 8 * S:16 * S]
                self.q = m("q", NC2 * S, F32R)
                self.v = m("v", ST * VROW)
                self.xin = self.v[:, 0:DC * S]
                self.expert_i = self.v[:, DC * S:DC * S + S].bitcast(I32)
                self.big = m("big", NC2 * S)
                self.big2 = m("big2", NC2 * S)
                self.probs = m("probs", 2 * 512)
                self.xn = m("xn", DC * S)
                self.xv = m("xv", DC * S)
                self.xl = m("xl", DC * S)
                self.sq = self.probs[:, 0:DC * S]
                self.rstd = m("rstd", S)
                self.recip = m("recip", 2 * S)
                self.is_v = m("is_v", S)
                self.keep_col = m("keep_col", ST, U8)
                self.keep_row = m("keep_row", S, U8)
                self.key_bias = m("key_bias", ST)
                self.mask_row = m("mask_row", S, BF16)
                self.max = m("max", ST * HEADS)
                self.max_parts = m("max_parts", ST * 32, BF16)
                self.max_rows = m("max_rows", S, BF16)
                self.stat = m("stat", 8)

                self.inputs_in = s("inputs_in")
                self.out_in_dram = s("out_in_dram", 16)
                self.v_cleared = s("v_cleared", 2)
                self.rows_cleared = s("rows_cleared")
                self.v_resized = s("v_resized", 2)
                self.masks_ready = s("masks_ready")
                self.mem_done = s("mem_done", 4)
                self.mem_saved = s("mem_saved", 4)
                self.gm_scores = s("gm_scores", 2)
                self.gm_max = s("gm_max", 2)
                self.gm_exp = s("gm_exp", 4)
                self.gm_probs = s("gm_probs", 2)
                self.gm_turned = s("gm_turned", 2)
                self.gm_turned_saved = s("gm_turned_saved", 2)
                self.gm_context = s("gm_context", 2)
                self.gm_context_saved = s("gm_context_saved", 2)
                self.gate_done = s("gate_done", 2)
                self.gate_saved = s("gate_saved", 4)
                self.sum_done = s("sum_done", 2)
                self.sq_ready = s("sq_ready", 7)
                self.sumsq_done = s("sumsq_done", 7)
                self.rstd_ready = s("rstd_ready", 7)
                self.normed = s("normed", 7)
                self.split = s("split", 3)
                self.hi_ready = s("hi_ready", 2)
                self.lo_ready = s("lo_ready", 2)
                self.q_stacked = s("q_stacked", 6)
                self.q_ready = s("q_ready", 6)
                self.k_stacked = s("k_stacked", 6)
                self.q2_lo = s("q2_lo", 4)
                self.qk_done = s("qk_done", 2)
                self.qk_saved = s("qk_saved", 2)
                self.rot_done = s("rot_done")
                self.rotated = s("rotated")
                self.cross_done = s("cross_done")
                self.v_done = s("v_done", 6)
                self.v_saved = s("v_saved", 6)
                self.k_done = s("k_done", 4)
                self.q2_done = s("q2_done", 4)
                self.q2_saved = s("q2_saved", 4)
                self.k_saved = s("k_saved", 10)
                self.k2_lo = s("k2_lo", 4)
                self.key_ready = s("key_ready", 48)
                self.scores = s("scores", 48)
                self.max_ready = s("max_ready", 48)
                self.max_split = s("max_split", 4)
                self.max_turned = s("max_turned", 4)
                self.max_saved = s("max_saved", 4)
                self.scores_t = s("scores_t", 48)
                self.probs_ready = s("probs_ready", 48)
                self.pv_done = s("pv_done", 48)
                self.recip_ready = s("recip_ready", 22)
                self.head_out = s("head_out", 22)
                self.added_done = s("added_done", 5)
                self.added = s("added", 5)
                self.up_done = s("up_done", 6)
                self.silu_ready = s("silu_ready", 6)
                self.hidden = s("hidden", 6)
                self.w1_done = s("w1_done", 4)
                self.gelu_ready = s("gelu_ready", 4)

            def chunk(self, tile, c, lo=0, hi=S):
                return tile[:, c * S + lo:c * S + hi]

            def half(self, bank, h, lo=0, hi=S):
                return self.ps[:, bank, h * S + lo:h * S + hi]

            def values(self, a, h, kt):
                at = kt * VROW + V_PAD + h * P - HEAD_DIM[a] * (h % GROUP[a])
                return self.v[:, at:at + P]

            def slots(self, kt, lo, width):
                at = kt * VROW + V_PAD
                return self.v[:, at:at + HEADS * P].rearrange("p (h c) -> p h c", c=P)[:, :, lo:lo + width]

        lanes = A, B = [Lane(t) for t in range(LANES)]
        pos_i = lanes[0].xv[:, 0:S].bitcast(I32)
        down_w = lanes[1].v

        def w(tile, at, chunk, lo, hi, width):
            return tile[:, at + chunk * width + lo:at + chunk * width + hi]

        def stack_place(start, j):
            at = j * PLACE_COLS + 32 * start
            return place[:, at:at + P]

        ident = const[:, K_IDENT:K_IDENT + P]
        ones = const[:, K_ONES:K_ONES + P]
        rot = const[:, K_ROT:K_ROT + P]
        identb = constb[:, KB_IDENT:KB_IDENT + P]
        onerow = constb[:, KB_ONEROW:KB_ONEROW + P]

        def sel(h):
            return constb[:, KB_SEL + h:KB_SEL + h + 1].to_broadcast([P, P])

        GROUP_BASE = [0, 4, 6]

        block = stack.enter_context(nc.Block())

        @block.sync
        def _(sp):
            for L in lanes:
                sp.sem_inc(L.out_in_dram.sem, 16)
            sp.dma_start(const[:], const_d).then_inc(const_in.sem, 16)
            sp.dma_start(constb[:], constb_d.bitcast(BF16)).then_inc(const_in.sem, 16)
            sp.dma_start(lanes[1].big[:, 0:T_END], trig_d).then_inc(const_in.sem, 16)
            sp.dma_start(vec[:], vec_d).then_inc(const_in.sem, 16)
            sp.dma_start(pos_i[:], pos_d.rearrange("a s -> (a s)").partition_broadcast(P))\
                .then_inc(const_in.sem, 16)
            sp.dma_start(gm_w[:], gm_d[0]).then_inc(weights_in["gm"].sem, 16)
            with sp.Fori(0, PAIRS) as it:
                for L in lanes:
                    n = it * LANES + L.t
                    sp.dma_start(L.ctx[:], ctx_d[bass.ds(n, 1)].rearrange("a p n -> (a p) n"))\
                        .then_inc(L.inputs_in.sem, 16)
                    sp.dma_start(L.xin[:], x_d[bass.ds(n, 1)].rearrange("a p n -> (a p) n"))\
                        .then_inc(L.inputs_in.sem, 16)
                    sp.dma_start(L.expert_i[:],
                                 expert_d[bass.ds(n, 1)].rearrange("a s -> (a s)").partition_broadcast(P))\
                        .then_inc(L.inputs_in.sem, 16)
                    sp.dma_start(L.keep_col[:], keep_col_d[bass.ds(n, 1)].bitcast(U8).rearrange("a (p n) -> (a p) n", p=P))\
                        .then_inc(L.inputs_in.sem, 16)
                    sp.dma_start(L.keep_row[0:1, :], keep_row_d[bass.ds(n, 1)].bitcast(U8)).then_inc(L.inputs_in.sem, 16)
                sp.dma_start(attn_w[:], l1a_d).then_inc(weights_in["l1a"].sem, 16)
                sp.dma_start(ffn_w[:], l1m_d).then_inc(weights_in["l1m"].sem, 16)
                for L in lanes:
                    sp.wait_ge(*L.gate_done.at(it, 1))
                sp.dma_start(gm_w[:], gm_d[1]).then_inc(weights_in["gm"].sem, 16)
                sp.wait_ge(*lanes[1].pv_done.at(it, 2 * HEADS))
                sp.dma_start(down_w[:, 0:M_DOWN_END], l1d_d).then_inc(weights_in["l1d"].sem, 16)
                for L in lanes:
                    sp.wait_ge(*L.added_done.at(it, 2))
                sp.dma_start(attn_w[:, 0:Q_END], l2q_d).then_inc(weights_in["l2q"].sem, 16)
                for L in lanes:
                    sp.wait_ge(*L.up_done.at(it, IC))
                sp.dma_start(ffn_w[:, 0:F_END], l2f_d).then_inc(weights_in["l2f"].sem, 16)
                for L in lanes:
                    sp.wait_ge(*L.gate_done.at(it, 2))
                sp.dma_start(gm_w[:], gm_d[0]).then_inc(weights_in["gm"].sem, 16)
            sp.wait_ge(weights_in["gm"].sem, 16 + PAIRS * 32)
            for L in lanes:
                sp.wait_ge(L.out_in_dram.sem, 16 + PAIRS * 16)

        @block.gpsimd
        def _(pool):
            def wait(sem, value):
                pool.wait_ge(sem, value)
                pool.sem_inc(pool_waits.sem, 1)

            with pool.Fori(0, PAIRS) as it:
                for L in lanes:
                    wait(L.out_in_dram.sem, it * 16 + 16)
                    nc.gpsimd.memset(L.max_rows[:], 0.0)
                    nc.gpsimd.memset(L.mask_row[:], 0.0).then_inc(L.rows_cleared.sem, 1)
                for L in lanes:
                    wait(*L.sq_ready.at(it, 1))
                    nc.gpsimd.memset(L.v[:], 0.0).then_inc(L.v_cleared.sem, 1)
                    wait(*L.v_cleared.at(it, 1))
                    for kt in range(ST):
                        last = nc.gpsimd.memset(L.slots(kt, 64, HEAD_DIM[SELF]), 1.0)
                    last.then_inc(L.v_cleared.sem, 1)
                def resize_for_cross(L):
                    wait(*L.pv_done.at(it, HEADS))
                    for kt in range(ST):
                        nc.gpsimd.memset(L.slots(kt, 8, 8), 0.0)
                        last = nc.gpsimd.memset(L.slots(kt, 72, 8), 0.0)
                    last.then_inc(L.v_resized.sem, 1)

                def resize_for_latent(L):
                    wait(*L.pv_done.at(it, 2 * HEADS))
                    if L.t == 1:
                        for M in lanes:
                            wait(*M.added_done.at(it, 3))
                    for kt in range(ST):
                        last = nc.gpsimd.memset(L.slots(kt, 64, HEAD_DIM[LATENT]), 1.0)
                    last.then_inc(L.v_resized.sem, 1)

                def stacked_keys(L, a):
                    n = 0 if a == SELF else 4
                    own = K_OWN16 if a == SELF else K_OWN8
                    for h in range(HEADS):
                        t = h // SHARE[a]
                        if h % (2 * SHARE[a]) == 0:
                            wait(*L.k_saved.at(it, n + t // 2 + 1))
                        if h == 8 and a == SELF:
                            wait(*L.k_stacked.at(it, 4))
                        mask, maxima = own + h % SHARE[a], K_SEL + h
                        nc.gpsimd.tensor_scalar(L.chunk(L.kz, h), L.chunk(L.big, t), const[:, mask:mask + 1],
                                                const[:, maxima:maxima + 1], ALU.mult, ALU.add)\
                            .then_inc(L.key_ready.sem, 1)

                def latent_keys(L, half):
                    wait(*L.scores_t.at(it, 2 * HEADS + 8 * half))
                    for h in range(8):
                        if h % 4 == 0:
                            wait(*L.k2_lo.at(it, 2 * half + h // 4 + 1))
                        mask = const[:, K_HALF + h % 2:K_HALF + h % 2 + 1]
                        for part in range(2):
                            last = nc.gpsimd.tensor_scalar(L.chunk(L.kz, 8 * part + h),
                                                           L.chunk(L.big, 4 * part + h // 2), mask, None, ALU.mult)
                        last.then_inc(L.key_ready.sem, 1)

                stacked_keys(A, SELF)
                stacked_keys(B, SELF)
                for L in lanes:
                    resize_for_cross(L)
                    stacked_keys(L, CROSS)
                resize_for_latent(A)
                latent_keys(A, 0)
                resize_for_latent(B)
                latent_keys(B, 0)
                latent_keys(A, 1)
                latent_keys(B, 1)

        @block.tensor
        def _(pe):
            mm = nc.tensor.matmul

            pe.wait_ge(const_in.sem, 80)
            pe.wait_ge(onehot_ready.sem, 1)
            for half, table in enumerate((T_COS, T_SIN)):
                for c in range(ST):
                    last = mm(lanes[0].half(0, half), lanes[1].big[:, table + c * P:table + (c + 1) * P],
                              lanes[0].chunk(lanes[0].big, c), start=(c == 0), stop=(c == ST - 1))
            last.then_inc(trig_done.sem, 1)

            with pe.Fori(0, PAIRS) as it:
                pe.wait_ge(trig_ready.sem, 1)

                def memory_projection(L, g):
                    if L.t == 0:
                        pe.wait_ge(weights_in["gm"].sem, it * 32 + 16 * (g + 1))
                    if g == 0:
                        pe.wait_ge(L.inputs_in.sem, it * 80 + 80)
                    else:
                        pe.wait_ge(*L.added.at(it, 5))
                    for c in range(DC):
                        last = mm(L.half(0, c), gm_w[:, GM_MEM + c * P:GM_MEM + (c + 1) * P], L.ctx[:, 0:S],
                                  start=True, stop=True)
                    last.then_inc(L.mem_done.sem, 1)
                    for kt in range(ST):
                        last = mm(L.half(1, kt), L.ctx[:, kt * P:(kt + 1) * P], gm_w[:, GM_MEM:GM_MEM + D],
                                  start=True, stop=True)
                    last.then_inc(L.mem_done.sem, 1)

                def gm_scores(L, g):
                    x = L.xin if g == 0 else L.x
                    pe.wait_ge(*L.mem_saved.at(it, 2 * g + 1))
                    for qt in range(ST):
                        for c in range(DC):
                            last = mm(L.half(2, qt), L.chunk(x, c, qt * P, (qt + 1) * P),
                                      L.chunk(L.big2, c), start=(c == 0), stop=(c == DC - 1))
                    last.then_inc(L.gm_scores.sem, 1)

                def gm_turn(L, g):
                    pe.wait_ge(*L.gm_probs.at(it, g + 1))
                    for kt in range(ST):
                        for qt in range(ST):
                            last = nc.tensor.transpose(L.half(3, kt, qt * P, (qt + 1) * P),
                                                       L.chunk(L.big, qt, kt * P, (kt + 1) * P), ident)
                    last.then_inc(L.gm_turned.sem, 1)

                def gm_context(L, g):
                    pe.wait_ge(*L.mem_saved.at(it, 2 * g + 2))
                    pe.wait_ge(*L.gm_turned_saved.at(it, g + 1))
                    for c in range(DC):
                        for kt in range(ST):
                            last = mm(L.half(0, c), L.chunk(L.big2, 2 + kt, c * P, (c + 1) * P),
                                      L.chunk(L.big, 2 + kt), start=(kt == 0), stop=(kt == ST - 1))
                    last.then_inc(L.gm_context.sem, 1)

                def gm_gate(L, g):
                    x = L.xin if g == 0 else L.x
                    pe.wait_ge(*L.gm_context_saved.at(it, g + 1))
                    for c in range(DC):
                        for f in range(2 * DC):
                            src = L.chunk(x, f) if f < DC else L.chunk(L.xv, f - DC)
                            last = mm(L.half(1, c), w(gm_w, GM_GATE, f, c * P, (c + 1) * P, D), src,
                                      start=(f == 0), stop=(f == 2 * DC - 1))
                    last.then_inc(L.gate_done.sem, 1)

                def sum_squares(L, n):
                    pe.wait_ge(*L.sq_ready.at(it, n + 1))
                    for c in range(DC):
                        last = mm(L.half(2, 0), ones, L.chunk(L.sq, c), start=(c == 0), stop=(c == DC - 1))
                    last.then_inc(L.sumsq_done.sem, 1)

                def layer_norm_sum(L, n):
                    pe.wait_ge(*L.added.at(it, 3 + n))
                    pe.wait_ge(*L.v_saved.at(it, 6))
                    for c in range(DC):
                        last = mm(L.half(3, 0), ones, L.chunk(L.x, c), start=(c == 0), stop=(c == DC - 1))
                    last.then_inc(L.sum_done.sem, 1)

                def self_qkv(L):
                    if L.t == 0:
                        pe.wait_ge(weights_in["l1a"].sem, it * 16 + 16)
                    pe.wait_ge(*L.split.at(it, 1))
                    parts = [(A_VQKV, L.xv, c) for c in range(DC)] + [(A_LQKV, L.xl, c) for c in range(DC)]
                    for m in range(4):
                        for i, (at, src, c) in enumerate(parts):
                            last = mm(L.half(m // 2, m % 2), w(attn_w, at, c, m * P, (m + 1) * P, 3 * D),
                                      L.chunk(src, c), start=(i == 0), stop=(i == 3))
                        if m % 2:
                            last.then_inc(L.qk_done.sem, 1)
                        yield
                    for kt in range(ST):
                        for i, (at, src, c) in enumerate(parts):
                            last = mm(L.half(3, kt), L.chunk(src, c, kt * P, (kt + 1) * P),
                                      w(attn_w, at, c, 2 * D, 3 * D, 3 * D), start=(i == 0), stop=(i == 3))
                        if kt == ST - 1:
                            last.then_inc(L.v_done.sem, 1)
                        yield

                def rotate_halves(L):
                    pe.wait_ge(*L.qk_saved.at(it, 2))
                    for m in range(4):
                        last = mm(L.half(m // 2, m % 2), rot, L.chunk(L.big, m), start=True, stop=True)
                    last.then_inc(L.rot_done.sem, 1)

                def stack_queries_and_keys(L, a):
                    n = 1 + (a == CROSS)
                    tiles = HEADS // SHARE[a]
                    pe.wait_ge(*L.hi_ready.at(it, n))
                    pe.wait_ge(*L.lo_ready.at(it, n))
                    if a == SELF:
                        pe.wait_ge(*L.v_saved.at(it, 1))
                    chunks = tiles // 4
                    for what, (hi, lo) in enumerate(((Q_HI, Q_LO), (K_HI, K_LO))):
                        for t in range(tiles):
                            bank = t // 2 if a == SELF else t // 2 + 2 * (1 - what)
                            c, j = what * chunks + t // 4, t % 4
                            if a == CROSS and what == 1 and t == 0:
                                pe.wait_ge(*L.v_saved.at(it, 2))
                            if a == SELF and what == 1 and t % 2 == 0:
                                pe.wait_ge(*L.q_ready.at(it, bank + 1))
                            mm(L.half(bank, t % 2), stack_place(hi, j), L.chunk(L.parts, c),
                               start=True, stop=False)
                            last = mm(L.half(bank, t % 2), stack_place(lo, j),
                                      L.chunk(L.parts, 2 * chunks + c), start=False, stop=True)
                            if t % 2:
                                last.then_inc((L.k_stacked if what else L.q_stacked).sem, 1)

                def query(L, a, h):
                    tile = h % 8 // 2 if a == LATENT else h // SHARE[a]
                    return lambda lo, hi, part=0: L.chunk(L.q, 4 * part + tile, lo, hi)

                def scores_for_max(L, block, h):
                    a, h0, heads = BLOCKS[block]
                    n0 = a * HEADS + h0
                    if h == 0:
                        if a < LATENT:
                            pe.wait_ge(*L.k_saved.at(it, [4, 6][a]))
                        if a == LATENT:
                            pe.wait_ge(*L.q2_lo.at(it, 2 * block - 2))
                            pe.wait_ge(*L.masks_ready.at(it, 1))
                        else:
                            pe.wait_ge(*L.q_ready.at(it, 4 + 2 * (a == CROSS)))
                    pe.wait_ge(*L.key_ready.at(it, n0 + h + 1))
                    if h >= 4:
                        pe.wait_ge(*L.max_ready.at(it, n0 + h - 3))
                    bank, q = h % 4, query(L, a, h)
                    for qt in range(ST):
                        keys = L.chunk(L.kz, h)
                        last = mm(L.half(bank, qt), q(qt * P, (qt + 1) * P), keys,
                                  start=True, stop=(a == CROSS))
                        if a == SELF:
                            last = mm(L.half(bank, qt, qt * P, (qt + 1) * P), identb,
                                      constb[:, KB_CAUSAL:KB_CAUSAL + P], start=False, stop=True)
                        elif a == LATENT:
                            last = mm(L.half(bank, qt), onerow, L.mask_row[:], start=False, stop=True)
                    last.then_inc(L.scores.sem, 1)

                def turn_max(L, block):
                    a, h0, heads = BLOCKS[block]
                    pe.wait_ge(*L.max_split.at(it, block + 1))
                    pe.wait_ge(*L.max_ready.at(it, a * HEADS + h0 + heads))
                    turned = L.ps[0:32, 3, 0:P].bitcast(BF16)
                    for qt in range(ST):
                        last = nc.tensor.transpose(turned[:, qt * P:(qt + 1) * P],
                                                   L.max_parts[:, qt * 32:(qt + 1) * 32], identb)
                    last.then_inc(L.max_turned.sem, 1)

                def attend(L, block):
                    a, h0, heads = BLOCKS[block]
                    n0 = a * HEADS + h0

                    def scores(h):
                        n = n0 + h
                        if h == 0:
                            pe.wait_ge(*L.max_saved.at(it, block + 1))
                        if h >= 2:
                            pe.wait_ge(*L.probs_ready.at(it, n - 1))
                        bank, q = h % 2, query(L, a, h)
                        for kt in (1, 0):
                            out = L.half(bank, 1 - kt)
                            keys = L.chunk(L.kz, h, kt * P, (kt + 1) * P)
                            last = mm(out, keys, q(0, S), start=True, stop=(a == CROSS))
                            if a == SELF:
                                last = mm(L.half(bank, 1 - kt, kt * P, (kt + 1) * P), identb,
                                          constb[:, KB_CAUSAL_T:KB_CAUSAL_T + P], start=False, stop=True)
                            elif a == LATENT:
                                mm(out, keys, q(0, S, 1), start=False, stop=False)
                                mm(out, L.chunk(L.kz, 8 + h, kt * P, (kt + 1) * P), q(0, S),
                                   start=False, stop=False)
                                last = mm(out, sel(h), L.max_rows[:], start=False, stop=True)
                        last.then_inc(L.scores_t.sem, 1)

                    def weigh(h):
                        n = n0 + h
                        g = (h0 + h) // GROUP[a]
                        if h % GROUP[a] == 0 and (g >= 2):
                            pe.wait_ge(*L.head_out.at(it, GROUP_BASE[a] + g - 1))
                        pe.wait_ge(*L.probs_ready.at(it, n + 1))
                        if h == 0:
                            pe.wait_ge(*L.v_saved.at(it, [1, 2, 6][a]))
                            if a > SELF:
                                pe.wait_ge(*L.v_resized.at(it, a))
                        for kt in range(ST):
                            lo = kt * P if a == SELF else 0
                            at = (h % 2) * 512 + (1 - kt) * S
                            last = mm(L.ps[:, 2 + g % 2, lo:S], L.values(a, h0 + h, kt),
                                      L.probs[:, at + lo:at + S],
                                      start=(h % GROUP[a] == 0 and kt == 0),
                                      stop=(h % GROUP[a] == GROUP[a] - 1 and kt == ST - 1))
                        last.then_inc(L.pv_done.sem, 1)

                    for h in range(heads + 1):
                        if h < heads:
                            scores(h)
                        if h >= 1:
                            weigh(h - 1)
                        yield

                def self_dense(L):
                    pe.wait_ge(*L.split.at(it, 2))
                    for m in range(DC):
                        i = 0
                        for at, src in ((A_VDENSE, L.xv), (A_LDENSE, L.xl)):
                            for c in range(DC):
                                last = mm(L.half(0, m), w(attn_w, at, c, m * P, (m + 1) * P, D),
                                          L.chunk(src, c), start=(i == 0), stop=(i == 3))
                                i += 1
                    last.then_inc(L.added_done.sem, 1)

                def cross_qkv(L):
                    pe.wait_ge(*L.normed.at(it, 3))
                    for c in range(DC):
                        mm(L.half(0, 0), w(attn_w, A_CQ, c, 0, P, P), L.chunk(L.xn, c),
                           start=(c == 0), stop=(c == DC - 1))
                    mm(L.half(0, 1), attn_w[:, A_CKV:A_CKV + P], L.ctx[:], start=True, stop=True)\
                        .then_inc(L.cross_done.sem, 1)
                    for kt in range(ST):
                        last = mm(L.ps[:, 1, kt * P:(kt + 1) * P], L.ctx[:, kt * P:(kt + 1) * P],
                                  attn_w[:, A_CKV + P:A_CKV + 2 * P], start=True, stop=True)
                    last.then_inc(L.v_done.sem, 1)

                def cross_dense(L):
                    pe.wait_ge(*L.head_out.at(it, GROUP_BASE[CROSS] + 2))
                    for m in range(DC):
                        last = mm(L.half(0, m), attn_w[:, A_CDENSE + m * P:A_CDENSE + (m + 1) * P],
                                  L.chunk(L.big2, 0), start=True, stop=True)
                    last.then_inc(L.added_done.sem, 1)

                def experts_up(L):
                    if L.t == 0:
                        pe.wait_ge(weights_in["l1m"].sem, it * 16 + 16)
                    pe.wait_ge(*L.split.at(it, 3))
                    for m in range(IC):
                        if m >= 4:
                            pe.wait_ge(*L.hidden.at(it, m - 3))
                        for half, (wv, wl) in enumerate(((M_VGATE, M_LGATE), (M_VUP, M_LUP))):
                            i = 0
                            for at, src in ((wv, L.xv), (wl, L.xl)):
                                for c in range(DC):
                                    last = mm(L.half(m % 4, half), w(ffn_w, at, c, m * P, (m + 1) * P, I_PAD),
                                              L.chunk(src, c), start=(i == 0), stop=(i == 3))
                                    i += 1
                            if half:
                                last.then_inc(L.up_done.sem, 1)
                            yield

                def experts_down(L):
                    if L.t == 0:
                        pe.wait_ge(weights_in["l1d"].sem, it * 16 + 16)
                    for m in range(DC):
                        i = 0
                        for k in range(IC):
                            if m == 0:
                                pe.wait_ge(*L.hidden.at(it, max(k + 1, 4)))
                            for at, src in ((M_VDOWN, L.big), (M_LDOWN, L.big2)):
                                last = mm(L.half(2 + m, 0), w(down_w, at, k, m * P, (m + 1) * P, D),
                                          L.chunk(src, k), start=(i == 0), stop=(i == 2 * IC - 1))
                                i += 1
                            if m == DC - 1 and k == IC - 1:
                                last.then_inc(L.added_done.sem, 1)
                            yield

                def latent_v(L):
                    if L.t == 0:
                        pe.wait_ge(weights_in["l2q"].sem, it * 16 + 16)
                    pe.wait_ge(*L.added.at(it, 3))
                    for j in range(4):
                        kt, n = j // 2, j % 2
                        mm(L.ps[:, j, :], L.ctx[:, kt * P:(kt + 1) * P],
                           attn_w[:, Q_WKV + INNER + n * 512:Q_WKV + INNER + (n + 1) * 512],
                           start=True, stop=True).then_inc(L.v_done.sem, 1)

                def latent_k(L, half):
                    if half == 0:
                        pe.wait_ge(*L.v_saved.at(it, 4))
                    for m in range(4):
                        last = mm(L.half(m // 2, m % 2),
                                  attn_w[:, Q_WKV + (4 * half + m) * P:Q_WKV + (4 * half + m + 1) * P],
                                  L.ctx[:], start=True, stop=True)
                        if m % 2:
                            last.then_inc(L.k_done.sem, 1)

                def latent_q(L, half):
                    if half == 0:
                        pe.wait_ge(*L.normed.at(it, 5))
                    else:
                        pe.wait_ge(*L.head_out.at(it, GROUP_BASE[LATENT] + 8))
                    for m in range(4):
                        for c in range(DC):
                            last = mm(L.half(2 + m // 2, m % 2),
                                      w(attn_w, Q_WQ, c, (4 * half + m) * P, (4 * half + m + 1) * P, INNER),
                                      L.chunk(L.xn, c), start=(c == 0), stop=(c == DC - 1))
                        if m % 2:
                            last.then_inc(L.q2_done.sem, 1)

                def latent_dense(L):
                    if L.t == 0:
                        pe.wait_ge(weights_in["l2f"].sem, it * 16 + 16)
                    pe.wait_ge(*L.head_out.at(it, GROUP_BASE[LATENT] + HEADS))
                    for m in range(DC):
                        for k in range(NC2):
                            last = mm(L.half(0, m), w(ffn_w, F_WO, k, m * P, (m + 1) * P, D),
                                      L.chunk(L.big2, k), start=(k == 0), stop=(k == NC2 - 1))
                    last.then_inc(L.added_done.sem, 1)

                def ffn_up(L):
                    pe.wait_ge(*L.normed.at(it, 6))
                    for m in range(NC2):
                        for c in range(DC):
                            last = mm(L.half(m // 2, m % 2), w(ffn_w, F_W1, c, m * P, (m + 1) * P, INNER),
                                      L.chunk(L.xn, c), start=(c == 0), stop=(c == DC - 1))
                        if m % 2:
                            last.then_inc(L.w1_done.sem, 1)
                            yield

                def ffn_down(L):
                    for m in range(DC):
                        for k in range(NC2):
                            if m == 0 and k % 2 == 0:
                                pe.wait_ge(*L.gelu_ready.at(it, k // 2 + 1))
                            last = mm(L.half(0, m), w(ffn_w, F_W2, k, m * P, (m + 1) * P, D),
                                      L.chunk(L.big, k), start=(k == 0), stop=(k == NC2 - 1))
                            if m == DC - 1 and k == NC2 - 1:
                                last.then_inc(L.added_done.sem, 1)
                            if k % 4 == 3:
                                yield

                def each(stage, *args):
                    for L in lanes:
                        stage(L, *args)

                def gated_memory(g):
                    each(memory_projection, g)
                    each(gm_scores, g)
                    each(gm_turn, g)
                    each(gm_context, g)
                    each(gm_gate, g)

                def to_self(L):
                    plan = PLAN["self", L.t]
                    for step in range(plan["end"]):
                        if step == plan["rotate"]:
                            rotate_halves(L)
                        if step == plan["stack"]:
                            stack_queries_and_keys(L, SELF)
                        for h in heads_at(plan, step, HEADS):
                            scores_for_max(L, 0, h)
                        if step == plan["turn"]:
                            turn_max(L, 0)
                        yield

                def to_cross(L):
                    plan = PLAN["cross", L.t]
                    for step in range(plan["end"]):
                        if step == plan["dense"]:
                            self_dense(L)
                        if step == plan["norm"]:
                            sum_squares(L, 2)
                        if step == plan["project"]:
                            cross_qkv(L)
                        if step == plan["stack"]:
                            stack_queries_and_keys(L, CROSS)
                        for h in heads_at(plan, step, HEADS):
                            scores_for_max(L, 1, h)
                        if step == plan["turn"]:
                            turn_max(L, 1)
                        yield

                def to_experts(L):
                    plan = PLAN["experts", L.t]
                    for step in range(plan["end"]):
                        if step == plan["dense"]:
                            cross_dense(L)
                        if step == plan["norm"]:
                            sum_squares(L, 3)
                        yield

                def to_latent(L, half):
                    plan = PLAN["half" if half else "latent", L.t]
                    for step in range(plan["end"]):
                        if half == 0:
                            if step == plan["values"]:
                                latent_v(L)
                            if step == plan["mean"]:
                                layer_norm_sum(L, 0)
                            if step == plan["norm"]:
                                sum_squares(L, 4)
                        if step == plan["project"]:
                            latent_k(L, half)
                            latent_q(L, half)
                        for h in heads_at(plan, step, 8):
                            scores_for_max(L, 2 + half, h)
                        if step == plan["turn"]:
                            turn_max(L, 2 + half)
                        yield

                def to_ffn(L):
                    plan = PLAN["ffn", L.t]
                    for step in range(plan["end"]):
                        if step == plan["dense"]:
                            latent_dense(L)
                        if step == plan["mean"]:
                            layer_norm_sum(L, 1)
                        if step == plan["norm"]:
                            sum_squares(L, 5)
                        yield

                def experts(L):
                    yield from experts_up(L)
                    yield from experts_down(L)

                def feed_forward(L):
                    yield from ffn_up(L)
                    yield from ffn_down(L)

                def first_norm(L):
                    sum_squares(L, 1)
                    yield

                gated_memory(0)
                each(sum_squares, 0)
                sum_squares(A, 1)
                alternate(self_qkv(A), first_norm(B))
                alternate(self_qkv(B), to_self(A))
                alternate(attend(A, 0), to_self(B))
                alternate(attend(B, 0), to_cross(A))
                alternate(attend(A, 1), to_cross(B))
                alternate(attend(B, 1), to_experts(A))
                alternate(experts(A), to_experts(B))
                alternate(experts(B), to_latent(A, 0))
                alternate(attend(A, 2), to_latent(B, 0))
                alternate(attend(B, 2), to_latent(A, 1))
                alternate(attend(A, 3), to_latent(B, 1))
                alternate(attend(B, 3), to_ffn(A))
                alternate(feed_forward(A), to_ffn(B))
                alone(feed_forward(B))
                gated_memory(1)
                each(sum_squares, 6)

        @block.scalar
        def _(act):
            fn = nc.scalar.activation
            act.wait_ge(const_in.sem, 80)
            fn(tanh_gates[:], vec[:, VEC_GATES:VEC_GATES + 2], ACT.Tanh).then_inc(tanh_ready.sem, 1)
            act.wait_ge(trig_done.sem, 1)
            fn(cos[:], lanes[0].half(0, 0), ACT.Copy)
            fn(place[:], lanes[1].big[:, T_PLACE:T_END], ACT.Copy)
            fn(sin[:], lanes[0].half(0, 1), ACT.Copy).then_inc(trig_ready.sem, 1)

            with act.Fori(0, PAIRS) as it:
                step = Steps(act, act_step, it)
                nc.scalar.preload_act_table_set("natural_log_exp_and_others")

                def memory_save(L, g):
                    for j in range(2):
                        act.wait_ge(*L.mem_done.at(it, 2 * g + j + 1))
                        fn(L.big2[:, j * 512:(j + 1) * 512], L.ps[:, j, :], ACT.Copy)\
                            .then_inc(L.mem_saved.sem, 1)

                def gm_exp(L, g):
                    act.wait_ge(*L.gm_max.at(it, g + 1))
                    for qt in range(ST):
                        fn(L.chunk(L.big, qt), L.half(2, qt), ACT.Exp, bias=L.stat[:, 2 + qt:3 + qt],
                           scale=D ** -0.5, accum_out=L.stat[:, 4 + qt:5 + qt]).then_inc(L.gm_exp.sem, 1)

                def gm_context_save(L, g):
                    act.wait_ge(*L.gm_context.at(it, g + 1))
                    fn(L.xv[:], L.ps[:, 0, :], ACT.Copy).then_inc(L.gm_context_saved.sem, 1)

                def gm_sigmoid(L, g):
                    bg = VEC[["L0_xattn_b_gate", "L3_xattn_b_gate"][g]]
                    act.wait_ge(*L.gate_done.at(it, g + 1))
                    for c in range(DC):
                        fn(L.chunk(L.xl, c), L.half(1, c), ACT.Sigmoid, bias=vec[:, bg + c:bg + c + 1])\
                            .then_inc(L.gate_saved.sem, 1)

                def rstd(L, n):
                    eps = const[:, K_EPS + (n in (4, 5)):K_EPS + (n in (4, 5)) + 1]
                    act.wait_ge(*L.sumsq_done.at(it, n + 1))
                    step.done(fn(L.rstd[:], L.half(2, 0), ACT.Ln, bias=eps, scale=1.0 / D))
                    fn(L.rstd[:], L.rstd[:], ACT.Exp, scale=-0.5).then_inc(L.rstd_ready.sem, 1)

                def qk_save(L):
                    for j in range(2):
                        yield
                        act.wait_ge(*L.qk_done.at(it, j + 1))
                        fn(L.big[:, j * 512:(j + 1) * 512], L.ps[:, j, :], ACT.Copy)\
                            .then_inc(L.qk_saved.sem, 1)
                        yield
                    yield
                    yield

                def self_hi(L):
                    act.wait_ge(*L.rotated.at(it, 1))
                    fn(L.parts[:, 0:1024], L.big[:, 1024:2048], ACT.Copy).then_inc(L.hi_ready.sem, 1)

                def cross_hi(L):
                    act.wait_ge(*L.cross_done.at(it, 1))
                    act.wait_ge(*L.scores_t.at(it, HEADS))
                    fn(L.parts[:, 0:512], L.ps[:, 0, :], ACT.Copy).then_inc(L.hi_ready.sem, 1)

                def stacked_queries(L, a):
                    n = 0 if a == SELF else 4
                    if a == CROSS:
                        act.wait_ge(*L.scores_t.at(it, HEADS))
                    for j in range(HEADS // SHARE[a] // 2):
                        act.wait_ge(*L.q_stacked.at(it, n + j + 1))
                        fn(L.q[:, j * 512:(j + 1) * 512], L.ps[:, j + (2 if a == CROSS else 0), :], ACT.Copy)\
                            .then_inc(L.q_ready.sem, 1)

                def stacked_keys(L, a):
                    n = 0 if a == SELF else 4
                    for j in range(HEADS // SHARE[a] // 2):
                        act.wait_ge(*L.k_stacked.at(it, n + j + 1))
                        fn(L.big[:, j * 512:(j + 1) * 512], L.ps[:, j, :], ACT.Copy)\
                            .then_inc(L.k_saved.sem, 1)

                def latent_k_hi(L, half):
                    for j in range(2):
                        act.wait_ge(*L.k_done.at(it, 2 * half + j + 1))
                        if half:
                            act.wait_ge(*L.key_ready.at(it, 40))
                        fn(L.big[:, j * 512:(j + 1) * 512].bitcast(F32R), L.ps[:, j, :], ACT.Copy)\
                            .then_inc(L.k_saved.sem, 1)

                def latent_v_save(L):
                    for j in range(4):
                        kt, n = j // 2, j % 2
                        act.wait_ge(*L.v_done.at(it, 3 + j))
                        act.wait_ge(*L.v_resized.at(it, 2))
                        fn(L.slots(kt, 0, 64)[:, n * 8:n * 8 + 8, :],
                           L.ps[:, j, :].rearrange("p (h d) -> p h d", h=8), ACT.Copy)\
                            .then_inc(L.v_saved.sem, 1)

                def latent_q_hi(L, half):
                    if half == 0:
                        act.wait_ge(*L.scores_t.at(it, 2 * HEADS))
                    for j in range(2):
                        act.wait_ge(*L.q2_done.at(it, 2 * half + j + 1))
                        fn(L.q[:, j * 512:(j + 1) * 512], L.ps[:, 2 + j, :], ACT.Copy)\
                            .then_inc(L.q2_saved.sem, 1)

                def max_save(L, block):
                    a = BLOCKS[block][0]
                    act.wait_ge(*L.max_turned.at(it, block + 1))
                    turned = L.ps[0:32, 3, 0:P].bitcast(BF16)
                    if a == LATENT:
                        act.wait_ge(*L.rows_cleared.at(it, 1))
                        last = fn(L.max_rows[0:32, :], turned, ACT.Copy)
                    else:
                        tiles = HEADS // SHARE[a]
                        last = fn(L.q[96:P, 0:tiles * S].rearrange("p (t s) -> p t s", s=S),
                                  turned.unsqueeze(1).to_broadcast([32, tiles, S]), ACT.Copy)
                    last.then_inc(L.max_saved.sem, 1)

                def probabilities(L, block):
                    a, h0, heads = BLOCKS[block]

                    def exps(h):
                        n = a * HEADS + h0 + h
                        act.wait_ge(*L.scores_t.at(it, n + 1))
                        if h >= 2:
                            act.wait_ge(*L.pv_done.at(it, n - 1))
                        dst = L.probs[:, (h % 2) * 512:(h % 2 + 1) * 512]
                        if a == LATENT:
                            for kt in range(ST):
                                last = fn(dst[:, (1 - kt) * S:(2 - kt) * S], L.half(h % 2, 1 - kt), ACT.Exp,
                                          bias=L.key_bias[:, kt:kt + 1], scale=SCALE[a])
                        else:
                            lo = P if a == SELF else 0
                            last = fn(dst[:, lo:512], L.ps[:, h % 2, lo:512], ACT.Exp, scale=SCALE[a])
                        last.then_inc(L.probs_ready.sem, 1)

                    def reciprocals(g):
                        r = L.recip[0:64, (g % 2) * S:(g % 2 + 1) * S]
                        act.wait_ge(*L.pv_done.at(it, a * HEADS + (g + 1) * GROUP[a]))
                        if g >= 2:
                            act.wait_ge(*L.head_out.at(it, GROUP_BASE[a] + g - 1))
                        step.done(fn(r, L.ps[64:P, 2 + g % 2, 0:S], ACT.Ln))
                        fn(r, r, ACT.Exp, scale=-1.0).then_inc(L.recip_ready.sem, 1)

                    for h in range(heads + 1):
                        if h < heads:
                            exps(h)
                        if h >= 1 and h % GROUP[a] == 0:
                            reciprocals((h0 + h) // GROUP[a] - 1)
                        yield

                def silu(L):
                    for m in range(IC):
                        yield
                        act.wait_ge(*L.up_done.at(it, m + 1))
                        if m >= 2:
                            act.wait_ge(*L.hidden.at(it, m - 1))
                        fn(L.probs[:, (m % 2) * 512:(m % 2) * 512 + S], L.half(m % 4, 0), ACT.Silu)\
                            .then_inc(L.silu_ready.sem, 1)
                        yield

                def gelu(L):
                    for j in range(4):
                        act.wait_ge(*L.w1_done.at(it, j + 1))
                        fn(L.big[:, j * 512:(j + 1) * 512], L.ps[:, j, :], ACT.Gelu)\
                            .then_inc(L.gelu_ready.sem, 1)
                        yield

                def each(stage, *args):
                    for L in lanes:
                        stage(L, *args)

                def log_exp_table():
                    nc.scalar.preload_act_table_set("natural_log_exp_and_others")

                def gated_memory(g):
                    each(memory_save, g)
                    each(gm_exp, g)
                    each(gm_context_save, g)
                    each(gm_sigmoid, g)
                    log_exp_table()

                def to_self(L):
                    plan = PLAN["self", L.t]
                    for step in range(plan["end"]):
                        if step == plan["split"]:
                            self_hi(L)
                        if step == plan["stack"]:
                            stacked_queries(L, SELF)
                            stacked_keys(L, SELF)
                        if step == plan["turn"]:
                            max_save(L, 0)
                        yield

                def to_cross(L):
                    plan = PLAN["cross", L.t]
                    for step in range(plan["end"]):
                        if step == plan["norm"]:
                            rstd(L, 2)
                        if step == plan["project"]:
                            cross_hi(L)
                        if step == plan["stack"]:
                            stacked_queries(L, CROSS)
                            stacked_keys(L, CROSS)
                        if step == plan["turn"]:
                            max_save(L, 1)
                        yield

                def to_experts(L):
                    plan = PLAN["experts", L.t]
                    for step in range(plan["end"]):
                        if step == plan["norm"]:
                            rstd(L, 3)
                        yield

                def to_latent(L, half):
                    plan = PLAN["half" if half else "latent", L.t]
                    for step in range(plan["end"]):
                        if half == 0:
                            if step == plan["values"]:
                                latent_v_save(L)
                            if step == plan["norm"]:
                                rstd(L, 4)
                        if step == plan["project"]:
                            latent_k_hi(L, half)
                            latent_q_hi(L, half)
                        if step == plan["turn"]:
                            max_save(L, 2 + half)
                        yield

                def to_ffn(L):
                    plan = PLAN["ffn", L.t]
                    for step in range(plan["end"]):
                        if step == plan["norm"]:
                            rstd(L, 5)
                        yield

                def experts(L):
                    yield from silu(L)
                    for _ in range(2 * IC):
                        yield

                def feed_forward(L):
                    yield from gelu(L)
                    for _ in range(4):
                        yield

                def first_norm(L):
                    rstd(L, 1)
                    yield

                gated_memory(0)
                each(rstd, 0)
                rstd(A, 1)
                alternate(qk_save(A), first_norm(B))
                alternate(qk_save(B), to_self(A))
                alternate(probabilities(A, 0), to_self(B))
                alternate(probabilities(B, 0), to_cross(A))
                alternate(probabilities(A, 1), to_cross(B))
                alternate(probabilities(B, 1), to_experts(A))
                alternate(experts(A), to_experts(B))
                alternate(experts(B), to_latent(A, 0))
                log_exp_table()
                alternate(probabilities(A, 2), to_latent(B, 0))
                alternate(probabilities(B, 2), to_latent(A, 1))
                alternate(probabilities(A, 3), to_latent(B, 1))
                alternate(probabilities(B, 3), to_ffn(A))
                alternate(feed_forward(A), to_ffn(B))
                alone(feed_forward(B))
                log_exp_table()
                gated_memory(1)
                each(rstd, 6)
                for L in lanes:
                    act.wait_ge(*L.normed.at(it, 7))
                    n = it * LANES + L.t
                    act.dma_start(out_d[bass.ds(n, 1)].rearrange("a p n -> (a p) n"), L.xn[:])\
                        .then_inc(L.out_in_dram.sem, 16)
                assert step.n == act_step.per_pass, step.n

        @block.vector
        def _(dve):
            tt = nc.vector.tensor_tensor
            ts = nc.vector.tensor_scalar
            stt = nc.vector.scalar_tensor_tensor

            dve.wait_ge(const_in.sem, 80)
            for c in range(ST):
                last = ts(lanes[0].chunk(lanes[0].big, c), pos_i[:], const[:, K_IOTA:K_IOTA + 1], float(c * P),
                          ALU.subtract, ALU.is_equal)
            last.then_inc(onehot_ready.sem, 1)

            def lines(tile, n, cols=S):
                return tile.rearrange("p (n s) -> p n s", s=cols)

            def spread(row, n):
                return row.unsqueeze(1).to_broadcast([P, n, S])

            with dve.Fori(0, PAIRS) as it:
                step = Steps(dve, vec_step, it)

                def masks(L):
                    dve.wait_ge(L.inputs_in.sem, it * 80 + 80)
                    step.done(ts(L.sq[:, 0:S], L.expert_i[:], 1.0, None, ALU.is_equal))
                    tt(L.is_v[:, 0:S - 1], L.sq[:, 0:S - 1], L.sq[:, 1:S], ALU.mult)
                    nc.vector.memset(L.is_v[:, S - 1:S], 0.0)
                    ts(L.key_bias[:], L.keep_col[:], 0.0, -BIG * SCALE[LATENT], ALU.is_equal, ALU.mult)
                    dve.wait_ge(*L.rows_cleared.at(it, 1))
                    ins = ts(L.mask_row[0:1, :], L.keep_row[0:1, :], 0.0, -BIG, ALU.is_equal, ALU.mult)
                    ins.then_inc(L.masks_ready.sem, 1)
                    dve.wait_ge(*L.masks_ready.at(it, 1))

                def gm_max(L, g):
                    dve.wait_ge(*L.gm_scores.at(it, g + 1))
                    step.done(nc.vector.tensor_reduce(L.stat[:, 0:2], L.ps[:, 2, :].rearrange(
                        "p (q k) -> p q k", q=ST), AX.X, ALU.max))
                    ts(L.stat[:, 2:4], L.stat[:, 0:2], -D ** -0.5, None, ALU.mult).then_inc(L.gm_max.sem, 1)

                def gm_normalise(L, g):
                    dve.wait_ge(*L.gm_exp.at(it, 2 * g + 2))
                    step.done(nc.vector.reciprocal(L.stat[:, 6:8], L.stat[:, 4:6]))
                    for qt in range(ST):
                        last = ts(L.chunk(L.big, qt), L.chunk(L.big, qt), L.stat[:, 6 + qt:7 + qt], None, ALU.mult)
                    last.then_inc(L.gm_probs.sem, 1)

                def gm_turned_save(L, g):
                    dve.wait_ge(*L.gm_turned.at(it, g + 1))
                    nc.vector.tensor_copy(L.big[:, 512:1024], L.ps[:, 3, :]).then_inc(L.gm_turned_saved.sem, 1)

                def gm_fuse(L, g):
                    x = L.xin if g == 0 else L.x
                    dve.wait_ge(*L.gate_saved.at(it, 2 * g + 2))
                    step.done(tt(L.xl[:], L.xl[:], L.xv[:], ALU.mult))
                    step.done(tt(L.xl[:], L.xl[:], x[:], ALU.add))

                def square(L, src):
                    tt(L.sq[:], src[:], src[:], ALU.mult).then_inc(L.sq_ready.sem, 1)

                def normalise(L, n, src, dst, weight, bias=None):
                    at = VEC[weight]
                    dve.wait_ge(*L.rstd_ready.at(it, n + 1))
                    for c in range(DC):
                        last = stt(out=L.chunk(dst, c), in0=L.chunk(src, c), scalar=vec[:, at + c:at + c + 1],
                                   in1=L.rstd[:], op0=ALU.mult, op1=ALU.mult)
                    if bias:
                        step.done(last)
                        at = VEC[bias]
                        for c in range(DC):
                            last = ts(L.chunk(dst, c), L.chunk(dst, c), vec[:, at + c:at + c + 1], None, ALU.add)
                    last.then_inc(L.normed.sem, 1)
                    dve.wait_ge(*L.normed.at(it, n + 1))

                def split(L, src):
                    step.done(tt(lines(L.xv[:], DC), lines(src, DC), spread(L.is_v[:], DC), ALU.mult))
                    tt(L.xl[:], src, L.xv[:], ALU.subtract).then_inc(L.split.sem, 1)

                def self_values(L):
                    dve.wait_ge(*L.v_done.at(it, 1))
                    dve.wait_ge(*L.v_cleared.at(it, 2))
                    for kt in range(ST):
                        last = nc.vector.tensor_copy(L.slots(kt, 0, HEAD_DIM[SELF]), L.half(3, kt).rearrange(
                            "p (h d) -> p h d", h=HEADS))
                    last.then_inc(L.v_saved.sem, 1)

                def rotate(L):
                    dve.wait_ge(*L.qk_saved.at(it, 2))
                    tt(lines(L.big2[:, 0:1024], 4), lines(L.big[:, 0:1024], 4), spread(cos[:], 4), ALU.mult)
                    dve.wait_ge(*L.rot_done.at(it, 1))
                    step.done(tt(lines(L.big2[:, 1024:2048], 4),
                                 L.ps[:, 0:2, :].rearrange("p b (n s) -> p (b n) s", s=S), spread(sin[:], 4),
                                 ALU.mult))
                    last = tt(L.big[:, 1024:2048], L.big2[:, 0:1024], L.big2[:, 1024:2048], ALU.add)
                    last.then_inc(L.rotated.sem, 1)
                    dve.wait_ge(*L.rotated.at(it, 1))

                def self_lo(L):
                    dve.wait_ge(*L.hi_ready.at(it, 1))
                    tt(L.parts[:, 1024:2048], L.big[:, 1024:2048], L.parts[:, 0:1024].bitcast(F32),
                       ALU.subtract).then_inc(L.lo_ready.sem, 1)

                def cross_lo(L):
                    dve.wait_ge(*L.hi_ready.at(it, 2))
                    tt(L.parts[:, 512:1024], L.ps[:, 0, :], L.parts[:, 0:512].bitcast(F32),
                       ALU.subtract).then_inc(L.lo_ready.sem, 1)

                def latent_k_lo(L, half):
                    for j in range(2):
                        dve.wait_ge(*L.k_saved.at(it, 6 + 2 * half + j + 1))
                        tt(L.big[:, 1024 + j * 512:1024 + (j + 1) * 512], L.ps[:, j, :],
                           L.big[:, j * 512:(j + 1) * 512], ALU.subtract).then_inc(L.k2_lo.sem, 1)

                def latent_q_lo(L, half):
                    for j in range(2):
                        dve.wait_ge(*L.q2_saved.at(it, 2 * half + j + 1))
                        tt(L.q[:, 1024 + j * 512:1024 + (j + 1) * 512], L.ps[:, 2 + j, :],
                           L.q[:, j * 512:(j + 1) * 512].bitcast(F32), ALU.subtract).then_inc(L.q2_lo.sem, 1)

                def cross_values(L):
                    dve.wait_ge(*L.v_done.at(it, 2))
                    dve.wait_ge(*L.pv_done.at(it, HEADS))
                    for kt in range(ST):
                        last = nc.vector.tensor_copy(
                            L.slots(kt, 0, HEAD_DIM[CROSS]),
                            L.ps[:, 1, kt * P:(kt + 1) * P].rearrange("p (h d) -> p h d", h=HEADS))
                    last.then_inc(L.v_saved.sem, 1)

                def maxima(L, block, h):
                    a, h0, heads = BLOCKS[block]
                    mx = L.max[:, 0:ST * heads].rearrange("p (q h) -> p q h", q=ST)
                    dve.wait_ge(*L.scores.at(it, a * HEADS + h0 + h + 1))
                    if a == SELF:
                        nc.vector.tensor_reduce(mx[:, 0:1, h], L.ps[:, h % 4, 0:P], AX.X, ALU.max)
                        last = nc.vector.tensor_reduce(mx[:, 1:2, h], L.ps[:, h % 4, S:2 * S], AX.X, ALU.max)
                    else:
                        last = nc.vector.tensor_reduce(mx[:, :, h], L.ps[:, h % 4, :].rearrange(
                            "p (q k) -> p q k", q=ST), AX.X, ALU.max)
                    last.then_inc(L.max_ready.sem, 1)
                    if h < heads - 1:
                        return
                    dve.wait_ge(*L.max_ready.at(it, a * HEADS + h0 + heads))
                    parts = L.max_parts[:].rearrange("p (q r) -> p q r", q=ST)[:, :, 0:2 * heads]\
                        .rearrange("p q (n h) -> p q n h", n=2)
                    step.done(nc.vector.tensor_copy(parts[:, :, 0, :], mx))
                    tt(parts[:, :, 1, :], mx, parts[:, :, 0, :], ALU.subtract).then_inc(L.max_split.sem, 1)

                def head_outputs(L, block):
                    a, h0, heads = BLOCKS[block]
                    for h in range(heads + 1):
                        if h >= 1 and h % GROUP[a] == 0:
                            g = (h0 + h) // GROUP[a] - 1
                            dve.wait_ge(*L.recip_ready.at(it, GROUP_BASE[a] + g + 1))
                            lo = 64 * (g % 2)
                            tt(L.big2[lo:lo + 64, (g // 2) * S:(g // 2 + 1) * S], L.ps[0:64, 2 + g % 2, 0:S],
                               L.recip[0:64, (g % 2) * S:(g % 2 + 1) * S], ALU.mult).then_inc(L.head_out.sem, 1)
                        yield

                def split_context(L):
                    dve.wait_ge(*L.head_out.at(it, 4))
                    split(L, L.big2[:, 0:512])

                def add(L, n):
                    dve.wait_ge(*L.added_done.at(it, n + 1))
                    src = L.ps[:, 2:4, 0:S] if n == 2 else L.ps[:, 0, :].rearrange("p (c s) -> p c s", s=S)
                    x = L.x[:].rearrange("p (c s) -> p c s", s=S)
                    if n < 3:
                        last = tt(x, src, x, ALU.add)
                    else:
                        if n == 3:
                            dve.wait_ge(tanh_ready.sem, 1)
                        last = stt(out=x, in0=src, scalar=tanh_gates[:, n - 3:n - 2], in1=x,
                                   op0=ALU.mult, op1=ALU.add)
                    last.then_inc(L.added.sem, 1)
                    dve.wait_ge(*L.added.at(it, n + 1))

                def hidden(L):
                    for _ in range(2):
                        yield
                    for m in range(IC):
                        dve.wait_ge(*L.silu_ready.at(it, m + 1))
                        s = L.probs[:, (m % 2) * 512:(m % 2) * 512 + S]
                        h = L.probs[:, (m % 2) * 512 + S:(m % 2) * 512 + 2 * S]
                        step.done(tt(h, L.half(m % 4, 1), s, ALU.mult))
                        step.done(tt(L.chunk(L.big, m), h, L.is_v[:], ALU.mult))
                        tt(L.chunk(L.big2, m), h, L.chunk(L.big, m), ALU.subtract).then_inc(L.hidden.sem, 1)
                        yield
                        yield

                def centre(L, n):
                    dve.wait_ge(*L.sum_done.at(it, n + 1))
                    for c in range(DC):
                        last = stt(out=L.chunk(L.xl, c), in0=L.half(3, 0), scalar=-1.0 / D, in1=L.chunk(L.x, c),
                                   op0=ALU.mult, op1=ALU.add)
                    step.done(last)
                    square(L, L.xl)

                def each(stage, *args):
                    for L in lanes:
                        stage(L, *args)

                def gated_memory(g):
                    each(gm_max, g)
                    each(gm_normalise, g)
                    each(gm_turned_save, g)
                    for L in lanes:
                        gm_fuse(L, g)
                        square(L, L.xl)

                each(masks)
                gated_memory(0)
                for L in lanes:
                    if L.t == 0:
                        dve.wait_ge(trig_ready.sem, 1)
                    normalise(L, 0, L.xl, L.x, "L0_xattn_norm_w")
                    square(L, L.x)

                def first_norm(L):
                    normalise(L, 1, L.x, L.xn, "L1_xattn_ln_in_w")
                    split(L, L.xn[:])
                    yield

                def values_of_self(L):
                    for _ in range(6):
                        yield

                def to_self(L):
                    plan = PLAN["self", L.t]
                    for turn in range(plan["end"]):
                        if turn == plan["rotate"]:
                            self_values(L)
                            rotate(L)
                        if turn == plan["split"]:
                            self_lo(L)
                        for h in heads_at(plan, turn, HEADS):
                            maxima(L, 0, h)
                        yield

                def to_cross(L):
                    plan = PLAN["cross", L.t]
                    for turn in range(plan["end"]):
                        if turn == plan["dense"]:
                            split_context(L)
                            add(L, 0)
                            square(L, L.x)
                        if turn == plan["norm"]:
                            normalise(L, 2, L.x, L.xn, "L1_xattn_ln_post_cross_w")
                        if turn == plan["project"]:
                            cross_lo(L)
                            cross_values(L)
                        for h in heads_at(plan, turn, HEADS):
                            maxima(L, 1, h)
                        yield

                def to_experts(L):
                    plan = PLAN["experts", L.t]
                    for turn in range(plan["end"]):
                        if turn == plan["dense"]:
                            add(L, 1)
                            square(L, L.x)
                        if turn == plan["norm"]:
                            normalise(L, 3, L.x, L.xn, "L1_xattn_ln_post_attn_w")
                            split(L, L.xn[:])
                        yield

                def to_latent(L, half):
                    plan = PLAN["half" if half else "latent", L.t]
                    for turn in range(plan["end"]):
                        if half == 0:
                            if turn == plan["values"]:
                                add(L, 2)
                            if turn == plan["mean"]:
                                centre(L, 0)
                            if turn == plan["norm"]:
                                normalise(L, 4, L.xl, L.xn, "L2_xattn_ln_q_g", "L2_xattn_ln_q_b")
                        if turn == plan["project"]:
                            latent_k_lo(L, half)
                            latent_q_lo(L, half)
                        for h in heads_at(plan, turn, 8):
                            maxima(L, 2 + half, h)
                        yield

                def to_ffn(L):
                    plan = PLAN["ffn", L.t]
                    for turn in range(plan["end"]):
                        if turn == plan["dense"]:
                            add(L, 3)
                        if turn == plan["mean"]:
                            centre(L, 1)
                        if turn == plan["norm"]:
                            normalise(L, 5, L.xl, L.xn, "L2_xattn_ln_ff_g", "L2_xattn_ln_ff_b")
                        yield

                def experts(L):
                    yield from hidden(L)
                    for _ in range(2 * IC - 2):
                        yield

                def feed_forward(L):
                    for _ in range(8):
                        yield
                    add(L, 4)

                alone(first_norm(A))
                alternate(values_of_self(A), first_norm(B))
                alternate(values_of_self(B), to_self(A))
                alternate(head_outputs(A, 0), to_self(B))
                alternate(head_outputs(B, 0), to_cross(A))
                alternate(head_outputs(A, 1), to_cross(B))
                alternate(head_outputs(B, 1), to_experts(A))
                alternate(experts(A), to_experts(B))
                alternate(experts(B), to_latent(A, 0))
                alternate(head_outputs(A, 2), to_latent(B, 0))
                alternate(head_outputs(B, 2), to_latent(A, 1))
                alternate(head_outputs(A, 3), to_latent(B, 1))
                alternate(head_outputs(B, 3), to_ffn(A))
                alternate(feed_forward(A), to_ffn(B))
                alone(feed_forward(B))
                gated_memory(1)
                for L in lanes:
                    normalise(L, 6, L.xl, L.xn, "L3_xattn_norm_w")
                assert step.n == vec_step.per_pass, step.n


def tables():
    f = np.float32
    dim = HEAD_DIM[SELF]
    inv = (f(1.0) / np.power(f(10000.0), np.arange(0, dim, 2, dtype=f) / f(dim))).astype(f)
    freqs = np.outer(np.arange(S, dtype=f), inv).astype(f)
    emb = np.concatenate([freqs, freqs], axis=-1)
    rows = np.arange(P)
    const = np.zeros((P, K_END), f)
    const[:, K_IDENT:K_IDENT + P] = np.eye(P)
    const[:, K_ONES:K_ONES + P] = 1.0
    for r in range(P):
        j = r % dim
        const[r + dim // 2 if j < dim // 2 else r - dim // 2, K_ROT + r] = -1.0 if j < dim // 2 else 1.0
    trig = np.zeros((P, T_END), f)
    for at, table in ((T_COS, np.cos(emb)), (T_SIN, np.sin(emb))):
        spread = table[:, rows % dim]
        for c in range(ST):
            trig[:, at + c * P:at + (c + 1) * P] = spread[c * P:(c + 1) * P]
    used = rows[:96]
    const[used, K_OWN16 + used % 32 // 16] = 1.0
    const[used, K_OWN8 + used % 32 // 8] = 1.0
    for h in range(HEADS):
        const[96 + h, K_SEL + h] = const[112 + h, K_SEL + h] = -1.0
    const[rows, K_HALF + rows // 64] = 1.0
    const[:, K_IOTA] = rows
    const[:, K_EPS] = 1e-6
    const[:, K_EPS + 1] = 1e-5
    b = np.zeros((P, KB_END), f)
    b[:, KB_IDENT:KB_IDENT + P] = np.eye(P)
    for j in range(4):
        for i, one in enumerate(PLACE_BLOCKS):
            at = T_PLACE + j * PLACE_COLS + 32 * i
            trig[32 * j + np.arange(32), at + np.arange(32)] = float(one)
    b[:, KB_CAUSAL:KB_CAUSAL + P] = np.where(rows[None, :] > rows[:, None], -BIG, 0.0)
    b[:, KB_CAUSAL_T:KB_CAUSAL_T + P] = np.where(rows[:, None] > rows[None, :], -BIG, 0.0)
    for h in range(8):
        b[h, KB_SEL + h] = b[8 + h, KB_SEL + h] = -1.0
    b[0, KB_ONEROW:KB_ONEROW + P] = 1.0
    return const, (b.view(np.uint32) >> 16).astype(np.uint16), trig


def kernel(**inputs):
    import concourse.bacc as _bacc
    from concourse.bass_utils import run_bass_kernel_spmd as _run

    a = {k: np.asarray(v) for k, v in inputs.items()}

    def chunks(m):
        k = m.shape[0] // P
        return m.reshape(k, P, m.shape[1]).transpose(1, 0, 2).reshape(P, k * m.shape[1])

    def padded(m, rows, cols):
        out = np.zeros((rows, cols), m.dtype)
        out[:m.shape[0], :m.shape[1]] = m
        return out

    def pack(*parts):
        return np.ascontiguousarray(np.concatenate(parts, axis=1))

    one = "L1_xattn_"
    two = "L2_xattn_"
    const, constb, trig = tables()
    arrays = {
        "x": np.ascontiguousarray(a["x"].transpose(0, 2, 1).reshape(BATCH, DC, P, S)
                                  .transpose(0, 2, 1, 3).reshape(BATCH, P, DC * S)),
        "ctx": np.ascontiguousarray(a["ctx_1024"].transpose(0, 2, 1)),
        "pos": np.ascontiguousarray(a["pos_1xS"]),
        "expert": np.ascontiguousarray(a["mask_BxS_ik0"]),
        "keep_row": np.ascontiguousarray(a["mask_BxS2_bk0"]).view(np.uint32),
        "keep_col": np.ascontiguousarray(
            a["mask_BxS2_bk0"].reshape(BATCH, ST, P).transpose(0, 2, 1)).reshape(BATCH, S).view(np.uint32),
        "gm": np.stack([pack(a[f"L{n}_xattn_W_mem"].T, chunks(a[f"L{n}_xattn_W_gate"].T)) for n in (0, 3)]),
        "l1a": pack(chunks(a[one + "v_qkv"]), chunks(a[one + "l_qkv"]), chunks(a[one + "v_dense"]),
                    chunks(a[one + "l_dense"]), chunks(a[one + "cq_w"]), a[one + "ckv_w"],
                    a[one + "cdense_w"]),
        "l1m": pack(*[chunks(padded(a[one + n], D, I_PAD)) for n in ("v_gate", "l_gate", "v_up", "l_up")]),
        "l1d": pack(*[chunks(padded(a[one + n], I_PAD, D)) for n in ("v_down", "l_down")]),
        "l2q": pack(chunks(a[two + "Wq"]), a[two + "Wkv"]),
        "l2f": pack(chunks(a[two + "Wo"]), chunks(a[two + "W1"]), chunks(a[two + "W2"])),
        "vec": pack(*[a[n].reshape(DC, P).T for n in VECTORS],
                    *[np.broadcast_to(a[two + n].reshape(1, 1), (P, 1)) for n in ("attn_gate", "ff_gate")]),
        "const": const,
        "constb": constb,
        "trig": trig,
    }
    nc = _bacc.Bacc("TRN2", target_bir_lowering=False, num_devices=1)
    args = [nc.dram_tensor(f"in_{n}", v.shape, mybir.dt.from_np(v.dtype), kind="ExternalInput").ap()
            for n, v in arrays.items()]
    args.append(nc.dram_tensor("out_0", (BATCH, P, DC * S), F32, kind="ExternalOutput").ap())
    build(nc, *args)
    r = _run(nc, [{f"in_{n}": v for n, v in arrays.items()}], core_ids=[0])
    got = r.results[0]["out_0"]
    return got.reshape(BATCH, P, DC, S).transpose(0, 3, 2, 1).reshape(BATCH, S, D)
```

```python
from contextlib import ExitStack
from itertools import chain

import numpy as np

import concourse.bass as bass
from concourse import mybir

F32 = mybir.dt.float32
F32R = mybir.dt.float32r
BF16 = mybir.dt.bfloat16
I32 = mybir.dt.int32
U8 = mybir.dt.uint8
ALU = mybir.AluOpType
ACT = mybir.ActivationFunctionType
AX = mybir.AxisListType

P = 128
BATCH, S, D = 4, 256, 256
C = 128
LANES = 2
PAIRS = BATCH // LANES
DC = D // P
ST = S // P
HEADS = 16
HIDDEN = 688
IC = -(-HIDDEN // P)
REST = HIDDEN - (IC - 1) * P
I_PAD = IC * P
INNER = 1024
NC2 = INNER // P
BIG = 2.0 ** 100

SELF, CROSS, LATENT = range(3)
BLOCKS = [(SELF, 0, 16), (CROSS, 0, 16), (LATENT, 0, 8), (LATENT, 8, 8)]
HEAD_DIM = [16, 8, 64]
SCALE = [16 ** -0.5, 8 ** -0.5, 64 ** -0.5]
GROUP = [4, 8, 1]
SHARE = [2, 4]
V_PAD = 56
VROW = V_PAD + HEADS * P


def columns(*sizes):
    at = [0]
    for s in sizes:
        at.append(at[-1] + s)
    return at


GM_MEM, GM_GATE, GM_END = columns(D, 2 * DC * D)
(A_VQKV, A_LQKV, A_VDENSE, A_LDENSE, A_CQ, A_CKV, A_CDENSE, A_END) = columns(
    DC * 3 * D, DC * 3 * D, DC * D, DC * D, DC * P, 2 * P, D)
(M_VGATE, M_LGATE, M_VUP, M_LUP, M_END) = columns(*[DC * I_PAD] * 4)
(M_VDOWN, M_LDOWN, M_DOWN_END) = columns(IC * D, (IC - 1) * D)
(Q_WQ, Q_WKV, Q_END) = columns(DC * INNER, 2 * INNER)
(F_WO, F_W1, F_W2, F_END) = columns(NC2 * D, DC * INNER, NC2 * D)
VECTORS = ["L0_xattn_b_gate", "L0_xattn_norm_w", "L1_xattn_ln_in_w", "L1_xattn_ln_post_cross_w",
           "L1_xattn_ln_post_attn_w", "L2_xattn_ln_q_g", "L2_xattn_ln_q_b", "L2_xattn_ln_ff_g",
           "L2_xattn_ln_ff_b", "L3_xattn_b_gate", "L3_xattn_norm_w"]
VEC = {n: DC * i for i, n in enumerate(VECTORS)}
VEC_GATES = DC * len(VECTORS)
VEC_END = VEC_GATES + 2
(K_IDENT, K_ONES, K_ROT, K_OWN16, K_OWN8, K_SEL, K_HALF, K_IOTA, K_EPS, K_END) = columns(
    P, P, P, 2, 4, HEADS, 2, 1, 2)
PLACE_BLOCKS = "110010100"
PLACE_COLS = 32 * len(PLACE_BLOCKS)
Q_HI, Q_LO, K_HI, K_LO = (PLACE_BLOCKS.index(x) for x in ("1010", "0100", "1100", "0010"))
(T_COS, T_SIN, T_PLACE, T_END) = columns(ST * P, ST * P, 4 * PLACE_COLS)
(KB_IDENT, KB_CAUSAL, KB_CAUSAL_T, KB_SEL, KB_ONEROW, KB_END) = columns(P, P, P, 8, P)


class Signal:

    def __init__(self, sem, per_pass):
        self.sem, self.per_pass = sem, per_pass

    def at(self, it, k):
        return self.sem, it * self.per_pass + k


class Steps:

    def __init__(self, engine, raised, it):
        self.engine, self.raised, self.it, self.n = engine, raised, it, 0

    def done(self, instruction):
        self.n += 1
        instruction.then_inc(self.raised.sem, 1)
        self.engine.wait_ge(*self.raised.at(self.it, self.n))


def alternate(first, second):
    for _ in first:
        next(second, None)
    for _ in second:
        pass


PLAN = {
    ("self", 0): {"rotate": 0, "split": 2, "stack": 4, "max": 6, "heads": 2, "turn": 14, "end": 15},
    ("early", 1): {"rotate": 0, "split": 3, "stack": 5, "end": 7},
    ("self", 1): {"max": 0, "heads": 1, "turn": 16, "end": 17},
    ("cross", 0): {"dense": 2, "norm": 4, "project": 6, "stack": 7, "max": 9, "heads": 3, "turn": 15, "end": 17},
    ("cross", 1): {"dense": 2, "norm": 4, "project": 6, "stack": 7, "max": 9, "heads": 3, "turn": 15, "end": 17},
    ("latent", 0): {"values": 0, "mean": 2, "norm": 4, "project": 6, "max": 9, "heads": 1, "turn": 19, "end": 20},
    ("latent", 1): {"values": 0, "mean": 1, "norm": 2, "project": 3, "max": 4, "heads": 3, "turn": 7, "end": 8},
    ("half", 0): {"project": 0, "max": 2, "heads": 2, "turn": 7, "end": 8},
    ("half", 1): {"project": 0, "max": 2, "heads": 2, "turn": 7, "end": 8},
    ("experts", 0): {"dense": 1, "norm": 3, "parts": 7, "weights": [10, 13], "end": 14},
    ("experts", 1): {"dense": 1, "norm": 4, "parts": 7, "weights": [14, 17], "end": 18},
    ("ffn", 0): {"weights": [0, 2], "dense": 1, "mean": 3, "norm": 5, "parts": 7, "end": 8},
    ("ffn", 1): {"weights": [2, 5], "dense": 0, "mean": 1, "norm": 3, "parts": 4, "end": 6},
}


def heads_at(plan, step, heads):
    if step < plan.get("max", plan["end"]):
        return []
    n = plan["heads"]
    return range(n * (step - plan["max"]), min(heads, n * (step - plan["max"] + 1)))


def alone(stage):
    for _ in stage:
        pass


def build(nc, x_d, ctx_d, pos_d, expert_d, keep_row_d, keep_col_d, gm_d, l1a_d, l1m_d, l1d_d, l2q_d, l2f_d,
          vec_d, const_d, constb_d, trig_d, out_d):
    with ExitStack() as stack:
        def sb(name, cols, dt=F32):
            return stack.enter_context(nc.sbuf_tensor(name, [P, cols], dt))

        def signal(name, per_pass=1):
            return Signal(stack.enter_context(nc.semaphore(name)), per_pass)

        gm_w = sb("gm_w", GM_END)
        attn_w = sb("attn_w", A_END)
        ffn_w = sb("ffn_w", M_END)
        vec = sb("vec", VEC_END)
        const = sb("const", K_END)
        constb = sb("constb", KB_END, BF16)
        place = sb("place", 4 * PLACE_COLS, F32R)
        cos = sb("cos", S)
        sin = sb("sin", S)
        tanh_gates = sb("tanh_gates", 2)

        weights_in = {n: signal(f"weights_in_{n}") for n in ("gm", "l1a", "l1m", "l1d", "l2q", "l2f")}
        const_in = signal("const_in")
        onehot_ready = signal("onehot_ready")
        trig_done = signal("trig_done")
        trig_ready = signal("trig_ready")
        tanh_ready = signal("tanh_ready")
        pool_waits = signal("pool_waits")
        vec_step = signal("vec_step", 74)
        act_step = signal("act_step", 58)

        class Lane:
            def __init__(self, t):
                self.t = t

                def s(name, per_pass=1):
                    return signal(f"{name}_{'AB'[t]}", per_pass)

                def m(name, cols, dt=F32):
                    return sb(f"{name}_{'AB'[t]}", cols, dt)

                self.ps = stack.enter_context(nc.psum_tensor(f"ps_{'AB'[t]}", [P, 4, 512], F32))
                self.x = m("x", DC * S)
                self.ctx = m("ctx", S)
                self.kz = m("kz", HEADS * S, F32R)
                self.parts = self.kz[:, 8 * S:16 * S]
                self.q = m("q", NC2 * S, F32R)
                self.v = m("v", ST * VROW)
                self.xin = self.v[:, 0:DC * S]
                self.expert_i = self.v[:, DC * S:DC * S + S].bitcast(I32)
                self.big = m("big", NC2 * S)
                self.big2 = m("big2", NC2 * S)
                self.probs = m("probs", 2 * 512)
                self.xn = m("xn", DC * S)
                self.xv = m("xv", DC * S)
                self.xl = m("xl", DC * S)
                self.sq = self.probs[:, 0:DC * S]
                self.rstd = m("rstd", S)
                self.recip = m("recip", 2 * S)
                self.is_v = m("is_v", S)
                self.keep_col = m("keep_col", ST, U8)
                self.keep_row = m("keep_row", S, U8)
                self.key_bias = m("key_bias", ST)
                self.mask_row = m("mask_row", S, BF16)
                self.max = m("max", ST * HEADS)
                self.max_parts = m("max_parts", ST * 32, BF16)
                self.max_rows = m("max_rows", S, BF16)
                self.stat = m("stat", 8)

                self.inputs_in = s("inputs_in")
                self.masks_in = s("masks_in")
                self.out_in_dram = s("out_in_dram", 16)
                self.v_cleared = s("v_cleared", 2)
                self.rows_cleared = s("rows_cleared")
                self.v_resized = s("v_resized", 2)
                self.masks_ready = s("masks_ready")
                self.mem_done = s("mem_done", 4)
                self.mem_saved = s("mem_saved", 4)
                self.gm_scores = s("gm_scores", 2)
                self.gm_max = s("gm_max", 2)
                self.gm_exp = s("gm_exp", 4)
                self.gm_probs = s("gm_probs", 2)
                self.gm_turned = s("gm_turned", 2)
                self.gm_turned_saved = s("gm_turned_saved", 2)
                self.gm_context = s("gm_context", 2)
                self.gm_context_saved = s("gm_context_saved", 2)
                self.gate_done = s("gate_done", 2)
                self.gate_saved = s("gate_saved", 2)
                self.sum_done = s("sum_done", 2)
                self.sq_ready = s("sq_ready", 7)
                self.sumsq_done = s("sumsq_done", 7)
                self.rstd_ready = s("rstd_ready", 7)
                self.normed = s("normed", 7)
                self.split_v = s("split_v", 3)
                self.split = s("split", 3)
                self.x_hi = s("x_hi", 2)
                self.x_lo = s("x_lo", 2)
                self.w_hi = s("w_hi", IC + 2)
                self.w_lo = s("w_lo", IC + 2)
                self.hi_ready = s("hi_ready", 2)
                self.lo_ready = s("lo_ready", 2)
                self.q_stacked = s("q_stacked", 6)
                self.q_ready = s("q_ready", 6)
                self.k_stacked = s("k_stacked", 6)
                self.q2_lo = s("q2_lo", 4)
                self.qk_done = s("qk_done", 2)
                self.qk_saved = s("qk_saved", 2)
                self.rot_done = s("rot_done")
                self.rotated = s("rotated")
                self.cross_done = s("cross_done")
                self.v_done = s("v_done", 6)
                self.v_saved = s("v_saved", 6)
                self.k_done = s("k_done", 4)
                self.q2_done = s("q2_done", 4)
                self.q2_saved = s("q2_saved", 4)
                self.k_saved = s("k_saved", 10)
                self.k2_lo = s("k2_lo", 4)
                self.key_lo = s("key_lo", 16)
                self.key_ready = s("key_ready", 48)
                self.scores = s("scores", 48)
                self.max_ready = s("max_ready", 48)
                self.max_split = s("max_split", 4)
                self.max_turned = s("max_turned", 4)
                self.max_saved = s("max_saved", 8)
                self.scores_t = s("scores_t", 48)
                self.probs_ready = s("probs_ready", 48)
                self.pv_done = s("pv_done", 48)
                self.recip_ready = s("recip_ready", 22)
                self.head_out = s("head_out", 22)
                self.added_done = s("added_done", 5)
                self.added = s("added", 5)
                self.up_done = s("up_done", 6)
                self.silu_ready = s("silu_ready", 6)
                self.hidden = s("hidden", 6)
                self.w1_done = s("w1_done", 4)
                self.gelu_ready = s("gelu_ready", 4)

            def unit(self, u, part):
                at = (u % 2) * 2048 + part * 1024
                return self.kz[:, at:at + 1024]

            def x_part(self, i, part, lo=0, hi=S):
                return self.chunk(self.q, 4 * part + i, lo, hi)

            def chunk(self, tile, c, lo=0, hi=S):
                return tile[:, c * S + lo:c * S + hi]

            def half(self, bank, h, lo=0, hi=S):
                return self.ps[:, bank, h * S + lo:h * S + hi]

            def values(self, a, h, kt):
                at = kt * VROW + V_PAD + h * P - HEAD_DIM[a] * (h % GROUP[a])
                return self.v[:, at:at + P]

            def slots(self, kt, lo, width):
                at = kt * VROW + V_PAD
                return self.v[:, at:at + HEADS * P].rearrange("p (h c) -> p h c", c=P)[:, :, lo:lo + width]

        lanes = A, B = [Lane(t) for t in range(LANES)]
        pos_i = lanes[0].xv[:, 0:S].bitcast(I32)
        down_w = lanes[1].v

        def w(tile, at, chunk, lo, hi, width):
            return tile[:, at + chunk * width + lo:at + chunk * width + hi]

        def up_unit(m):
            n = 8 if m < IC - 1 else 4
            return ffn_w[:, 0:M_END].rearrange("p (n i) -> p n i", i=I_PAD)[:, 0:n, m * P:(m + 1) * P]

        def w1_unit(u):
            return ffn_w[:, F_W1:F_W2].rearrange("p (n i) -> p n i", i=INNER)[:, :, u * 512:(u + 1) * 512]

        def stack_place(start, j):
            at = j * PLACE_COLS + 32 * start
            return place[:, at:at + P]

        ident = const[:, K_IDENT:K_IDENT + P]
        ones = const[:, K_ONES:K_ONES + P]
        rot = const[:, K_ROT:K_ROT + P]
        identb = constb[:, KB_IDENT:KB_IDENT + P]
        onerow = constb[:, KB_ONEROW:KB_ONEROW + P]

        def sel(h):
            return constb[:, KB_SEL + h:KB_SEL + h + 1].to_broadcast([P, P])

        GROUP_BASE = [0, 4, 6]

        block = stack.enter_context(nc.Block())

        @block.sync
        def _(sp):
            for L in lanes:
                sp.sem_inc(L.out_in_dram.sem, 16)
            sp.dma_start(const[:], const_d).then_inc(const_in.sem, 16)
            sp.dma_start(pos_i[:], pos_d.rearrange("a s -> (a s)").partition_broadcast(P))\
                .then_inc(const_in.sem, 16)
            sp.dma_start(lanes[1].big[:, 0:T_END], trig_d).then_inc(const_in.sem, 16)
            sp.dma_start(gm_w[:], gm_d[0]).then_inc(weights_in["gm"].sem, 16)
            with sp.Fori(0, PAIRS) as it:
                for L in lanes:
                    n = it * LANES + L.t
                    sp.dma_start(L.ctx[:], ctx_d[bass.ds(n, 1)].rearrange("a p n -> (a p) n"))\
                        .then_inc(L.inputs_in.sem, 16)
                    sp.dma_start(L.xin[:], x_d[bass.ds(n, 1)].rearrange("a p n -> (a p) n"))\
                        .then_inc(L.inputs_in.sem, 16)
                for L in lanes:
                    n = it * LANES + L.t
                    sp.dma_start(L.expert_i[:],
                                 expert_d[bass.ds(n, 1)].rearrange("a s -> (a s)").partition_broadcast(P))\
                        .then_inc(L.masks_in.sem, 16)
                    sp.dma_start(L.keep_col[:], keep_col_d[bass.ds(n, 1)].bitcast(U8).rearrange("a (p n) -> (a p) n", p=P))\
                        .then_inc(L.masks_in.sem, 16)
                    sp.dma_start(L.keep_row[0:1, :], keep_row_d[bass.ds(n, 1)].bitcast(U8)).then_inc(L.masks_in.sem, 16)
                sp.dma_start(attn_w[:], l1a_d).then_inc(weights_in["l1a"].sem, 16)
                sp.dma_start(ffn_w[:], l1m_d).then_inc(weights_in["l1m"].sem, 16)
                for L in lanes:
                    sp.wait_ge(*L.gate_done.at(it, 1))
                sp.dma_start(gm_w[:], gm_d[1]).then_inc(weights_in["gm"].sem, 16)
                sp.wait_ge(*lanes[1].pv_done.at(it, 2 * HEADS))
                sp.dma_start(down_w[:, 0:M_DOWN_END], l1d_d).then_inc(weights_in["l1d"].sem, 16)
                for L in lanes:
                    sp.wait_ge(*L.added_done.at(it, 2))
                sp.dma_start(attn_w[:, 0:Q_END], l2q_d).then_inc(weights_in["l2q"].sem, 16)
                for L in lanes:
                    sp.wait_ge(*L.up_done.at(it, IC))
                sp.dma_start(ffn_w[:, 0:F_END], l2f_d).then_inc(weights_in["l2f"].sem, 16)
                for L in lanes:
                    sp.wait_ge(*L.gate_done.at(it, 2))
                sp.dma_start(gm_w[:], gm_d[0]).then_inc(weights_in["gm"].sem, 16)
            sp.wait_ge(weights_in["gm"].sem, 16 + PAIRS * 32)
            for L in lanes:
                sp.wait_ge(L.out_in_dram.sem, 16 + PAIRS * 16)

        @block.gpsimd
        def _(pool):
            def wait(sem, value):
                pool.wait_ge(sem, value)
                pool.sem_inc(pool_waits.sem, 1)

            with pool.Fori(0, PAIRS) as it:
                for L in lanes:
                    nc.gpsimd.memset(L.max_rows[:], 0.0)
                    nc.gpsimd.memset(L.mask_row[:], 0.0).then_inc(L.rows_cleared.sem, 1)
                for L in lanes:
                    wait(*L.sq_ready.at(it, 1))
                    nc.gpsimd.memset(L.v[:], 0.0).then_inc(L.v_cleared.sem, 1)
                    wait(*L.v_cleared.at(it, 1))
                    for kt in range(ST):
                        last = nc.gpsimd.memset(L.slots(kt, 64, HEAD_DIM[SELF]), 1.0)
                    last.then_inc(L.v_cleared.sem, 1)
                def resize_for_cross(L):
                    wait(*L.pv_done.at(it, HEADS))
                    for kt in range(ST):
                        nc.gpsimd.memset(L.slots(kt, 8, 8), 0.0)
                        last = nc.gpsimd.memset(L.slots(kt, 72, 8), 0.0)
                    last.then_inc(L.v_resized.sem, 1)

                def resize_for_latent(L):
                    wait(*L.pv_done.at(it, 2 * HEADS))
                    if L.t == 1:
                        for M in lanes:
                            wait(*M.added_done.at(it, 3))
                    for kt in range(ST):
                        last = nc.gpsimd.memset(L.slots(kt, 64, HEAD_DIM[LATENT]), 1.0)
                    last.then_inc(L.v_resized.sem, 1)

                def stacked_keys(L, a):
                    n = 0 if a == SELF else 4
                    own = K_OWN16 if a == SELF else K_OWN8
                    for h in range(HEADS):
                        t = h // SHARE[a]
                        if h % (2 * SHARE[a]) == 0:
                            wait(*L.k_saved.at(it, n + t // 2 + 1))
                        if h == 8 and a == SELF:
                            wait(*L.k_stacked.at(it, 4))
                        mask, maxima = own + h % SHARE[a], K_SEL + h
                        nc.gpsimd.tensor_scalar(L.chunk(L.kz, h), L.chunk(L.big, t), const[:, mask:mask + 1],
                                                const[:, maxima:maxima + 1], ALU.mult, ALU.add)\
                            .then_inc(L.key_ready.sem, 1)

                def latent_keys_lo(L, half):
                    wait(*L.scores_t.at(it, 2 * HEADS + 8 * half))
                    for h in range(8):
                        if h % 4 == 0:
                            wait(*L.k2_lo.at(it, 2 * half + h // 4 + 1))
                        nc.gpsimd.tensor_scalar(L.chunk(L.kz, 8 + h), L.chunk(L.big, 4 + h // 2),
                                                const[:, K_HALF + h % 2:K_HALF + h % 2 + 1], None, ALU.mult)\
                            .then_inc(L.key_lo.sem, 1)

                stacked_keys(A, SELF)
                stacked_keys(B, SELF)
                for L in lanes:
                    resize_for_cross(L)
                    stacked_keys(L, CROSS)
                resize_for_latent(A)
                latent_keys_lo(A, 0)
                resize_for_latent(B)
                latent_keys_lo(B, 0)
                latent_keys_lo(A, 1)
                latent_keys_lo(B, 1)
                for L in lanes:
                    wait(*L.pv_done.at(it, 3 * HEADS))

        @block.tensor
        def _(pe):
            mm = nc.tensor.matmul

            pe.wait_ge(const_in.sem, 80)
            pe.wait_ge(onehot_ready.sem, 1)
            for half, table in enumerate((T_COS, T_SIN)):
                for c in range(ST):
                    last = mm(lanes[0].half(0, half), lanes[1].big[:, table + c * P:table + (c + 1) * P],
                              lanes[0].chunk(lanes[0].big, c), start=(c == 0), stop=(c == ST - 1))
            last.then_inc(trig_done.sem, 1)

            with pe.Fori(0, PAIRS) as it:
                pe.wait_ge(trig_ready.sem, 1)

                def memory_projection(L, g):
                    if L.t == 0:
                        pe.wait_ge(weights_in["gm"].sem, it * 32 + 16 * (g + 1))
                    if g == 0:
                        pe.wait_ge(L.inputs_in.sem, it * 32 + 32)
                    else:
                        pe.wait_ge(*L.added.at(it, 5))
                    for c in range(DC):
                        last = mm(L.half(0, c), gm_w[:, GM_MEM + c * P:GM_MEM + (c + 1) * P], L.ctx[:, 0:S],
                                  start=True, stop=True)
                    last.then_inc(L.mem_done.sem, 1)
                    for kt in range(ST):
                        last = mm(L.half(1, kt), L.ctx[:, kt * P:(kt + 1) * P], gm_w[:, GM_MEM:GM_MEM + D],
                                  start=True, stop=True)
                    last.then_inc(L.mem_done.sem, 1)

                def gm_scores(L, g):
                    x = L.xin if g == 0 else L.x
                    pe.wait_ge(*L.mem_saved.at(it, 2 * g + 1))
                    for qt in range(ST):
                        for c in range(DC):
                            last = mm(L.half(2, qt), L.chunk(x, c, qt * P, (qt + 1) * P),
                                      L.chunk(L.big2, c), start=(c == 0), stop=(c == DC - 1))
                    last.then_inc(L.gm_scores.sem, 1)

                def gm_turn(L, g):
                    pe.wait_ge(*L.gm_probs.at(it, g + 1))
                    for kt in range(ST):
                        for qt in range(ST):
                            last = nc.tensor.transpose(L.half(3, kt, qt * P, (qt + 1) * P),
                                                       L.chunk(L.big, qt, kt * P, (kt + 1) * P), ident)
                    last.then_inc(L.gm_turned.sem, 1)

                def gm_context(L, g):
                    pe.wait_ge(*L.mem_saved.at(it, 2 * g + 2))
                    pe.wait_ge(*L.gm_turned_saved.at(it, g + 1))
                    for c in range(DC):
                        for kt in range(ST):
                            last = mm(L.half(0, c), L.chunk(L.big2, 2 + kt, c * P, (c + 1) * P),
                                      L.chunk(L.big, 2 + kt), start=(kt == 0), stop=(kt == ST - 1))
                    last.then_inc(L.gm_context.sem, 1)

                def gm_gate(L, g, c, features):
                    x = L.xin if g == 0 else L.x
                    if features[0] < DC:
                        pe.wait_ge(*L.mem_saved.at(it, 2 * g + 2))
                    if features[-1] >= DC:
                        pe.wait_ge(*L.gm_context_saved.at(it, g + 1))
                    for f in features:
                        src = L.chunk(x, f) if f < DC else L.chunk(L.xv, f - DC)
                        last = mm(L.half(1, c), w(gm_w, GM_GATE, f, c * P, (c + 1) * P, D), src,
                                  start=(f == 0), stop=(f == 2 * DC - 1))
                    return last

                def gm_gate_rest(L, g):
                    gm_gate(L, g, 0, range(DC, 2 * DC))
                    gm_gate(L, g, 1, range(2 * DC)).then_inc(L.gate_done.sem, 1)

                def sum_squares(L, n):
                    pe.wait_ge(*L.sq_ready.at(it, n + 1))
                    mm(L.half(2, 0), ones, L.chunk(L.sq, 0), start=True, stop=True)\
                        .then_inc(L.sumsq_done.sem, 1)

                def layer_norm_sum(L, n):
                    pe.wait_ge(*L.added.at(it, 3 + n))
                    pe.wait_ge(*L.v_saved.at(it, 6))
                    for c in range(DC):
                        last = mm(L.half(3, 0), ones, L.chunk(L.x, c), start=(c == 0), stop=(c == DC - 1))
                    last.then_inc(L.sum_done.sem, 1)

                def product(out, weights, n, width, lo, L):
                    terms = [(i, a, b) for i in range(4) for a, b in ((0, 0), (0, 1), (1, 0))]
                    for t, (i, a, b) in enumerate(terms):
                        at = (n + i) * width + lo
                        last = mm(out, weights(a)[:, at:at + P], L.x_part(i, b), start=(t == 0),
                                  stop=(t == len(terms) - 1))
                    return last

                def self_qkv(L):
                    if L.t == 0:
                        pe.wait_ge(weights_in["l1a"].sem, it * 16 + 16)
                    pe.wait_ge(*L.split_v.at(it, 1))
                    parts = [(A_VQKV, L.xv, c) for c in range(DC)] + [(A_LQKV, L.xl, c) for c in range(DC)]
                    for m in range(4):
                        for i, (at, src, c) in enumerate(parts):
                            if m == 0 and i == DC:
                                pe.wait_ge(*L.split.at(it, 1))
                            last = mm(L.half(m // 2, m % 2), w(attn_w, at, c, m * P, (m + 1) * P, 3 * D),
                                      L.chunk(src, c), start=(i == 0), stop=(i == 3))
                        if m % 2:
                            last.then_inc(L.qk_done.sem, 1)
                        yield
                    for kt in range(ST):
                        for i, (at, src, c) in enumerate(parts):
                            last = mm(L.half(3, kt), L.chunk(src, c, kt * P, (kt + 1) * P),
                                      w(attn_w, at, c, 2 * D, 3 * D, 3 * D), start=(i == 0), stop=(i == 3))
                        if kt == ST - 1:
                            last.then_inc(L.v_done.sem, 1)
                        yield

                def rotate_halves(L):
                    pe.wait_ge(*L.qk_saved.at(it, 2))
                    for m in range(4):
                        last = mm(L.half(m // 2, m % 2), rot, L.chunk(L.big, m), start=True, stop=True)
                    last.then_inc(L.rot_done.sem, 1)

                def stack_queries_and_keys(L, a):
                    n = 1 + (a == CROSS)
                    tiles = HEADS // SHARE[a]
                    pe.wait_ge(*L.hi_ready.at(it, n))
                    pe.wait_ge(*L.lo_ready.at(it, n))
                    if a == SELF:
                        pe.wait_ge(*L.v_saved.at(it, 1))
                    chunks = tiles // 4
                    for what, (hi, lo) in enumerate(((Q_HI, Q_LO), (K_HI, K_LO))):
                        for t in range(tiles):
                            bank = t // 2 if a == SELF else t // 2 + 2 * (1 - what)
                            c, j = what * chunks + t // 4, t % 4
                            if a == CROSS and what == 1 and t == 0:
                                pe.wait_ge(*L.v_saved.at(it, 2))
                            if a == SELF and what == 1 and t % 2 == 0:
                                pe.wait_ge(*L.q_ready.at(it, bank + 1))
                            mm(L.half(bank, t % 2), stack_place(hi, j), L.chunk(L.parts, c),
                               start=True, stop=False)
                            last = mm(L.half(bank, t % 2), stack_place(lo, j),
                                      L.chunk(L.parts, 2 * chunks + c), start=False, stop=True)
                            if t % 2:
                                last.then_inc((L.k_stacked if what else L.q_stacked).sem, 1)

                def query(L, a, h):
                    tile = h % 8 // 2 if a == LATENT else h // SHARE[a]
                    return lambda lo, hi, part=0: L.chunk(L.q, 4 * part + tile, lo, hi)

                def scores_for_max(L, block, h):
                    a, h0, heads = BLOCKS[block]
                    n0 = a * HEADS + h0
                    if h == 0:
                        if a < LATENT:
                            pe.wait_ge(*L.k_saved.at(it, [4, 6][a]))
                        if a == LATENT:
                            pe.wait_ge(*L.q2_lo.at(it, 2 * block - 2))
                            pe.wait_ge(*L.masks_ready.at(it, 1))
                        else:
                            pe.wait_ge(*L.q_ready.at(it, 4 + 2 * (a == CROSS)))
                    pe.wait_ge(*L.key_ready.at(it, n0 + h + 1))
                    if h >= 4:
                        pe.wait_ge(*L.max_ready.at(it, n0 + h - 3))
                    bank, q = h % 4, query(L, a, h)
                    for qt in range(ST):
                        keys = L.chunk(L.kz, h)
                        last = mm(L.half(bank, qt), q(qt * P, (qt + 1) * P), keys,
                                  start=True, stop=(a == CROSS))
                        if a == SELF:
                            last = mm(L.half(bank, qt, qt * P, (qt + 1) * P), identb,
                                      constb[:, KB_CAUSAL:KB_CAUSAL + P], start=False, stop=True)
                        elif a == LATENT:
                            last = mm(L.half(bank, qt), onerow, L.mask_row[:], start=False, stop=True)
                    last.then_inc(L.scores.sem, 1)

                def turn_max(L, block):
                    a, h0, heads = BLOCKS[block]
                    pe.wait_ge(*L.max_split.at(it, block + 1))
                    pe.wait_ge(*L.max_ready.at(it, a * HEADS + h0 + heads))
                    turned = L.ps[0:32, 3, 0:P].bitcast(BF16)
                    for qt in range(ST):
                        last = nc.tensor.transpose(turned[:, qt * P:(qt + 1) * P],
                                                   L.max_parts[:, qt * 32:(qt + 1) * 32], identb)
                    last.then_inc(L.max_turned.sem, 1)

                def attend(L, block):
                    a, h0, heads = BLOCKS[block]
                    n0 = a * HEADS + h0

                    def scores(h):
                        n = n0 + h
                        if h == 0:
                            pe.wait_ge(*L.max_saved.at(it, 2 * block + (2 if a == LATENT else 1)))
                        if a < LATENT and h == 2 * SHARE[a]:
                            pe.wait_ge(*L.max_saved.at(it, 2 * block + 2))
                        if h >= 2:
                            pe.wait_ge(*L.probs_ready.at(it, n - 1))
                        bank, q = h % 2, query(L, a, h)
                        for kt in (1, 0):
                            out = L.half(bank, 1 - kt)
                            keys = L.chunk(L.kz, h, kt * P, (kt + 1) * P)
                            last = mm(out, keys, q(0, S), start=True, stop=(a == CROSS))
                            if a == SELF:
                                last = mm(L.half(bank, 1 - kt, kt * P, (kt + 1) * P), identb,
                                          constb[:, KB_CAUSAL_T:KB_CAUSAL_T + P], start=False, stop=True)
                            elif a == LATENT:
                                if kt == 1:
                                    pe.wait_ge(*L.key_lo.at(it, h0 + h + 1))
                                mm(out, keys, q(0, S, 1), start=False, stop=False)
                                mm(out, L.chunk(L.kz, 8 + h, kt * P, (kt + 1) * P), q(0, S),
                                   start=False, stop=False)
                                last = mm(out, sel(h), L.max_rows[:], start=False, stop=True)
                        last.then_inc(L.scores_t.sem, 1)

                    def weigh(h):
                        n = n0 + h
                        g = (h0 + h) // GROUP[a]
                        if h % GROUP[a] == 0 and (g >= 2):
                            pe.wait_ge(*L.head_out.at(it, GROUP_BASE[a] + g - 1))
                        pe.wait_ge(*L.probs_ready.at(it, n + 1))
                        if h == 0:
                            pe.wait_ge(*L.v_saved.at(it, [1, 2, 6][a]))
                            if a > SELF:
                                pe.wait_ge(*L.v_resized.at(it, a))
                        for kt in range(ST):
                            lo = kt * P if a == SELF else 0
                            at = (h % 2) * 512 + (1 - kt) * S
                            last = mm(L.ps[:, 2 + g % 2, lo:S], L.values(a, h0 + h, kt),
                                      L.probs[:, at + lo:at + S],
                                      start=(h % GROUP[a] == 0 and kt == 0),
                                      stop=(h % GROUP[a] == GROUP[a] - 1 and kt == ST - 1))
                        last.then_inc(L.pv_done.sem, 1)

                    for h in range(heads + 1):
                        if h < heads:
                            scores(h)
                        if h >= 1:
                            weigh(h - 1)
                        yield

                def self_dense(L):
                    pe.wait_ge(*L.split_v.at(it, 2))
                    for m in range(DC):
                        i = 0
                        for at, src in ((A_VDENSE, L.xv), (A_LDENSE, L.xl)):
                            if m == 0 and i == DC:
                                pe.wait_ge(*L.split.at(it, 2))
                            for c in range(DC):
                                last = mm(L.half(0, m), w(attn_w, at, c, m * P, (m + 1) * P, D),
                                          L.chunk(src, c), start=(i == 0), stop=(i == 3))
                                i += 1
                    last.then_inc(L.added_done.sem, 1)

                def cross_qkv(L):
                    pe.wait_ge(*L.normed.at(it, 3))
                    for c in range(DC):
                        mm(L.half(0, 0), w(attn_w, A_CQ, c, 0, P, P), L.chunk(L.xn, c),
                           start=(c == 0), stop=(c == DC - 1))
                    mm(L.half(0, 1), attn_w[:, A_CKV:A_CKV + P], L.ctx[:], start=True, stop=True)\
                        .then_inc(L.cross_done.sem, 1)
                    for kt in range(ST):
                        last = mm(L.ps[:, 1, kt * P:(kt + 1) * P], L.ctx[:, kt * P:(kt + 1) * P],
                                  attn_w[:, A_CKV + P:A_CKV + 2 * P], start=True, stop=True)
                    last.then_inc(L.v_done.sem, 1)

                def cross_dense(L):
                    pe.wait_ge(*L.head_out.at(it, GROUP_BASE[CROSS] + 2))
                    for m in range(DC):
                        last = mm(L.half(0, m), attn_w[:, A_CDENSE + m * P:A_CDENSE + (m + 1) * P],
                                  L.chunk(L.big2, 0), start=True, stop=True)
                    last.then_inc(L.added_done.sem, 1)

                def experts_up(L):
                    pe.wait_ge(*L.x_lo.at(it, 1))
                    for m in range(IC):
                        if m >= 4:
                            pe.wait_ge(*L.hidden.at(it, m - 3))
                        pe.wait_ge(*L.w_lo.at(it, m + 1))
                        for half in range(2):
                            if m < IC - 1 or half == 0:
                                last = product(L.half(m % 4, half), lambda part: L.unit(m, part),
                                               4 * half, P, 0, L)
                            if half == (m < IC - 1):
                                last.then_inc(L.up_done.sem, 1)
                            yield

                def experts_down(L):
                    if L.t == 0:
                        pe.wait_ge(weights_in["l1d"].sem, it * 16 + 16)
                    for m in range(DC):
                        i = 0
                        for k in range(IC):
                            if m == 0:
                                pe.wait_ge(*L.hidden.at(it, max(k + 1, 4)))
                            for at, src in ((M_VDOWN, L.big), (M_LDOWN, L.big2))[:2 if k < IC - 1 else 1]:
                                last = mm(L.half(2 + m, 0), w(down_w, at, k, m * P, (m + 1) * P, D),
                                          L.chunk(src, k), start=(i == 0), stop=(i == 2 * IC - 2))
                                i += 1
                            if m == DC - 1 and k == IC - 1:
                                last.then_inc(L.added_done.sem, 1)
                            yield

                def latent_v(L):
                    if L.t == 0:
                        pe.wait_ge(weights_in["l2q"].sem, it * 16 + 16)
                    pe.wait_ge(*L.added.at(it, 3))
                    for j in range(4):
                        kt, n = j // 2, j % 2
                        mm(L.ps[:, j, :], L.ctx[:, kt * P:(kt + 1) * P],
                           attn_w[:, Q_WKV + INNER + n * 512:Q_WKV + INNER + (n + 1) * 512],
                           start=True, stop=True).then_inc(L.v_done.sem, 1)

                def latent_k(L, half):
                    if half == 0:
                        pe.wait_ge(*L.v_saved.at(it, 4))
                    for m in range(4):
                        last = mm(L.half(m // 2, m % 2),
                                  attn_w[:, Q_WKV + (4 * half + m) * P:Q_WKV + (4 * half + m + 1) * P],
                                  L.ctx[:], start=True, stop=True)
                        if m % 2:
                            last.then_inc(L.k_done.sem, 1)

                def latent_q(L, half):
                    if half == 0:
                        pe.wait_ge(*L.normed.at(it, 5))
                    else:
                        pe.wait_ge(*L.head_out.at(it, GROUP_BASE[LATENT] + 8))
                    for m in range(4):
                        for c in range(DC):
                            last = mm(L.half(2 + m // 2, m % 2),
                                      w(attn_w, Q_WQ, c, (4 * half + m) * P, (4 * half + m + 1) * P, INNER),
                                      L.chunk(L.xn, c), start=(c == 0), stop=(c == DC - 1))
                        if m % 2:
                            last.then_inc(L.q2_done.sem, 1)

                def latent_dense(L):
                    if L.t == 0:
                        pe.wait_ge(weights_in["l2f"].sem, it * 16 + 16)
                    pe.wait_ge(*L.head_out.at(it, GROUP_BASE[LATENT] + HEADS))
                    for m in range(DC):
                        for k in range(NC2):
                            last = mm(L.half(0, m), w(ffn_w, F_WO, k, m * P, (m + 1) * P, D),
                                      L.chunk(L.big2, k), start=(k == 0), stop=(k == NC2 - 1))
                    last.then_inc(L.added_done.sem, 1)

                def ffn_up(L):
                    pe.wait_ge(*L.x_lo.at(it, 2))
                    for m in range(NC2):
                        u, at = IC + m // 4, m % 4 * P
                        if m % 4 == 0:
                            pe.wait_ge(*L.w_lo.at(it, u + 1))
                        terms = [(c, a, b) for c in range(DC) for a, b in ((0, 0), (0, 1), (1, 0))]
                        for t, (c, a, b) in enumerate(terms):
                            last = mm(L.half(m // 2, m % 2), L.unit(u, a)[:, c * 512 + at:c * 512 + at + P],
                                      L.x_part(c, b), start=(t == 0), stop=(t == len(terms) - 1))
                        if m % 2:
                            last.then_inc(L.w1_done.sem, 1)
                            yield

                def ffn_down(L):
                    for m in range(DC):
                        for k in range(NC2):
                            if m == 0 and k % 2 == 0:
                                pe.wait_ge(*L.gelu_ready.at(it, k // 2 + 1))
                            last = mm(L.half(0, m), w(ffn_w, F_W2, k, m * P, (m + 1) * P, D),
                                      L.chunk(L.big, k), start=(k == 0), stop=(k == NC2 - 1))
                            if m == DC - 1 and k == NC2 - 1:
                                last.then_inc(L.added_done.sem, 1)
                            if k % 4 == 3:
                                yield

                def each(stage, *args):
                    for L in lanes:
                        stage(L, *args)

                def gated_memory(g):
                    each(memory_projection, g)
                    each(gm_scores, g)
                    each(gm_gate, g, 0, range(DC))
                    each(gm_turn, g)
                    each(gm_context, g)
                    each(gm_gate_rest, g)

                def to_self(L, name="self"):
                    plan = PLAN[name, L.t]
                    for step in range(plan["end"]):
                        if step == plan.get("rotate"):
                            rotate_halves(L)
                        if step == plan.get("stack"):
                            stack_queries_and_keys(L, SELF)
                        for h in heads_at(plan, step, HEADS):
                            scores_for_max(L, 0, h)
                        if step == plan.get("turn"):
                            turn_max(L, 0)
                        yield

                def to_cross(L):
                    plan = PLAN["cross", L.t]
                    for step in range(plan["end"]):
                        if step == plan["dense"]:
                            self_dense(L)
                        if step == plan["norm"]:
                            sum_squares(L, 2)
                        if step == plan["project"]:
                            cross_qkv(L)
                        if step == plan["stack"]:
                            stack_queries_and_keys(L, CROSS)
                        for h in heads_at(plan, step, HEADS):
                            scores_for_max(L, 1, h)
                        if step == plan["turn"]:
                            turn_max(L, 1)
                        yield

                def to_experts(L):
                    plan = PLAN["experts", L.t]
                    for step in range(plan["end"]):
                        if step == plan["dense"]:
                            cross_dense(L)
                        if step == plan["norm"]:
                            sum_squares(L, 3)
                        yield

                def to_latent(L, half):
                    plan = PLAN["half" if half else "latent", L.t]
                    for step in range(plan["end"]):
                        if half == 0:
                            if step == plan["values"]:
                                latent_v(L)
                            if step == plan["mean"]:
                                layer_norm_sum(L, 0)
                            if step == plan["norm"]:
                                sum_squares(L, 4)
                        if step == plan["project"]:
                            latent_k(L, half)
                            latent_q(L, half)
                        for h in heads_at(plan, step, 8):
                            scores_for_max(L, 2 + half, h)
                        if step == plan["turn"]:
                            turn_max(L, 2 + half)
                        yield

                def to_ffn(L):
                    plan = PLAN["ffn", L.t]
                    for step in range(plan["end"]):
                        if step == plan["dense"]:
                            latent_dense(L)
                        if step == plan["mean"]:
                            layer_norm_sum(L, 1)
                        if step == plan["norm"]:
                            sum_squares(L, 5)
                        yield

                def experts(L):
                    yield from experts_up(L)
                    yield from experts_down(L)

                def feed_forward(L):
                    yield from ffn_up(L)
                    yield from ffn_down(L)

                def first_norm(L):
                    sum_squares(L, 1)
                    yield

                gated_memory(0)
                each(sum_squares, 0)
                sum_squares(A, 1)
                alternate(self_qkv(A), first_norm(B))
                alternate(chain(self_qkv(B), to_self(B, "early")), to_self(A))
                alternate(attend(A, 0), to_self(B))
                alternate(attend(B, 0), to_cross(A))
                alternate(attend(A, 1), to_cross(B))
                alternate(attend(B, 1), to_experts(A))
                alternate(experts(A), to_experts(B))
                alternate(experts(B), to_latent(A, 0))
                alternate(attend(A, 2), to_latent(B, 0))
                alternate(attend(B, 2), to_latent(A, 1))
                alternate(attend(A, 3), to_latent(B, 1))
                alternate(attend(B, 3), to_ffn(A))
                alternate(feed_forward(A), to_ffn(B))
                alone(feed_forward(B))
                gated_memory(1)
                each(sum_squares, 6)

        @block.scalar
        def _(act):
            fn = nc.scalar.activation
            act.dma_start(vec[:], vec_d).then_inc(const_in.sem, 16)
            act.dma_start(constb[:], constb_d.bitcast(BF16)).then_inc(const_in.sem, 16)
            act.wait_ge(const_in.sem, 80)
            fn(tanh_gates[:], vec[:, VEC_GATES:VEC_GATES + 2], ACT.Tanh).then_inc(tanh_ready.sem, 1)
            act.wait_ge(trig_done.sem, 1)
            fn(cos[:], lanes[0].half(0, 0), ACT.Copy)
            fn(place[:], lanes[1].big[:, T_PLACE:T_END], ACT.Copy)
            fn(sin[:], lanes[0].half(0, 1), ACT.Copy).then_inc(trig_ready.sem, 1)

            with act.Fori(0, PAIRS) as it:
                step = Steps(act, act_step, it)
                nc.scalar.preload_act_table_set("natural_log_exp_and_others")

                def table(name):
                    nc.scalar.preload_act_table_set(name)

                def memory_save(L, g):
                    for j in range(2):
                        act.wait_ge(*L.mem_done.at(it, 2 * g + j + 1))
                        fn(L.big2[:, j * 512:(j + 1) * 512], L.ps[:, j, :], ACT.Copy)\
                            .then_inc(L.mem_saved.sem, 1)

                def gm_exp(L, g):
                    act.wait_ge(*L.gm_max.at(it, g + 1))
                    for qt in range(ST):
                        fn(L.chunk(L.big, qt), L.half(2, qt), ACT.Exp, bias=L.stat[:, 2 + qt:3 + qt],
                           scale=D ** -0.5, accum_out=L.stat[:, 4 + qt:5 + qt]).then_inc(L.gm_exp.sem, 1)

                def gm_context_save(L, g):
                    act.wait_ge(*L.gm_context.at(it, g + 1))
                    fn(L.xv[:], L.ps[:, 0, :], ACT.Copy).then_inc(L.gm_context_saved.sem, 1)

                def gm_sigmoid(L, g):
                    bg = VEC[["L0_xattn_b_gate", "L3_xattn_b_gate"][g]]
                    act.wait_ge(*L.gate_done.at(it, g + 1))
                    for c in range(DC):
                        last = fn(L.chunk(L.xl, c), L.half(1, c), ACT.Sigmoid, bias=vec[:, bg + c:bg + c + 1])
                    last.then_inc(L.gate_saved.sem, 1)

                def rstd(L, n):
                    eps = const[:, K_EPS + (n in (4, 5)):K_EPS + (n in (4, 5)) + 1]
                    if (n, L.t) in ((3, 1), (4, 0), (5, 1)):
                        table("natural_log_exp_and_others")
                    act.wait_ge(*L.sumsq_done.at(it, n + 1))
                    step.done(fn(L.rstd[:], L.half(2, 0), ACT.Ln, bias=eps, scale=1.0 / D))
                    fn(L.rstd[:], L.rstd[:], ACT.Exp, scale=-0.5).then_inc(L.rstd_ready.sem, 1)

                def x_hi(L):
                    act.wait_ge(*L.split.at(it, 3))
                    fn(L.q[:, 0:512], L.xv[:], ACT.Copy)
                    fn(L.q[:, 512:1024], L.xl[:], ACT.Copy).then_inc(L.x_hi.sem, 1)

                def xn_hi(L):
                    act.wait_ge(*L.normed.at(it, 6))
                    fn(L.q[:, 0:512], L.xn[:], ACT.Copy).then_inc(L.x_hi.sem, 1)

                def w1_hi(L, u):
                    act.wait_ge(weights_in["l2f"].sem, it * 16 + 16)
                    act.wait_ge(*L.scores_t.at(it, 3 * HEADS))
                    fn(L.unit(IC + u, 0).rearrange("p (n i) -> p n i", i=512), w1_unit(u), ACT.Copy)\
                        .then_inc(L.w_hi.sem, 1)

                def up_hi(L, m):
                    act.wait_ge(weights_in["l1m"].sem, it * 16 + 16)
                    if m >= 2:
                        act.wait_ge(*L.up_done.at(it, m - 1))
                    n = 8 if m < IC - 1 else 4
                    fn(L.unit(m, 0)[:, 0:n * P].rearrange("p (n i) -> p n i", i=P), up_unit(m), ACT.Copy)\
                        .then_inc(L.w_hi.sem, 1)

                def qk_save(L):
                    for j in range(2):
                        yield
                        act.wait_ge(*L.qk_done.at(it, j + 1))
                        fn(L.big[:, j * 512:(j + 1) * 512], L.ps[:, j, :], ACT.Copy)\
                            .then_inc(L.qk_saved.sem, 1)
                        yield
                    yield
                    yield

                def self_hi(L):
                    act.wait_ge(*L.rotated.at(it, 1))
                    fn(L.parts[:, 0:1024], L.big[:, 1024:2048], ACT.Copy).then_inc(L.hi_ready.sem, 1)

                def cross_hi(L):
                    act.wait_ge(*L.cross_done.at(it, 1))
                    act.wait_ge(*L.scores_t.at(it, HEADS))
                    fn(L.parts[:, 0:512], L.ps[:, 0, :], ACT.Copy).then_inc(L.hi_ready.sem, 1)

                def stacked_queries(L, a):
                    n = 0 if a == SELF else 4
                    if a == CROSS:
                        act.wait_ge(*L.scores_t.at(it, HEADS))
                    for j in range(HEADS // SHARE[a] // 2):
                        act.wait_ge(*L.q_stacked.at(it, n + j + 1))
                        fn(L.q[:, j * 512:(j + 1) * 512], L.ps[:, j + (2 if a == CROSS else 0), :], ACT.Copy)\
                            .then_inc(L.q_ready.sem, 1)

                def stacked_keys(L, a):
                    n = 0 if a == SELF else 4
                    for j in range(HEADS // SHARE[a] // 2):
                        act.wait_ge(*L.k_stacked.at(it, n + j + 1))
                        fn(L.big[:, j * 512:(j + 1) * 512], L.ps[:, j, :], ACT.Copy)\
                            .then_inc(L.k_saved.sem, 1)

                def latent_k_hi(L, half):
                    for j in range(2):
                        act.wait_ge(*L.k_done.at(it, 2 * half + j + 1))
                        if half:
                            act.wait_ge(*L.key_ready.at(it, 40))
                            act.wait_ge(*L.key_lo.at(it, 8))
                        fn(L.big[:, j * 512:(j + 1) * 512].bitcast(F32R), L.ps[:, j, :], ACT.Copy)\
                            .then_inc(L.k_saved.sem, 1)

                def latent_v_save(L):
                    for j in range(4):
                        kt, n = j // 2, j % 2
                        act.wait_ge(*L.v_done.at(it, 3 + j))
                        act.wait_ge(*L.v_resized.at(it, 2))
                        fn(L.slots(kt, 0, 64)[:, n * 8:n * 8 + 8, :],
                           L.ps[:, j, :].rearrange("p (h d) -> p h d", h=8), ACT.Copy)\
                            .then_inc(L.v_saved.sem, 1)

                def latent_q_hi(L, half):
                    if half == 0:
                        act.wait_ge(*L.scores_t.at(it, 2 * HEADS))
                    for j in range(2):
                        act.wait_ge(*L.q2_done.at(it, 2 * half + j + 1))
                        fn(L.q[:, j * 512:(j + 1) * 512], L.ps[:, 2 + j, :], ACT.Copy)\
                            .then_inc(L.q2_saved.sem, 1)

                def max_save(L, block):
                    a = BLOCKS[block][0]
                    act.wait_ge(*L.max_turned.at(it, block + 1))
                    turned = L.ps[0:32, 3, 0:P].bitcast(BF16)
                    if a == LATENT:
                        act.wait_ge(*L.rows_cleared.at(it, 1))
                        fn(L.max_rows[0:32, :], turned, ACT.Copy).then_inc(L.max_saved.sem, 2)
                    else:
                        for lo, hi in ((0, 2), (2, HEADS // SHARE[a])):
                            fn(L.q[96:P, lo * S:hi * S].rearrange("p (t s) -> p t s", s=S),
                               turned.unsqueeze(1).to_broadcast([32, hi - lo, S]), ACT.Copy)\
                                .then_inc(L.max_saved.sem, 1)

                def probabilities(L, block):
                    a, h0, heads = BLOCKS[block]

                    def exps(h):
                        n = a * HEADS + h0 + h
                        act.wait_ge(*L.scores_t.at(it, n + 1))
                        if h >= 2:
                            act.wait_ge(*L.pv_done.at(it, n - 1))
                        dst = L.probs[:, (h % 2) * 512:(h % 2 + 1) * 512]
                        if a == LATENT:
                            for kt in range(ST):
                                last = fn(dst[:, (1 - kt) * S:(2 - kt) * S], L.half(h % 2, 1 - kt), ACT.Exp,
                                          bias=L.key_bias[:, kt:kt + 1], scale=SCALE[a])
                        else:
                            lo = P if a == SELF else 0
                            last = fn(dst[:, lo:512], L.ps[:, h % 2, lo:512], ACT.Exp, scale=SCALE[a])
                        last.then_inc(L.probs_ready.sem, 1)

                    def reciprocals(g):
                        r = L.recip[0:64, (g % 2) * S:(g % 2 + 1) * S]
                        act.wait_ge(*L.pv_done.at(it, a * HEADS + (g + 1) * GROUP[a]))
                        if g >= 2:
                            act.wait_ge(*L.head_out.at(it, GROUP_BASE[a] + g - 1))
                        step.done(fn(r, L.ps[64:P, 2 + g % 2, 0:S], ACT.Ln))
                        fn(r, r, ACT.Exp, scale=-1.0).then_inc(L.recip_ready.sem, 1)

                    for h in range(heads + 1):
                        if h < heads:
                            exps(h)
                        if h >= 1 and h % GROUP[a] == 0:
                            reciprocals((h0 + h) // GROUP[a] - 1)
                        yield

                def silu(L):
                    for m in range(IC):
                        yield
                        if m + 2 < IC:
                            up_hi(L, m + 2)
                        act.wait_ge(*L.up_done.at(it, m + 1))
                        if m >= 2:
                            act.wait_ge(*L.hidden.at(it, m - 1))
                        rows = P if m < IC - 1 else 64
                        fn(L.probs[0:rows, (m % 2) * 512:(m % 2) * 512 + S], L.half(m % 4, 0)[0:rows],
                           ACT.Silu).then_inc(L.silu_ready.sem, 1)
                        yield

                def gelu(L):
                    for j in range(4):
                        act.wait_ge(*L.w1_done.at(it, j + 1))
                        fn(L.big[:, j * 512:(j + 1) * 512], L.ps[:, j, :], ACT.Gelu)\
                            .then_inc(L.gelu_ready.sem, 1)
                        yield

                def each(stage, *args):
                    for L in lanes:
                        stage(L, *args)

                def gated_memory(g):
                    each(memory_save, g)
                    each(gm_exp, g)
                    each(gm_context_save, g)
                    table("sigmoid_and_others")
                    each(gm_sigmoid, g)
                    table("natural_log_exp_and_others")

                def to_self(L, name="self"):
                    plan = PLAN[name, L.t]
                    for step in range(plan["end"]):
                        if step == plan.get("split"):
                            self_hi(L)
                        if step == plan.get("stack"):
                            stacked_queries(L, SELF)
                            stacked_keys(L, SELF)
                        if step == plan.get("turn"):
                            max_save(L, 0)
                        yield

                def to_cross(L):
                    plan = PLAN["cross", L.t]
                    for step in range(plan["end"]):
                        if step == plan["norm"]:
                            rstd(L, 2)
                        if step == plan["project"]:
                            cross_hi(L)
                        if step == plan["stack"]:
                            stacked_queries(L, CROSS)
                            stacked_keys(L, CROSS)
                        if step == plan["turn"]:
                            max_save(L, 1)
                        yield

                def to_experts(L):
                    plan = PLAN["experts", L.t]
                    for step in range(plan["end"]):
                        if step in plan["weights"]:
                            up_hi(L, plan["weights"].index(step))
                        if step == plan["norm"]:
                            rstd(L, 3)
                        if step == plan["parts"]:
                            x_hi(L)
                        yield

                def to_latent(L, half):
                    plan = PLAN["half" if half else "latent", L.t]
                    for step in range(plan["end"]):
                        if half == 0:
                            if step == plan["values"]:
                                latent_v_save(L)
                            if step == plan["norm"]:
                                rstd(L, 4)
                        if step == plan["project"]:
                            latent_k_hi(L, half)
                            latent_q_hi(L, half)
                        if step == plan["turn"]:
                            max_save(L, 2 + half)
                        yield

                def to_ffn(L):
                    plan = PLAN["ffn", L.t]
                    for step in range(plan["end"]):
                        if step == plan["norm"]:
                            rstd(L, 5)
                        if step == plan["parts"]:
                            xn_hi(L)
                        if step in plan["weights"]:
                            w1_hi(L, plan["weights"].index(step))
                        yield

                def experts(L):
                    yield from silu(L)
                    for _ in range(2 * IC):
                        yield

                def feed_forward(L):
                    yield from gelu(L)
                    for _ in range(4):
                        yield

                def first_norm(L):
                    rstd(L, 1)
                    yield

                gated_memory(0)
                each(rstd, 0)
                alone(first_norm(A))
                alternate(qk_save(A), first_norm(B))
                alternate(chain(qk_save(B), to_self(B, "early")), to_self(A))
                alternate(probabilities(A, 0), to_self(B))
                alternate(probabilities(B, 0), to_cross(A))
                alternate(probabilities(A, 1), to_cross(B))
                alternate(probabilities(B, 1), to_experts(A))
                alternate(experts(A), to_experts(B))
                alternate(experts(B), to_latent(A, 0))
                table("natural_log_exp_and_others")
                alternate(probabilities(A, 2), to_latent(B, 0))
                alternate(probabilities(B, 2), to_latent(A, 1))
                alternate(probabilities(A, 3), to_latent(B, 1))
                alternate(probabilities(B, 3), to_ffn(A))
                alternate(feed_forward(A), to_ffn(B))
                alone(feed_forward(B))
                table("natural_log_exp_and_others")
                gated_memory(1)
                each(rstd, 6)
                for L in lanes:
                    act.wait_ge(*L.normed.at(it, 7))
                    n = it * LANES + L.t
                    act.dma_start(out_d[bass.ds(n, 1)].rearrange("a p n -> (a p) n"), L.xn[:])\
                        .then_inc(L.out_in_dram.sem, 16)
                assert step.n == act_step.per_pass, step.n

        @block.vector
        def _(dve):
            tt = nc.vector.tensor_tensor
            ts = nc.vector.tensor_scalar
            stt = nc.vector.scalar_tensor_tensor

            dve.wait_ge(const_in.sem, 80)
            for c in range(ST):
                last = ts(lanes[0].chunk(lanes[0].big, c), pos_i[:], const[:, K_IOTA:K_IOTA + 1], float(c * P),
                          ALU.subtract, ALU.is_equal)
            last.then_inc(onehot_ready.sem, 1)

            def lines(tile, n, cols=S):
                return tile.rearrange("p (n s) -> p n s", s=cols)

            def spread(row, n):
                return row.unsqueeze(1).to_broadcast([P, n, S])

            with dve.Fori(0, PAIRS) as it:
                step = Steps(dve, vec_step, it)

                def masks(L):
                    dve.wait_ge(L.inputs_in.sem, it * 32 + 32)
                    dve.wait_ge(L.masks_in.sem, it * 48 + 48)
                    step.done(ts(L.sq[:, 0:S], L.expert_i[:], 1.0, None, ALU.is_equal))
                    tt(L.is_v[:, 0:S - 1], L.sq[:, 0:S - 1], L.sq[:, 1:S], ALU.mult)
                    nc.vector.memset(L.is_v[:, S - 1:S], 0.0)
                    ts(L.key_bias[:], L.keep_col[:], 0.0, -BIG * SCALE[LATENT], ALU.is_equal, ALU.mult)
                    dve.wait_ge(*L.rows_cleared.at(it, 1))
                    ins = ts(L.mask_row[0:1, :], L.keep_row[0:1, :], 0.0, -BIG, ALU.is_equal, ALU.mult)
                    ins.then_inc(L.masks_ready.sem, 1)
                    dve.wait_ge(*L.masks_ready.at(it, 1))

                def gm_max(L, g):
                    dve.wait_ge(*L.gm_scores.at(it, g + 1))
                    step.done(nc.vector.tensor_reduce(L.stat[:, 0:2], L.ps[:, 2, :].rearrange(
                        "p (q k) -> p q k", q=ST), AX.X, ALU.max))
                    ts(L.stat[:, 2:4], L.stat[:, 0:2], -D ** -0.5, None, ALU.mult).then_inc(L.gm_max.sem, 1)

                def gm_normalise(L, g):
                    dve.wait_ge(*L.gm_exp.at(it, 2 * g + 2))
                    step.done(nc.vector.reciprocal(L.stat[:, 6:8], L.stat[:, 4:6]))
                    for qt in range(ST):
                        last = ts(L.chunk(L.big, qt), L.chunk(L.big, qt), L.stat[:, 6 + qt:7 + qt], None, ALU.mult)
                    last.then_inc(L.gm_probs.sem, 1)

                def gm_turned_save(L, g):
                    dve.wait_ge(*L.gm_turned.at(it, g + 1))
                    nc.vector.tensor_copy(L.big[:, 512:1024], L.ps[:, 3, :]).then_inc(L.gm_turned_saved.sem, 1)

                def gm_fuse(L, g):
                    x = L.xin if g == 0 else L.x
                    dve.wait_ge(*L.gate_saved.at(it, g + 1))
                    step.done(tt(L.xl[:], L.xl[:], L.xv[:], ALU.mult))
                    step.done(tt(L.xl[:], L.xl[:], x[:], ALU.add))

                def square(L, src):
                    step.done(tt(L.sq[:], src[:], src[:], ALU.mult))
                    tt(L.chunk(L.sq, 0), L.chunk(L.sq, 0), L.chunk(L.sq, 1), ALU.add).then_inc(L.sq_ready.sem, 1)

                def normalise(L, n, src, dst, weight, bias=None):
                    at = VEC[weight]
                    dve.wait_ge(*L.rstd_ready.at(it, n + 1))
                    for c in range(DC):
                        last = stt(out=L.chunk(dst, c), in0=L.chunk(src, c), scalar=vec[:, at + c:at + c + 1],
                                   in1=L.rstd[:], op0=ALU.mult, op1=ALU.mult)
                    if bias:
                        step.done(last)
                        at = VEC[bias]
                        for c in range(DC):
                            last = ts(L.chunk(dst, c), L.chunk(dst, c), vec[:, at + c:at + c + 1], None, ALU.add)
                    last.then_inc(L.normed.sem, 1)
                    dve.wait_ge(*L.normed.at(it, n + 1))

                def split(L, n, src):
                    tt(lines(L.xv[:], DC), lines(src, DC), spread(L.is_v[:], DC), ALU.mult)\
                        .then_inc(L.split_v.sem, 1)
                    dve.wait_ge(*L.split_v.at(it, n))
                    tt(L.xl[:], src, L.xv[:], ALU.subtract).then_inc(L.split.sem, 1)

                def x_lo(L):
                    dve.wait_ge(*L.x_hi.at(it, 1))
                    tt(L.q[:, 1024:1536], L.xv[:], L.q[:, 0:512].bitcast(F32), ALU.subtract)
                    tt(L.q[:, 1536:2048], L.xl[:], L.q[:, 512:1024].bitcast(F32), ALU.subtract)\
                        .then_inc(L.x_lo.sem, 1)

                def xn_lo(L):
                    dve.wait_ge(*L.x_hi.at(it, 2))
                    tt(L.q[:, 1024:1536], L.xn[:], L.q[:, 0:512].bitcast(F32), ALU.subtract)\
                        .then_inc(L.x_lo.sem, 1)

                def w1_lo(L, u):
                    dve.wait_ge(*L.w_hi.at(it, IC + u + 1))
                    hi, lo = (L.unit(IC + u, part).rearrange("p (n i) -> p n i", i=512) for part in range(2))
                    tt(lo, w1_unit(u), hi.bitcast(F32), ALU.subtract).then_inc(L.w_lo.sem, 1)

                def up_lo(L, m):
                    dve.wait_ge(*L.w_hi.at(it, m + 1))
                    n = 8 if m < IC - 1 else 4
                    hi, lo = (L.unit(m, part)[:, 0:n * P].rearrange("p (n i) -> p n i", i=P)
                              for part in range(2))
                    tt(lo, up_unit(m), hi.bitcast(F32), ALU.subtract).then_inc(L.w_lo.sem, 1)

                def self_values(L):
                    dve.wait_ge(*L.v_done.at(it, 1))
                    dve.wait_ge(*L.v_cleared.at(it, 2))
                    for kt in range(ST):
                        last = nc.vector.tensor_copy(L.slots(kt, 0, HEAD_DIM[SELF]), L.half(3, kt).rearrange(
                            "p (h d) -> p h d", h=HEADS))
                    last.then_inc(L.v_saved.sem, 1)

                def rotate(L):
                    dve.wait_ge(*L.qk_saved.at(it, 2))
                    tt(lines(L.big2[:, 0:1024], 4), lines(L.big[:, 0:1024], 4), spread(cos[:], 4), ALU.mult)
                    dve.wait_ge(*L.rot_done.at(it, 1))
                    step.done(tt(lines(L.big2[:, 1024:2048], 4),
                                 L.ps[:, 0:2, :].rearrange("p b (n s) -> p (b n) s", s=S), spread(sin[:], 4),
                                 ALU.mult))
                    last = tt(L.big[:, 1024:2048], L.big2[:, 0:1024], L.big2[:, 1024:2048], ALU.add)
                    last.then_inc(L.rotated.sem, 1)
                    dve.wait_ge(*L.rotated.at(it, 1))

                def self_lo(L):
                    dve.wait_ge(*L.hi_ready.at(it, 1))
                    tt(L.parts[:, 1024:2048], L.big[:, 1024:2048], L.parts[:, 0:1024].bitcast(F32),
                       ALU.subtract).then_inc(L.lo_ready.sem, 1)

                def cross_lo(L):
                    dve.wait_ge(*L.hi_ready.at(it, 2))
                    tt(L.parts[:, 512:1024], L.ps[:, 0, :], L.parts[:, 0:512].bitcast(F32),
                       ALU.subtract).then_inc(L.lo_ready.sem, 1)

                def latent_keys_hi(L, half):
                    dve.wait_ge(*L.scores_t.at(it, 2 * HEADS + 8 * half))
                    for h in range(8):
                        if h % 4 == 0:
                            dve.wait_ge(*L.k_saved.at(it, 6 + 2 * half + h // 4 + 1))
                        ts(L.chunk(L.kz, h), L.chunk(L.big, h // 2), const[:, K_HALF + h % 2:K_HALF + h % 2 + 1],
                           None, ALU.mult).then_inc(L.key_ready.sem, 1)

                def latent_k_lo(L, half):
                    for j in range(2):
                        dve.wait_ge(*L.k_saved.at(it, 6 + 2 * half + j + 1))
                        tt(L.big[:, 1024 + j * 512:1024 + (j + 1) * 512], L.ps[:, j, :],
                           L.big[:, j * 512:(j + 1) * 512], ALU.subtract).then_inc(L.k2_lo.sem, 1)

                def latent_q_lo(L, half):
                    for j in range(2):
                        dve.wait_ge(*L.q2_saved.at(it, 2 * half + j + 1))
                        tt(L.q[:, 1024 + j * 512:1024 + (j + 1) * 512], L.ps[:, 2 + j, :],
                           L.q[:, j * 512:(j + 1) * 512].bitcast(F32), ALU.subtract).then_inc(L.q2_lo.sem, 1)

                def cross_values(L):
                    dve.wait_ge(*L.v_done.at(it, 2))
                    dve.wait_ge(*L.pv_done.at(it, HEADS))
                    for kt in range(ST):
                        last = nc.vector.tensor_copy(
                            L.slots(kt, 0, HEAD_DIM[CROSS]),
                            L.ps[:, 1, kt * P:(kt + 1) * P].rearrange("p (h d) -> p h d", h=HEADS))
                    last.then_inc(L.v_saved.sem, 1)

                def maxima(L, block, h):
                    a, h0, heads = BLOCKS[block]
                    mx = L.max[:, 0:ST * heads].rearrange("p (q h) -> p q h", q=ST)
                    dve.wait_ge(*L.scores.at(it, a * HEADS + h0 + h + 1))
                    if a == SELF:
                        nc.vector.tensor_reduce(mx[:, 0:1, h], L.ps[:, h % 4, 0:P], AX.X, ALU.max)
                        last = nc.vector.tensor_reduce(mx[:, 1:2, h], L.ps[:, h % 4, S:2 * S], AX.X, ALU.max)
                    else:
                        last = nc.vector.tensor_reduce(mx[:, :, h], L.ps[:, h % 4, :].rearrange(
                            "p (q k) -> p q k", q=ST), AX.X, ALU.max)
                    last.then_inc(L.max_ready.sem, 1)
                    if h < heads - 1:
                        return
                    dve.wait_ge(*L.max_ready.at(it, a * HEADS + h0 + heads))
                    parts = L.max_parts[:].rearrange("p (q r) -> p q r", q=ST)[:, :, 0:2 * heads]\
                        .rearrange("p q (n h) -> p q n h", n=2)
                    step.done(nc.vector.tensor_copy(parts[:, :, 0, :], mx))
                    tt(parts[:, :, 1, :], mx, parts[:, :, 0, :], ALU.subtract).then_inc(L.max_split.sem, 1)

                def head_outputs(L, block):
                    a, h0, heads = BLOCKS[block]
                    for h in range(heads + 1):
                        if h >= 1 and h % GROUP[a] == 0:
                            g = (h0 + h) // GROUP[a] - 1
                            dve.wait_ge(*L.recip_ready.at(it, GROUP_BASE[a] + g + 1))
                            lo = 64 * (g % 2)
                            tt(L.big2[lo:lo + 64, (g // 2) * S:(g // 2 + 1) * S], L.ps[0:64, 2 + g % 2, 0:S],
                               L.recip[0:64, (g % 2) * S:(g % 2 + 1) * S], ALU.mult).then_inc(L.head_out.sem, 1)
                        yield

                def split_context(L):
                    dve.wait_ge(*L.head_out.at(it, 4))
                    split(L, 2, L.big2[:, 0:512])

                def add(L, n):
                    dve.wait_ge(*L.added_done.at(it, n + 1))
                    src = L.ps[:, 2:4, 0:S] if n == 2 else L.ps[:, 0, :].rearrange("p (c s) -> p c s", s=S)
                    x = L.x[:].rearrange("p (c s) -> p c s", s=S)
                    if n < 3:
                        last = tt(x, src, x, ALU.add)
                    else:
                        if n == 3:
                            dve.wait_ge(tanh_ready.sem, 1)
                        last = stt(out=x, in0=src, scalar=tanh_gates[:, n - 3:n - 2], in1=x,
                                   op0=ALU.mult, op1=ALU.add)
                    last.then_inc(L.added.sem, 1)
                    dve.wait_ge(*L.added.at(it, n + 1))

                def hidden(L):
                    for _ in range(2):
                        yield
                    for m in range(IC):
                        if m + 2 < IC:
                            up_lo(L, m + 2)
                        dve.wait_ge(*L.silu_ready.at(it, m + 1))
                        s = L.probs[:, (m % 2) * 512:(m % 2) * 512 + S]
                        h = L.probs[:, (m % 2) * 512 + S:(m % 2) * 512 + 2 * S]
                        if m < IC - 1:
                            step.done(tt(h, L.half(m % 4, 1), s, ALU.mult))
                            step.done(tt(L.chunk(L.big, m), h, L.is_v[:], ALU.mult))
                            last = tt(L.chunk(L.big2, m), h, L.chunk(L.big, m), ALU.subtract)
                        else:
                            v, l = (L.chunk(L.big, m)[64 * i:64 * i + 64] for i in range(2))
                            step.done(tt(h[0:64], L.half(m % 4, 0)[64:P], s[0:64], ALU.mult))
                            step.done(tt(v, h[0:64], L.is_v[0:64], ALU.mult))
                            last = tt(l, h[0:64], v, ALU.subtract)
                        last.then_inc(L.hidden.sem, 1)
                        yield
                        yield

                def centre(L, n):
                    dve.wait_ge(*L.sum_done.at(it, n + 1))
                    for c in range(DC):
                        last = stt(out=L.chunk(L.xl, c), in0=L.half(3, 0), scalar=-1.0 / D, in1=L.chunk(L.x, c),
                                   op0=ALU.mult, op1=ALU.add)
                    step.done(last)
                    square(L, L.xl)

                def each(stage, *args):
                    for L in lanes:
                        stage(L, *args)

                def gated_memory(g):
                    each(gm_max, g)
                    each(gm_normalise, g)
                    each(gm_turned_save, g)
                    if g == 0:
                        each(masks)
                    for L in lanes:
                        gm_fuse(L, g)
                        square(L, L.xl)

                gated_memory(0)
                for L in lanes:
                    if L.t == 0:
                        dve.wait_ge(trig_ready.sem, 1)
                    normalise(L, 0, L.xl, L.x, "L0_xattn_norm_w")
                    square(L, L.x)

                def first_norm(L):
                    dve.wait_ge(L.out_in_dram.sem, it * 16 + 16)
                    normalise(L, 1, L.x, L.xn, "L1_xattn_ln_in_w")
                    split(L, 1, L.xn[:])
                    yield

                def values_of_self(L):
                    for _ in range(6):
                        yield

                def to_self(L, name="self"):
                    plan = PLAN[name, L.t]
                    for turn in range(plan["end"]):
                        if turn == plan.get("rotate"):
                            self_values(L)
                            rotate(L)
                        if turn == plan.get("split"):
                            self_lo(L)
                        for h in heads_at(plan, turn, HEADS):
                            maxima(L, 0, h)
                        yield

                def to_cross(L):
                    plan = PLAN["cross", L.t]
                    for turn in range(plan["end"]):
                        if turn == plan["dense"]:
                            split_context(L)
                            add(L, 0)
                            square(L, L.x)
                        if turn == plan["norm"]:
                            normalise(L, 2, L.x, L.xn, "L1_xattn_ln_post_cross_w")
                        if turn == plan["project"]:
                            cross_lo(L)
                            cross_values(L)
                        for h in heads_at(plan, turn, HEADS):
                            maxima(L, 1, h)
                        yield

                def to_experts(L):
                    plan = PLAN["experts", L.t]
                    for turn in range(plan["end"]):
                        if turn == plan["dense"]:
                            add(L, 1)
                            square(L, L.x)
                        if turn in plan["weights"]:
                            up_lo(L, plan["weights"].index(turn))
                        if turn == plan["norm"]:
                            normalise(L, 3, L.x, L.xn, "L1_xattn_ln_post_attn_w")
                            split(L, 3, L.xn[:])
                        if turn == plan["parts"]:
                            x_lo(L)
                        yield

                def to_latent(L, half):
                    plan = PLAN["half" if half else "latent", L.t]
                    for turn in range(plan["end"]):
                        if half == 0:
                            if turn == plan["values"]:
                                add(L, 2)
                            if turn == plan["mean"]:
                                centre(L, 0)
                            if turn == plan["norm"]:
                                normalise(L, 4, L.xl, L.xn, "L2_xattn_ln_q_g", "L2_xattn_ln_q_b")
                        if turn == plan["project"]:
                            latent_k_lo(L, half)
                            latent_keys_hi(L, half)
                            latent_q_lo(L, half)
                        for h in heads_at(plan, turn, 8):
                            maxima(L, 2 + half, h)
                        yield

                def to_ffn(L):
                    plan = PLAN["ffn", L.t]
                    for turn in range(plan["end"]):
                        if turn == plan["dense"]:
                            add(L, 3)
                        if turn == plan["mean"]:
                            centre(L, 1)
                        if turn == plan["norm"]:
                            normalise(L, 5, L.xl, L.xn, "L2_xattn_ln_ff_g", "L2_xattn_ln_ff_b")
                        if turn == plan["parts"]:
                            xn_lo(L)
                        if turn in plan["weights"]:
                            w1_lo(L, plan["weights"].index(turn))
                        yield

                def experts(L):
                    yield from hidden(L)
                    for _ in range(2 * IC - 2):
                        yield

                def feed_forward(L):
                    for _ in range(8):
                        yield
                    add(L, 4)

                alone(first_norm(A))
                alternate(values_of_self(A), first_norm(B))
                alternate(chain(values_of_self(B), to_self(B, "early")), to_self(A))
                alternate(head_outputs(A, 0), to_self(B))
                alternate(head_outputs(B, 0), to_cross(A))
                alternate(head_outputs(A, 1), to_cross(B))
                alternate(head_outputs(B, 1), to_experts(A))
                alternate(experts(A), to_experts(B))
                alternate(experts(B), to_latent(A, 0))
                alternate(head_outputs(A, 2), to_latent(B, 0))
                alternate(head_outputs(B, 2), to_latent(A, 1))
                alternate(head_outputs(A, 3), to_latent(B, 1))
                alternate(head_outputs(B, 3), to_ffn(A))
                alternate(feed_forward(A), to_ffn(B))
                alone(feed_forward(B))
                gated_memory(1)
                for L in lanes:
                    normalise(L, 6, L.xl, L.xn, "L3_xattn_norm_w")
                assert step.n == vec_step.per_pass, step.n


def tables():
    f = np.float32
    dim = HEAD_DIM[SELF]
    inv = (f(1.0) / np.power(f(10000.0), np.arange(0, dim, 2, dtype=f) / f(dim))).astype(f)
    freqs = np.outer(np.arange(S, dtype=f), inv).astype(f)
    emb = np.concatenate([freqs, freqs], axis=-1)
    rows = np.arange(P)
    const = np.zeros((P, K_END), f)
    const[:, K_IDENT:K_IDENT + P] = np.eye(P)
    const[:, K_ONES:K_ONES + P] = 1.0
    for r in range(P):
        j = r % dim
        const[r + dim // 2 if j < dim // 2 else r - dim // 2, K_ROT + r] = -1.0 if j < dim // 2 else 1.0
    trig = np.zeros((P, T_END), f)
    for at, table in ((T_COS, np.cos(emb)), (T_SIN, np.sin(emb))):
        spread = table[:, rows % dim]
        for c in range(ST):
            trig[:, at + c * P:at + (c + 1) * P] = spread[c * P:(c + 1) * P]
    used = rows[:96]
    const[used, K_OWN16 + used % 32 // 16] = 1.0
    const[used, K_OWN8 + used % 32 // 8] = 1.0
    for h in range(HEADS):
        const[96 + h, K_SEL + h] = const[112 + h, K_SEL + h] = -1.0
    const[rows, K_HALF + rows // 64] = 1.0
    const[:, K_IOTA] = rows
    const[:, K_EPS] = 1e-6
    const[:, K_EPS + 1] = 1e-5
    b = np.zeros((P, KB_END), f)
    b[:, KB_IDENT:KB_IDENT + P] = np.eye(P)
    for j in range(4):
        for i, one in enumerate(PLACE_BLOCKS):
            at = T_PLACE + j * PLACE_COLS + 32 * i
            trig[32 * j + np.arange(32), at + np.arange(32)] = float(one)
    b[:, KB_CAUSAL:KB_CAUSAL + P] = np.where(rows[None, :] > rows[:, None], -BIG, 0.0)
    b[:, KB_CAUSAL_T:KB_CAUSAL_T + P] = np.where(rows[:, None] > rows[None, :], -BIG, 0.0)
    for h in range(8):
        b[h, KB_SEL + h] = b[8 + h, KB_SEL + h] = -1.0
    b[0, KB_ONEROW:KB_ONEROW + P] = 1.0
    return const, (b.view(np.uint32) >> 16).astype(np.uint16), trig


def kernel(**inputs):
    import concourse.bacc as _bacc
    from concourse.bass_utils import run_bass_kernel_spmd as _run

    a = {k: np.asarray(v) for k, v in inputs.items()}

    def chunks(m):
        k = m.shape[0] // P
        return m.reshape(k, P, m.shape[1]).transpose(1, 0, 2).reshape(P, k * m.shape[1])

    def padded(m, rows, cols):
        out = np.zeros((rows, cols), m.dtype)
        out[:m.shape[0], :m.shape[1]] = m
        return out

    def paired(first, second):
        out = padded(first, I_PAD, first.shape[1])
        at = (IC - 1) * P + 64
        out[at:at + REST] = second[HIDDEN - REST:]
        return out

    def pack(*parts):
        return np.ascontiguousarray(np.concatenate(parts, axis=1))

    one = "L1_xattn_"
    two = "L2_xattn_"
    const, constb, trig = tables()
    arrays = {
        "x": np.ascontiguousarray(a["x"].transpose(0, 2, 1).reshape(BATCH, DC, P, S)
                                  .transpose(0, 2, 1, 3).reshape(BATCH, P, DC * S)),
        "ctx": np.ascontiguousarray(a["ctx_1024"].transpose(0, 2, 1)),
        "pos": np.ascontiguousarray(a["pos_1xS"]),
        "expert": np.ascontiguousarray(a["mask_BxS_ik0"]),
        "keep_row": np.ascontiguousarray(a["mask_BxS2_bk0"]).view(np.uint32),
        "keep_col": np.ascontiguousarray(
            a["mask_BxS2_bk0"].reshape(BATCH, ST, P).transpose(0, 2, 1)).reshape(BATCH, S).view(np.uint32),
        "gm": np.stack([pack(a[f"L{n}_xattn_W_mem"].T, chunks(a[f"L{n}_xattn_W_gate"].T)) for n in (0, 3)]),
        "l1a": pack(chunks(a[one + "v_qkv"]), chunks(a[one + "l_qkv"]), chunks(a[one + "v_dense"]),
                    chunks(a[one + "l_dense"]), chunks(a[one + "cq_w"]), a[one + "ckv_w"],
                    a[one + "cdense_w"]),
        "l1m": pack(*[chunks(paired(a[f"{one}{e}_gate"].T, a[f"{one}{e}_up"].T).T) for e in "vl"],
                    *[chunks(padded(a[f"{one}{e}_up"], D, I_PAD)) for e in "vl"]),
        "l1d": pack(chunks(paired(a[one + "v_down"], a[one + "l_down"])),
                    chunks(a[one + "l_down"][:(IC - 1) * P])),
        "l2q": pack(chunks(a[two + "Wq"]), a[two + "Wkv"]),
        "l2f": pack(chunks(a[two + "Wo"]), chunks(a[two + "W1"]), chunks(a[two + "W2"])),
        "vec": pack(*[a[n].reshape(DC, P).T for n in VECTORS],
                    *[np.broadcast_to(a[two + n].reshape(1, 1), (P, 1)) for n in ("attn_gate", "ff_gate")]),
        "const": const,
        "constb": constb,
        "trig": trig,
    }
    nc = _bacc.Bacc("TRN2", target_bir_lowering=False, num_devices=1)
    args = [nc.dram_tensor(f"in_{n}", v.shape, mybir.dt.from_np(v.dtype), kind="ExternalInput").ap()
            for n, v in arrays.items()]
    args.append(nc.dram_tensor("out_0", (BATCH, P, DC * S), F32, kind="ExternalOutput").ap())
    build(nc, *args)
    r = _run(nc, [{f"in_{n}": v for n, v in arrays.items()}], core_ids=[0])
    got = r.results[0]["out_0"]
    return got.reshape(BATCH, P, DC, S).transpose(0, 3, 2, 1).reshape(BATCH, S, D)
```
